# Optimizing a Trainium2 kernel written in Bass

```python
import numpy as np
import jax
import jax.numpy as jnp

def _softmax(x, axis=-1):
    return jax.nn.softmax(x, axis=axis)

def _gelu(x):
    return jax.nn.gelu(x, approximate=True)

def _silu(x):
    return jax.nn.silu(x)

def _sigmoid(x):
    return jax.nn.sigmoid(x)

def _layernorm(x, axis=-1, eps=1e-05):
    m = jnp.mean(x, axis=axis, keepdims=True)
    v = jnp.var(x, axis=axis, keepdims=True)
    return (x - m) / jnp.sqrt(v + eps)

def _scatter_add(tgt, idx, src, axis=0):
    return tgt.at[idx].add(src)

def _segment_sum(src, seg, n):
    return jax.ops.segment_sum(src, seg, n)
kernel_name = 'mk_hybrid_d1_jaxref_r4_c2bfea'

def setup_inputs(seed: int=0):
    np.random.seed(seed)
    _w = jnp.asarray

    def _L0_attn_a_setup():
        import jax, jax.numpy as jnp
        import numpy as np
        B, L, D_MODEL, D_INNER, D_STATE, DT_RANK, K = (2, 256, 256, 512, 16, 64, 4)
        key = jax.random.key(seed)
        ks = jax.random.split(key, 8)
        sc = lambda n: 1.0 / np.sqrt(n)
        return {'x': jax.random.normal(ks[0], (B, L, D_MODEL), jnp.float32), 'W_in': jax.random.normal(ks[1], (2 * D_INNER, D_MODEL), jnp.float32) * sc(D_MODEL), 'conv_w': jax.random.normal(ks[2], (D_INNER, K), jnp.float32) * sc(K), 'conv_b': jax.random.normal(ks[3], (D_INNER,), jnp.float32) * 0.1, 'W_x': jax.random.normal(ks[4], (DT_RANK + 2 * D_STATE, D_INNER), jnp.float32) * sc(D_INNER), 'W_dt': jax.random.normal(ks[5], (D_INNER, DT_RANK), jnp.float32) * sc(DT_RANK), 'b_dt': jax.random.normal(ks[6], (D_INNER,), jnp.float32) * 0.1, 'A_log': jnp.log(jnp.tile(jnp.arange(1.0, D_STATE + 1.0, dtype=jnp.float32)[None, :], (D_INNER, 1))), 'Dp': jnp.ones((D_INNER,), jnp.float32), 'W_out': jax.random.normal(ks[7], (D_MODEL, D_INNER), jnp.float32) * sc(D_INNER)}
    _L0_attn_a_in = _L0_attn_a_setup()

    def _L0_attn_b_setup():
        import jax, jax.numpy as jnp
        import numpy as np
        from jax import lax
        B, L, D = (2, 1024, 256)
        H = 8
        DK = D // H
        DV = D // H
        CONV_K = 4
        CHUNK = 32
        EPS = 1e-05

        def _silu(x):
            return x * jax.nn.sigmoid(x)

        def _causal_depthwise_conv_silu(x, w):
            K = w.shape[1]
            l = x.shape[1]
            xp = jnp.pad(x, ((0, 0), (K - 1, 0), (0, 0)))
            y = sum((xp[:, i:i + l, :] * w[:, i] for i in range(K)))
            return _silu(y)

        def _l2norm(x):
            return x * lax.rsqrt(jnp.sum(x * x, axis=-1, keepdims=True) + 1e-12)

        def _delta_rule_chunkwise(q, k, v, beta, chunk=CHUNK):
            b, h, l, dk = q.shape
            dv = v.shape[-1]
            n = l // chunk
            q = _l2norm(q)
            k = _l2norm(k)
            v = v * beta[..., None]
            kb = k * beta[..., None]
            resh = lambda t: t.reshape(b, h, n, chunk, t.shape[-1])
            q, k, v, kb = map(resh, (q, k, v, kb))
            tri_strict = jnp.tril(jnp.ones((chunk, chunk), dtype=bool), -1)
            attn = jnp.where(tri_strict, -(kb @ jnp.swapaxes(k, -1, -2)), 0.0)
            col = jnp.arange(chunk)
            for i in range(1, chunk):
                row = attn[..., i, :]
                upd = jnp.einsum('bhnj,bhnjk->bhnk', row, attn)
                attn = attn.at[..., i, :].set(jnp.where(col < i, row + upd, row))
            attn = attn + jnp.eye(chunk, dtype=attn.dtype)
            u = attn @ v
            w = attn @ kb
            tri_incl = jnp.tril(jnp.ones((chunk, chunk), dtype=bool))
            qc, kc, uc, wc = (jnp.moveaxis(t, 2, 0) for t in (q, k, u, w))

            def step(S, inp):
                qi, ki, ui, wi = inp
                attn_i = jnp.where(tri_incl, qi @ jnp.swapaxes(ki, -1, -2), 0.0)
                ui = ui - wi @ S
                oi = qi @ S + attn_i @ ui
                S = S + jnp.swapaxes(ki, -1, -2) @ ui
                return (S, oi)
            S0 = jnp.zeros((b, h, dk, dv), dtype=q.dtype)
            S, o = lax.scan(step, S0, (qc, kc, uc, wc))
            o = jnp.moveaxis(o, 0, 2).reshape(b, h, l, dv)
            return (o, S)
        key = jax.random.key(seed)
        ks = jax.random.split(key, 10)
        s = 0.02
        return {'hidden_states': jax.random.normal(ks[0], (B, L, D), jnp.float32), 'q_w': jax.random.normal(ks[1], (D, D), jnp.float32) * s, 'k_w': jax.random.normal(ks[2], (D, D), jnp.float32) * s, 'v_w': jax.random.normal(ks[3], (D, D), jnp.float32) * s, 'conv_q_w': jax.random.normal(ks[4], (D, CONV_K), jnp.float32) * 0.3, 'conv_k_w': jax.random.normal(ks[5], (D, CONV_K), jnp.float32) * 0.3, 'conv_v_w': jax.random.normal(ks[6], (D, CONV_K), jnp.float32) * 0.3, 'b_w': jax.random.normal(ks[7], (D, H), jnp.float32) * s, 'mix_w': jax.random.normal(ks[8], (D, H), jnp.float32) * s, 'mix_b': jnp.full((H,), -1.0, jnp.float32), 'mix_bias': jnp.full((H,), -1.0, jnp.float32), 'o_norm_w': jnp.ones((DV,), jnp.float32), 'o_w': jax.random.normal(ks[9], (D, D), jnp.float32) * s}
    _L0_attn_b_in = _L0_attn_b_setup()

    def _L0_ffn_setup():
        import jax, jax.numpy as jnp
        import numpy as np
        B, S, D, E, H, K = (64, 512, 256, 32, 1024, 8)
        key = jax.random.key(seed)
        k0, k1, k2, k3 = jax.random.split(key, 4)
        x = jax.random.normal(k0, (B, S, D), jnp.float32)
        gate_w = jax.random.normal(k1, (E, D), jnp.float32) * (1.0 / np.sqrt(D))
        gate_b = jnp.zeros((E,), jnp.float32)
        w1 = jax.random.normal(k2, (E, D + 1, H), jnp.float32) * (1.0 / np.sqrt(D + 1))
        w2 = jax.random.normal(k3, (E, H + 1, D), jnp.float32) * (1.0 / np.sqrt(H + 1))
        return {'x': x, 'gate_w': gate_w, 'gate_b': gate_b, 'w1': w1, 'w2': w2}
    _L0_ffn_in = _L0_ffn_setup()
    _d = {'L0_attn_a_x': _L0_attn_a_in['x'], 'L0_attn_a_W_in': _L0_attn_a_in['W_in'], 'L0_attn_a_conv_w': _L0_attn_a_in['conv_w'], 'L0_attn_a_conv_b': _L0_attn_a_in['conv_b'], 'L0_attn_a_W_x': _L0_attn_a_in['W_x'], 'L0_attn_a_W_dt': _L0_attn_a_in['W_dt'], 'L0_attn_a_b_dt': _L0_attn_a_in['b_dt'], 'L0_attn_a_A_log': _L0_attn_a_in['A_log'], 'L0_attn_a_Dp': _L0_attn_a_in['Dp'], 'L0_attn_a_W_out': _L0_attn_a_in['W_out'], 'L0_attn_b_q_w': _L0_attn_b_in['q_w'], 'L0_attn_b_k_w': _L0_attn_b_in['k_w'], 'L0_attn_b_v_w': _L0_attn_b_in['v_w'], 'L0_attn_b_conv_q_w': _L0_attn_b_in['conv_q_w'], 'L0_attn_b_conv_k_w': _L0_attn_b_in['conv_k_w'], 'L0_attn_b_conv_v_w': _L0_attn_b_in['conv_v_w'], 'L0_attn_b_b_w': _L0_attn_b_in['b_w'], 'L0_attn_b_mix_w': _L0_attn_b_in['mix_w'], 'L0_attn_b_mix_b': _L0_attn_b_in['mix_b'], 'L0_attn_b_mix_bias': _L0_attn_b_in['mix_bias'], 'L0_attn_b_o_norm_w': _L0_attn_b_in['o_norm_w'], 'L0_attn_b_o_w': _L0_attn_b_in['o_w'], 'L0_ffn_gate_w': _L0_ffn_in['gate_w'], 'L0_ffn_gate_b': _L0_ffn_in['gate_b'], 'L0_ffn_w1': _L0_ffn_in['w1'], 'L0_ffn_w2': _L0_ffn_in['w2']}
    _x0 = _d['L0_attn_a_x']
    _d['L0_attn_a_x'] = jax.random.normal(jax.random.fold_in(jax.random.key(seed), 1), (8, 512, 256), dtype=_x0.dtype)
    del _x0
    return _d

def reference(L0_attn_a_x, L0_attn_a_W_in, L0_attn_a_conv_w, L0_attn_a_conv_b, L0_attn_a_W_x, L0_attn_a_W_dt, L0_attn_a_b_dt, L0_attn_a_A_log, L0_attn_a_Dp, L0_attn_a_W_out, L0_attn_b_q_w, L0_attn_b_k_w, L0_attn_b_v_w, L0_attn_b_conv_q_w, L0_attn_b_conv_k_w, L0_attn_b_conv_v_w, L0_attn_b_b_w, L0_attn_b_mix_w, L0_attn_b_mix_b, L0_attn_b_mix_bias, L0_attn_b_o_norm_w, L0_attn_b_o_w, L0_ffn_gate_w, L0_ffn_gate_b, L0_ffn_w1, L0_ffn_w2):

    def _L0_attn_a_ref(x, W_in, conv_w, conv_b, W_x, W_dt, b_dt, A_log, Dp, W_out):
        import jax, jax.numpy as jnp
        import numpy as np
        B, L, D_MODEL, D_INNER, D_STATE, DT_RANK, K = (2, 256, 256, 512, 16, 64, 4)
        xz = x @ W_in.T
        xc, z = jnp.split(xz, 2, axis=-1)
        d_inner = xc.shape[-1]
        k = conv_w.shape[1]
        xt = xc.transpose(0, 2, 1)
        yt = jax.lax.conv_general_dilated(xt, conv_w[:, None, :], window_strides=(1,), padding=[(k - 1, 0)], dimension_numbers=('NCH', 'OIH', 'NCH'), feature_group_count=d_inner)
        xc = yt.transpose(0, 2, 1) + conv_b
        xc = jax.nn.silu(xc)
        dBC = xc @ W_x.T
        dt_rank = W_dt.shape[1]
        d_state = A_log.shape[1]
        delta = dBC[..., :dt_rank]
        Bm = dBC[..., dt_rank:dt_rank + d_state]
        Cm = dBC[..., dt_rank + d_state:]
        delta = jax.nn.softplus(delta @ W_dt.T + b_dt)
        A = -jnp.exp(A_log)
        deltaA = jnp.exp(delta[..., None] * A)
        BX = delta[..., None] * Bm[:, :, None, :] * xc[..., None]

        def combine(e1, e2):
            a1, x1 = e1
            a2, x2 = e2
            return (a1 * a2, a2 * x1 + x2)
        _, hs = jax.lax.associative_scan(combine, (deltaA, BX), axis=1)
        y = jnp.einsum('bldn,bln->bld', hs, Cm) + Dp * xc
        out = y * jax.nn.silu(z) @ W_out.T
        return out

    def _L0_attn_b_ref(hidden_states, q_w, k_w, v_w, conv_q_w, conv_k_w, conv_v_w, b_w, mix_w, mix_b, mix_bias, o_norm_w, o_w):
        import jax, jax.numpy as jnp
        import numpy as np
        from jax import lax
        B, L, D = (2, 1024, 256)
        H = 8
        DK = D // H
        DV = D // H
        CONV_K = 4
        CHUNK = 32
        EPS = 1e-05

        def _silu(x):
            return x * jax.nn.sigmoid(x)

        def _causal_depthwise_conv_silu(x, w):
            K = w.shape[1]
            l = x.shape[1]
            xp = jnp.pad(x, ((0, 0), (K - 1, 0), (0, 0)))
            y = sum((xp[:, i:i + l, :] * w[:, i] for i in range(K)))
            return _silu(y)

        def _l2norm(x):
            return x * lax.rsqrt(jnp.sum(x * x, axis=-1, keepdims=True) + 1e-12)

        def _delta_rule_chunkwise(q, k, v, beta, chunk=CHUNK):
            b, h, l, dk = q.shape
            dv = v.shape[-1]
            n = l // chunk
            q = _l2norm(q)
            k = _l2norm(k)
            v = v * beta[..., None]
            kb = k * beta[..., None]
            resh = lambda t: t.reshape(b, h, n, chunk, t.shape[-1])
            q, k, v, kb = map(resh, (q, k, v, kb))
            tri_strict = jnp.tril(jnp.ones((chunk, chunk), dtype=bool), -1)
            attn = jnp.where(tri_strict, -(kb @ jnp.swapaxes(k, -1, -2)), 0.0)
            col = jnp.arange(chunk)
            for i in range(1, chunk):
                row = attn[..., i, :]
                upd = jnp.einsum('bhnj,bhnjk->bhnk', row, attn)
                attn = attn.at[..., i, :].set(jnp.where(col < i, row + upd, row))
            attn = attn + jnp.eye(chunk, dtype=attn.dtype)
            u = attn @ v
            w = attn @ kb
            tri_incl = jnp.tril(jnp.ones((chunk, chunk), dtype=bool))
            qc, kc, uc, wc = (jnp.moveaxis(t, 2, 0) for t in (q, k, u, w))

            def step(S, inp):
                qi, ki, ui, wi = inp
                attn_i = jnp.where(tri_incl, qi @ jnp.swapaxes(ki, -1, -2), 0.0)
                ui = ui - wi @ S
                oi = qi @ S + attn_i @ ui
                S = S + jnp.swapaxes(ki, -1, -2) @ ui
                return (S, oi)
            S0 = jnp.zeros((b, h, dk, dv), dtype=q.dtype)
            S, o = lax.scan(step, S0, (qc, kc, uc, wc))
            o = jnp.moveaxis(o, 0, 2).reshape(b, h, l, dv)
            return (o, S)
        b, l, _ = hidden_states.shape
        q = _causal_depthwise_conv_silu(hidden_states @ q_w, conv_q_w)
        k = _causal_depthwise_conv_silu(hidden_states @ k_w, conv_k_w)
        v = _causal_depthwise_conv_silu(hidden_states @ v_w, conv_v_w)
        v_token = v.reshape(b, l, H, DV)
        q = q.reshape(b, l, H, DK)
        k = k.reshape(b, l, H, DK)
        beta = jax.nn.sigmoid(hidden_states @ b_w)
        q_r = jnp.swapaxes(q, 1, 2)
        k_r = jnp.swapaxes(k, 1, 2)
        v_r = jnp.swapaxes(v_token, 1, 2)
        beta_r = jnp.swapaxes(beta, 1, 2)
        o, _S = _delta_rule_chunkwise(q_r, k_r, v_r, beta_r)
        o = jnp.swapaxes(o, 1, 2)
        g = jax.nn.sigmoid(hidden_states @ mix_w + mix_b + mix_bias)[..., None]
        o = g * o + (1.0 - g) * v_token
        o = o * lax.rsqrt(jnp.mean(o * o, axis=-1, keepdims=True) + EPS) * o_norm_w
        o = o.reshape(b, l, H * DV) @ o_w
        return o

    def _L0_ffn_ref(x, gate_w, gate_b, w1, w2):
        import jax, jax.numpy as jnp
        import numpy as np
        B, S, D, E, H, K = (64, 512, 256, 32, 1024, 8)
        b, s, d = x.shape
        logits = jnp.einsum('bsd,ed->bse', x, gate_w) + gate_b
        probs = jax.nn.softmax(logits, axis=-2)
        vals_t, idx_t = jax.lax.top_k(probs.transpose(0, 2, 1), K)
        vals = vals_t.transpose(0, 2, 1)
        idx = idx_t.transpose(0, 2, 1)
        flat_idx = idx.reshape(b, K * E)
        tok = jnp.take_along_axis(x, flat_idx[:, :, None], axis=1)
        tok = tok.reshape(b, K, E, d)
        merged = jnp.einsum('bked,bke->bed', tok, vals)
        ones = jnp.ones(merged.shape[:-1] + (1,), merged.dtype)
        h = jnp.einsum('bei,eih->beh', jnp.concatenate([merged, ones], -1), w1)
        h = jax.nn.gelu(h, approximate=False)
        o = jnp.einsum('bej,ejo->beo', jnp.concatenate([h, ones], -1), w2)
        out_tok = jnp.einsum('beo,bke->bkeo', o, vals).reshape(b, K * E, d)
        out = jnp.zeros_like(x).at[jnp.arange(b)[:, None], flat_idx].add(out_tok)
        return out
    x = L0_attn_a_x
    x = x + _L0_attn_a_ref(_layernorm(x, axis=-1), L0_attn_a_W_in, L0_attn_a_conv_w, L0_attn_a_conv_b, L0_attn_a_W_x, L0_attn_a_W_dt, L0_attn_a_b_dt, L0_attn_a_A_log, L0_attn_a_Dp, L0_attn_a_W_out)
    x = x + _L0_ffn_ref(_layernorm(x, axis=-1), L0_ffn_gate_w, L0_ffn_gate_b, L0_ffn_w1, L0_ffn_w2)
    x = x + _L0_attn_b_ref(_layernorm(x, axis=-1), L0_attn_b_q_w, L0_attn_b_k_w, L0_attn_b_v_w, L0_attn_b_conv_q_w, L0_attn_b_conv_k_w, L0_attn_b_conv_v_w, L0_attn_b_b_w, L0_attn_b_mix_w, L0_attn_b_mix_b, L0_attn_b_mix_bias, L0_attn_b_o_norm_w, L0_attn_b_o_w)
    x = x + _L0_ffn_ref(_layernorm(x, axis=-1), L0_ffn_gate_w, L0_ffn_gate_b, L0_ffn_w1, L0_ffn_w2)
    return x

_drawn_inputs = setup_inputs


def setup_inputs(seed=0):
    import zlib

    import numpy as np

    out = dict(_drawn_inputs(seed))
    spreads = {'L0_attn_a_Dp': (1.0, 0.2),
     'L0_attn_b_mix_b': (-1.0, 0.6),
     'L0_attn_b_mix_bias': (-1.0, 0.6),
     'L0_attn_b_o_norm_w': (1.0, 0.2),
     'L0_ffn_gate_b': (0.0, 0.8)}
    factors = {'L0_attn_b_q_w': 3.112,
     'L0_attn_b_k_w': 3.097,
     'L0_attn_b_conv_q_w': 3.142,
     'L0_attn_b_conv_k_w': 3.128,
     'L0_attn_b_b_w': 8.0,
     'L0_attn_b_mix_w': 8.0}
    for name, (base, spread) in spreads.items():
        noise = np.random.default_rng([zlib.crc32(name.encode()), seed]).standard_normal(out[name].shape)
        drawn = base * np.exp(spread * noise) if base else spread * noise
        out[name] = jnp.asarray(drawn.astype(out[name].dtype))
    for name, factor in factors.items():
        out[name] = (out[name] * factor).astype(out[name].dtype)
    return out
```

```python
from contextlib import ExitStack

import concourse.bass as bass
from concourse import mybir

ALU = mybir.AluOpType
ACT = mybir.ActivationFunctionType
F32 = mybir.dt.float32
AX_X = mybir.AxisListType.X
ds = bass.ds

P = 128
B, L, D = 8, 512, 256
ST = L // P
KD = D // P
BANK = 512
EPS = 1e-5

DI, NS, RK, KC = 512, 16, 64, 4
DT = DI // P
H, DK, C = 8, 32, 32
HS = P // DK
NC = L // C
CT = P // C
E, HID, TOP = 32, 1024, 8
EG = 4
NG = E // EG
MH = HID // P


class Mem:

    def __init__(self, nc, ctx):
        self.nc, self.ctx, self.sems = nc, ctx, []

    def sb(self, name, *shape):
        return self.ctx.enter_context(self.nc.sbuf_tensor(name, list(shape), F32))

    def sem(self, name):
        self.sems.append(self.nc.alloc_semaphore(name))
        return self.sems[-1]

    def end_phase(self):
        self.nc.clear_and_free_semaphores(self.sems)
        self.nc.all_engine_barrier()


class Chain:

    def __init__(self, eng, sem, base):
        self.eng, self.sem, self.base, self.n = eng, sem, base, 0

    def step(self, ins):
        self.n += 1
        ins.then_inc(self.sem, 1)

    def wait(self, passed=None):
        self.eng.wait_ge(self.sem, self.base + self.n)
        if passed:
            self.eng.sem_inc(passed, 1)


def free_bcast(ap, axis, n):
    shape = list(ap.shape)
    shape.insert(axis, n)
    return ap.unsqueeze(axis).to_broadcast(shape)


class NormSems:
    def __init__(self, m, tag):
        self.stats, self.turn, self.mv, self.std, self.rstd, self.xln = (
            m.sem(f"{tag}_{s}") for s in ("ln_stats", "ln_turn", "ln_mean_var", "ln_std", "ln_rstd", "ln_done"))


class NormBufs:
    def __init__(self, m, tag):
        self.stats = m.sb(f"{tag}_bn_stats", P, ST, 6)
        self.mv = m.sb(f"{tag}_mean_var", P, ST, 2)
        self.std = m.sb(f"{tag}_std", P, ST)
        self.rstd = m.sb(f"{tag}_rstd", P, ST)


def norm_vector(nc, dve, b, x, out, nb, ns):
    for st in range(ST):
        nc.vector.bn_stats(nb.stats[:, st, :], x[:, st, :]).then_inc(ns.stats, 1)
    carried_wait(dve, ns.turn, (ns.stats, ST * (b + 1)))
    for st in range(ST):
        nc.vector.bn_aggr(nb.mv[:, st, :], nb.stats[:, st, :]).then_inc(ns.mv, 1)
    dve.wait_ge(ns.std, b + 1)
    nc.vector.reciprocal(nb.rstd[:, :], nb.std[:, :]).then_inc(ns.rstd, 1)
    dve.wait_ge(ns.rstd, b + 1)
    for st in range(ST):
        nc.vector.tensor_scalar(out[:, st, :], x[:, st, :], nb.mv[:, st, 0:1], nb.rstd[:, st:st + 1],
                                ALU.subtract, ALU.mult).then_inc(ns.xln, 1)


def norm_scalar(nc, act, b, nb, ns, eps):
    act.wait_ge(ns.mv, ST * (b + 1))
    nc.scalar.activation(nb.std[:, :], nb.mv[:, :, 1], ACT.Sqrt, bias=eps[:, :]).then_inc(ns.std, 1)


def transpose_tiles(nc, xln, ident, banks, done):
    for kt in range(KD):
        for st in range(ST):
            ins = nc.tensor.transpose(banks[kt][:, st * P:(st + 1) * P], xln[:, st, kt * P:(kt + 1) * P], ident[:, :])
        ins.then_inc(done, 1)


def carried_wait(eng, passed, *waits):
    for sem, value in waits:
        eng.wait_ge(sem, value)
    eng.sem_inc(passed, 1)


def token_major(x_dram, b):
    return x_dram[ds(b, 1), :, :].rearrange("o (s p) d -> p (o s) d", p=P)


class Weights:

    def __init__(self, m, w1, w2):
        self.w1_dram, self.w2_dram = w1, w2
        self.w1 = [m.sb(f"w1_slot{j}", P, KD, HID) for j in range(EG)]
        self.w2 = [m.sb(f"w2_slot{j}", P, MH, D) for j in range(EG)]
        self.w1_loaded = [m.sem(f"w1_loaded{j}") for j in range(EG)]
        self.w2_loaded = [m.sem(f"w2_loaded{j}") for j in range(EG)]
        self.w1_used = [m.sem(f"w1_used{j}") for j in range(EG)]
        self.w2_used = [m.sem(f"w2_used{j}") for j in range(EG)]

    def load(self, nc, j, group):
        e = group * EG + j
        nc.sync.dma_start(self.w1[j][:, :, :], self.w1_dram[ds(e, 1), 0:D, :].rearrange(
            "o (p t) n -> p (o t) n", t=KD)).then_inc(self.w1_loaded[j], 16)
        nc.sync.dma_start(self.w2[j][:, :, :], self.w2_dram[ds(e, 1), 0:HID, :].rearrange(
            "o (p k) n -> p (o k) n", k=MH)).then_inc(self.w2_loaded[j], 16)


def mamba_phase(nc, banks, consts, weights, x_in, x_out, prm, scratch):
    ident, eps = consts["ident"], consts["eps"]
    ybank, fbank = banks[0:4], banks[4:8]
    with ExitStack() as ctx:
        m = Mem(nc, ctx)
        w_in = m.sb("w_in", P, KD, 2 * DI)
        w_x = m.sb("w_x", P, DT, RK + 2 * NS)
        w_dt = m.sb("w_dt", RK, DI)
        w_out = m.sb("w_out", P, DT, D)
        conv_w = m.sb("conv_w", P, DT, KC)
        conv_b = m.sb("conv_b", P, DT)
        b_dt = m.sb("b_dt", P, DT)
        dp = m.sb("dp", P, DT)
        a_neg = m.sb("a_neg", P, DT, NS)
        a_exp = m.sb("a_exp", P, DT, NS)
        dp_diag = m.sb("dp_diag", P, DT, P)
        x = m.sb("x_mamba", P, ST, D)
        dx = m.sb("delta_x", P, DT, L)
        xln = dx[:, 0:2, :].rearrange("p t l -> p (t l)").rearrange("p (s d) -> p s d", d=D)
        xt = dx[:, 2:4, :]
        nb = NormBufs(m, "mamba")
        xpad = m.sb("xpad", P, DT, KC - 1 + L)
        conv = m.sb("conv", P, DT, L)
        zs = m.sb("z_silu", P, DT, L)
        xc = m.sb("x_conv", P, DT, L)
        dbc = m.sb("dbc", RK + 2 * NS, L)
        delta = m.sb("delta", P, DT, L)
        bc = [m.sb(f"b_and_c{i}", P, 2, L) for i in range(2)]
        decay = [m.sb(f"decay{i}", P, DT, L) for i in range(2)]
        bx = [m.sb(f"bx{i}", P, DT, L) for i in range(2)]
        hs = m.sb("state", P, DT, L)
        hc = [m.sb(f"state_c{i}", P, DT, L) for i in range(2)]

        ns = NormSems(m, "mamba")
        S = {k: m.sem("ma_" + k) for k in (
            "params_loaded", "a_exp", "a_ready", "dp_diag", "pads_zero", "x_loaded", "xt_psum", "xt_ready",
            "xz_psum", "xz_read", "conv_step", "xc_ready", "dbc_psum", "dbc_ready", "bc_stored",
            "bc_loaded0", "bc_loaded1", "delta_psum", "soft", "soft_done", "delta_ready", "dx_ready", "decay_ready", "bx_ready",
            "scan_done", "hc_ready", "sum_done", "y_psum", "yz_done", "out_psum", "out_added", "x_stored")}
        N_PARAMS = 9

        passed = m.sem(f"sync_passed_{m.nc.next_id()}")
        with nc.Block() as block:
            @block.sync
            def _(sp):
                for dst, src in (
                        (w_in[:, :, :], prm["W_inT"].rearrange("(k p) n -> p k n", p=P)),
                        (w_x[:, :, :], prm["W_xT"].rearrange("(k p) n -> p k n", p=P)),
                        (w_dt[:, :], prm["W_dtT"]),
                        (w_out[:, :, :], prm["W_outT"].rearrange("(k p) n -> p k n", p=P)),
                        (conv_w[:, :, :], prm["conv_w"].rearrange("(t p) k -> p t k", p=P)),
                        (conv_b[:, :], prm["conv_bT"]),
                        (b_dt[:, :], prm["b_dtT"]),
                        (dp[:, :], prm["DpT"]),
                        (a_exp[:, :, :], prm["A_log"].rearrange("(t p) n -> p t n", p=P))):
                    sp.dma_start(dst, src).then_inc(S["params_loaded"], 16)
                for j in range(EG):
                    weights.load(nc, j, 0)
                sp.sem_inc(S["x_stored"], 16)
                with sp.Fori(0, B) as b:
                    carried_wait(sp, passed, (S["x_stored"], 16 * b + 16))
                    sp.dma_start(x[:, :, :], token_major(x_in, b)).then_inc(S["x_loaded"], 16)
                    carried_wait(sp, passed, (S["dbc_ready"], b + 1))
                    sp.dma_start(scratch[ds(b, 1), :, :].rearrange("o r l -> (o r) l"),
                                 dbc[RK:RK + 2 * NS, :]).then_inc(S["bc_stored"], 16)
                    carried_wait(sp, passed, (S["bc_stored"], 16 * b + 16))
                    for n in range(NS):
                        carried_wait(sp, passed, (S["hc_ready"], NS * b + n + 1), (S["bx_ready"], NS * b + n + 1))
                        src = scratch[ds(b, 1), n:n + NS + 1:NS, :].rearrange("o r l -> (o r) l")
                        sp.dma_start(bc[n % 2][:, :, :], src.partition_broadcast(P)).then_inc(
                            S[f"bc_loaded{n % 2}"], 16)
                    carried_wait(sp, passed, (S["out_added"], 2 * b + 4))
                    sp.dma_start(token_major(x_out, b), x[:, :, :]).then_inc(S["x_stored"], 16)
                sp.wait_ge(S["x_stored"], 16 * (B + 1))

            @block.gpsimd
            def _(pool):
                for i in range(2):
                    nc.gpsimd.memset(decay[i][:, :, 0], 0.0).then_inc(S["pads_zero"], 1)
                nc.gpsimd.memset(xpad[:, :, 0:KC - 1], 0.0).then_inc(S["pads_zero"], 1)
                pool.sem_inc(S["bx_ready"], 2)
                with pool.Fori(0, B) as b:
                    pool.wait_ge(S["soft"], 2 * b + 2)
                    nc.gpsimd.tensor_tensor(delta[:, :, :], delta[:, :, :], conv[:, :, :], ALU.add).then_inc(S["delta_ready"], 1)
                    pool.wait_ge(S["delta_ready"], b + 1)
                    pool.wait_ge(S["xc_ready"], b + 1)
                    nc.gpsimd.tensor_tensor(dx[:, :, :], delta[:, :, :], xc[:, :, :], ALU.mult).then_inc(S["dx_ready"], 1)
                    pool.wait_ge(S["dx_ready"], b + 1)
                    for n in range(NS):
                        pool.wait_ge(S[f"bc_loaded{n % 2}"], 16 * (NS // 2) * b + 16 * (n // 2 + 1))
                        pool.wait_ge(S["scan_done"], NS * b + n + 1)
                        nc.gpsimd.tensor_tensor(bx[n % 2][:, :, :], dx[:, :, :],
                                                free_bcast(bc[n % 2][:, 0, :], 1, DT), ALU.mult).then_inc(S["bx_ready"], 1)

            @block.scalar
            def _(act):
                act.wait_ge(S["params_loaded"], 16 * N_PARAMS)
                nc.scalar.activation(a_neg[:, :, :], a_exp[:, :, :], ACT.Exp).then_inc(S["a_exp"], 1)
                act.wait_ge(S["pads_zero"], 3)
                act.wait_ge(S["a_ready"], 1)
                act.sem_inc(S["soft_done"], DT)
                with act.Fori(0, B) as b:
                    norm_scalar(nc, act, b, nb, ns, eps)
                    for kt in range(KD):
                        act.wait_ge(S["xt_psum"], KD * b + kt + 1)
                        nc.scalar.copy(xt[:, kt, :], fbank[kt][:, :]).then_inc(S["xt_ready"], 1)
                    for t in range(DT):
                        act.wait_ge(S["xz_psum"], 2 * DT * b + t + 1)
                        nc.scalar.activation(conv[:, t, :], fbank[t][:, :], ACT.Identity, bias=conv_b[:, t:t + 1],
                                             scale=conv_w[:, t, KC - 1:KC])
                        nc.scalar.copy(xpad[:, t, KC - 1:], fbank[t][:, :]).then_inc(S["xz_read"], 1)
                    act.wait_ge(S["yz_done"], DT * b + DT)
                    for t in range(DT):
                        act.wait_ge(S["xz_psum"], 2 * DT * b + DT + t + 1)
                        nc.scalar.activation(zs[:, t, :], fbank[t][:, :], ACT.Silu).then_inc(S["xz_read"], 1)
                    act.wait_ge(S["conv_step"], DT * (KC - 1) * b + DT * (KC - 1))
                    nc.scalar.activation(xc[:, :, :], conv[:, :, :], ACT.Silu).then_inc(S["xc_ready"], 1)
                    act.wait_ge(S["dbc_psum"], b + 1)
                    nc.scalar.copy(dbc[:, :], fbank[0][0:RK + 2 * NS, :]).then_inc(S["dbc_ready"], 1)
                    for t in range(DT):
                        act.wait_ge(S["delta_psum"], DT * b + t + 1)
                        nc.scalar.activation(conv[:, t, :], fbank[t][:, :], ACT.Abs, bias=b_dt[:, t:t + 1])
                        nc.scalar.activation(delta[:, t, :], fbank[t][:, :], ACT.Relu,
                                             bias=b_dt[:, t:t + 1]).then_inc(S["soft_done"], 1)
                    act.wait_ge(S["soft_done"], DT * b + 2 * DT)
                    nc.scalar.activation(conv[:, :, :], conv[:, :, :], ACT.Exp, scale=-1.0).then_inc(S["soft"], 1)
                    act.wait_ge(S["soft"], 2 * b + 1)
                    nc.scalar.activation(conv[:, :, :], conv[:, :, :], ACT.Ln, bias=1.0).then_inc(S["soft"], 1)
                    act.wait_ge(S["delta_ready"], b + 1)
                    for n in range(NS):
                        act.wait_ge(S["scan_done"], NS * b + n + 1)
                        for t in range(DT):
                            ins = nc.scalar.activation(decay[n % 2][:, t, 1:], delta[:, t, 1:], ACT.Exp,
                                                       scale=a_neg[:, t, n:n + 1])
                        ins.then_inc(S["decay_ready"], 1)

            @block.vector
            def _(dve):
                dve.wait_ge(S["a_exp"], 1)
                nc.vector.tensor_scalar(a_neg[:, :, :], a_neg[:, :, :], -1.0, None, ALU.mult).then_inc(S["a_ready"], 1)
                for t in range(DT):
                    nc.vector.tensor_scalar(dp_diag[:, t, :], ident[:, :], dp[:, t:t + 1], None,
                                            ALU.mult).then_inc(S["dp_diag"], 1)
                dve.wait_ge(S["pads_zero"], 3)
                dve.sem_inc(S["scan_done"], 2)
                dve.sem_inc(S["hc_ready"], 2)
                dve.sem_inc(S["yz_done"], DT)
                dve.sem_inc(S["out_added"], 2)
                with dve.Fori(0, B) as b:
                    dve.wait_ge(S["x_loaded"], 16 * b + 16)
                    norm_vector(nc, dve, b, x, xln, nb, ns)
                    for k in range(KC - 1):
                        for t in range(DT):
                            if k == 0:
                                dve.wait_ge(S["xz_read"], 2 * DT * b + t + 1)
                            else:
                                dve.wait_ge(S["conv_step"], DT * (KC - 1) * b + DT * (k - 1) + t + 1)
                            nc.vector.scalar_tensor_tensor(conv[:, t, :], xpad[:, t, k:k + L], conv_w[:, t, k:k + 1],
                                                           conv[:, t, :], ALU.mult, ALU.add).then_inc(S["conv_step"], 1)
                    for n in range(NS):
                        dve.wait_ge(S["decay_ready"], NS * b + n + 1)
                        dve.wait_ge(S["bx_ready"], NS * b + n + 3)
                        dve.wait_ge(S["hc_ready"], NS * b + n + 2)
                        nc.vector.tensor_tensor_scan(hs[:, :, :].rearrange("p t l -> p (t l)"),
                                                     decay[n % 2][:, :, :].rearrange("p t l -> p (t l)"),
                                                     bx[n % 2][:, :, :].rearrange("p t l -> p (t l)"), 0.0,
                                                     ALU.mult, ALU.add).then_inc(S["scan_done"], 1)
                        dve.wait_ge(S["scan_done"], NS * b + n + 3)
                        dve.wait_ge(S["sum_done"], NS * b + n + 1)
                        dve.wait_ge(S[f"bc_loaded{n % 2}"], 16 * (NS // 2) * b + 16 * (n // 2 + 1))
                        nc.vector.tensor_tensor(hc[n % 2][:, :, :], hs[:, :, :],
                                                free_bcast(bc[n % 2][:, 1, :], 1, DT), ALU.mult).then_inc(S["hc_ready"], 1)
                    for t in range(DT):
                        dve.wait_ge(S["y_psum"], b + 1)
                        nc.vector.tensor_tensor(conv[:, t, :], ybank[t][:, :], zs[:, t, :], ALU.mult).then_inc(S["yz_done"], 1)
                    for i in range(2):
                        dve.wait_ge(S["out_psum"], 2 * b + i + 1)
                        pair = x[:, 2 * i:2 * i + 2, :].rearrange("p s d -> p (s d)")
                        nc.vector.tensor_tensor(pair, pair, fbank[i][:, :], ALU.add).then_inc(S["out_added"], 1)

            @block.tensor
            def _(pe):
                pe.wait_ge(S["params_loaded"], 16 * N_PARAMS)
                pe.wait_ge(S["dp_diag"], DT)
                pe.sem_inc(S["sum_done"], 2)
                with pe.Fori(0, B) as b:
                    pe.wait_ge(ns.xln, ST * b + ST)
                    pe.wait_ge(S["out_added"], 2 * b + 2)
                    transpose_tiles(nc, xln, ident, fbank, S["xt_psum"])
                    pe.wait_ge(S["xt_ready"], KD * b + KD)
                    pe.wait_ge(S["soft_done"], DT * b + DT)
                    for t in range(2 * DT):
                        if t >= DT:
                            pe.wait_ge(S["xz_read"], 2 * DT * b + t - DT + 1)
                        for k in range(KD):
                            ins = nc.tensor.matmul(fbank[t % DT][:, :], w_in[:, k, t * P:(t + 1) * P], xt[:, k, :],
                                                   start=(k == 0), stop=(k == KD - 1))
                        ins.then_inc(S["xz_psum"], 1)
                    pe.wait_ge(S["xc_ready"], b + 1)
                    pe.wait_ge(S["xz_read"], 2 * DT * b + 2 * DT)
                    for k in range(DT):
                        ins = nc.tensor.matmul(fbank[0][0:RK + 2 * NS, :], w_x[:, k, :], xc[:, k, :],
                                               start=(k == 0), stop=(k == DT - 1))
                    ins.then_inc(S["dbc_psum"], 1)
                    pe.wait_ge(S["dbc_ready"], b + 1)
                    for t in range(DT):
                        nc.tensor.matmul(fbank[t][:, :], w_dt[:, t * P:(t + 1) * P], dbc[0:RK, :],
                                         start=True, stop=True).then_inc(S["delta_psum"], 1)
                    pe.wait_ge(S["yz_done"], DT * b + DT)
                    for n in range(NS):
                        pe.wait_ge(S["hc_ready"], NS * b + n + 3)
                        for t in range(DT):
                            ins = nc.tensor.matmul(ybank[t][:, :], ident[:, :], hc[n % 2][:, t, :],
                                                   start=(n == 0), stop=False)
                        ins.then_inc(S["sum_done"], 1)
                    for t in range(DT):
                        ins = nc.tensor.matmul(ybank[t][:, :], dp_diag[:, t, :], xc[:, t, :], start=False, stop=True)
                    ins.then_inc(S["y_psum"], 1)
                    pe.wait_ge(S["yz_done"], DT * b + 2 * DT)
                    pe.wait_ge(S["soft_done"], DT * b + 2 * DT)
                    for i in range(2):
                        for st in range(2 * i, 2 * i + 2):
                            for k in range(DT):
                                ins = nc.tensor.matmul(fbank[i][:, (st % 2) * D:(st % 2 + 1) * D],
                                                       conv[:, k, st * P:(st + 1) * P], w_out[:, k, :],
                                                       start=(k == 0), stop=(k == DT - 1))
                        ins.then_inc(S["out_psum"], 1)
        m.end_phase()


def moe_phase(nc, banks, consts, weights, x_in, x_out, prm, second):
    tag = "moe2" if second else "moe1"
    ident, eps = consts["ident"], consts["eps"]
    with ExitStack() as ctx:
        m = Mem(nc, ctx)
        gate = m.sb(f"{tag}_gate", P, KD, E)
        gate_b = m.sb(f"{tag}_gate_b", E, 1)
        b1 = m.sb(f"{tag}_b1", P, E, MH)
        b2 = m.sb(f"{tag}_b2", E, D)
        x = [m.sb(f"{tag}_x{i}", P, ST, D) for i in range(2)]
        xln = m.sb(f"{tag}_xln", P, ST, D)
        xt = m.sb(f"{tag}_xt", P, KD, L)
        nb = NormBufs(m, tag)
        logits = m.sb(f"{tag}_logits", E, L)
        nmax = m.sb(f"{tag}_nmax", E, 1)
        total = m.sb(f"{tag}_total", E, 1)
        inv = m.sb(f"{tag}_inv", E, 1)
        probs = m.sb(f"{tag}_probs", E, L)
        top = m.sb(f"{tag}_top", E, TOP)
        rest = m.sb(f"{tag}_rest", E, L)
        route = m.sb(f"{tag}_route", E, L)
        route_all = m.sb(f"{tag}_route_all", E, B, L)
        route_t = m.sb(f"{tag}_route_t", P, ST, E)
        merged = m.sb(f"{tag}_merged", P, KD, E, B)
        pre = m.sb(f"{tag}_pre", P, EG, MH, B)
        act_h = m.sb(f"{tag}_gelu", P, EG, MH, B)
        o_t = m.sb(f"{tag}_o_t", P, KD, B, E)
        o_all = m.sb(f"{tag}_o_all", E, B, D)

        ns = NormSems(m, tag)
        S = {k: m.sem(f"{tag}_{k}") for k in (
            "params_loaded", "x_loaded", "xt_psum", "xt_ready", "logit_psum", "soft", "exp_done",
            "route_ready", "route_kept", "route_t_psum", "route_t_ready", "merged_psum", "merged_ready",
            "pre_ready", "gelu_ready", "o_copied", "o_tr_psum", "o_ready",
            "x_again0", "x_again1", "y_psum", "y_added", "x_stored0", "x_stored1")}
        N_PARAMS = 4
        done_before = NG if second else 0
        loaded_before = 16 * (NG if second else 1)
        SOFT = 6

        def store_sum(sp, b):
            sp.wait_ge(S["y_added"], 2 * b + 2)
            sp.dma_start(token_major(x_out, b), x[b % 2][:, :, :]).then_inc(S[f"x_stored{b % 2}"], 16)

        passed = m.sem(f"sync_passed_{m.nc.next_id()}")
        with nc.Block() as block:
            @block.sync
            def _(sp):
                for dst, src in ((gate[:, :, :], prm["gate_wT"].rearrange("(k p) e -> p k e", p=P)),
                                 (gate_b[:, :], prm["gate_b"].unsqueeze(1)),
                                 (b1[:, :, :], weights.w1_dram[:, D, :].rearrange("e (p m) -> p e m", m=MH)),
                                 (b2[:, :], weights.w2_dram[:, HID, :])):
                    sp.dma_start(dst, src).then_inc(S["params_loaded"], 16)
                with sp.Fori(0, B) as b:
                    carried_wait(sp, passed, (ns.xln, ST * b + ST))
                    sp.dma_start(x[0][:, :, :], token_major(x_in, b)).then_inc(S["x_loaded"], 16)
                with sp.Fori(1, NG) as g:
                    group = (NG - 1) - g if second else g
                    for j in range(EG):
                        carried_wait(sp, passed, (weights.w1_used[j], g + done_before), (weights.w2_used[j], g + done_before))
                        weights.load(nc, j, group)
                for b in range(B):
                    i = b % 2
                    if b == 0:
                        sp.wait_ge(ns.xln, ST * (B + 1))
                    if b >= 2:
                        sp.wait_ge(S[f"x_stored{i}"], 16 * (b // 2))
                    sp.dma_start(x[i][:, :, :], token_major(x_in, b)).then_inc(S[f"x_again{i}"], 16)
                    if b >= 1:
                        store_sum(sp, b - 1)
                store_sum(sp, B - 1)
                for i in range(2):
                    sp.wait_ge(S[f"x_stored{i}"], 16 * (B // 2))

            @block.gpsimd
            def _(pool):
                pool.sem_inc(S["route_kept"], 1)
                with pool.Fori(0, B) as b:
                    pool.wait_ge(S["route_ready"], b + 1)
                    nc.gpsimd.tensor_copy(route_all[:, ds(b, 1), :].rearrange("e o l -> e (o l)"),
                                          route[:, :]).then_inc(S["route_kept"], 1)

            @block.scalar
            def _(act):
                act.wait_ge(S["params_loaded"], 16 * N_PARAMS)
                with act.Fori(0, B) as b:
                    norm_scalar(nc, act, b, nb, ns, eps)
                    for kt in range(KD):
                        act.wait_ge(S["xt_psum"], KD * b + kt + 1)
                        nc.scalar.copy(xt[:, kt, :], banks[kt][:, :]).then_inc(S["xt_ready"], 1)
                    act.wait_ge(S["soft"], SOFT * b + 2)
                    nc.scalar.activation(probs[:, :], logits[:, :], ACT.Exp, bias=nmax[:, :],
                                         accum_out=total[:, :]).then_inc(S["exp_done"], 1)
                act.sem_inc(S["gelu_ready"], EG)
                with act.Fori(0, NG) as g:
                    for j in range(EG):
                        act.wait_ge(S["pre_ready"], EG * g + EG + j + 1)
                        nc.scalar.activation(act_h[:, j, :, :], pre[:, j, :, :], ACT.Gelu).then_inc(S["gelu_ready"], 1)

            @block.vector
            def _(dve):
                dve.sem_inc(ns.xln, ST)
                dve.sem_inc(S["merged_ready"], KD)
                dve.wait_ge(S["params_loaded"], 16 * N_PARAMS)
                with dve.Fori(0, B) as b:
                    dve.wait_ge(S["x_loaded"], 16 * b + 16)
                    norm_vector(nc, dve, b, x[0], xln, nb, ns)
                    ch = Chain(dve, S["soft"], SOFT * b)
                    dve.wait_ge(S["logit_psum"], b + 1)
                    ch.step(nc.vector.tensor_scalar(logits[:, :], banks[2][0:E, :], gate_b[:, :], None, ALU.add))
                    ch.wait()
                    ch.step(nc.vector.tensor_reduce(nmax[:, :], logits[:, :], AX_X, ALU.max, negate=True))
                    dve.wait_ge(S["exp_done"], b + 1)
                    ch.step(nc.vector.reciprocal(inv[:, :], total[:, :]))
                    ch.wait()
                    ch.step(nc.vector.tensor_scalar(probs[:, :], probs[:, :], inv[:, :], None, ALU.mult))
                    ch.wait(passed)
                    ch.step(nc.vector.max(top[:, :], probs[:, :]))
                    ch.wait(passed)
                    ch.step(nc.vector.match_replace(rest[:, :], top[:, :], probs[:, :], 0.0))
                    ch.wait()
                    dve.wait_ge(S["route_kept"], b + 1)
                    nc.vector.tensor_tensor(route[:, :], probs[:, :], rest[:, :], ALU.subtract).then_inc(S["route_ready"], 1)
                    dve.wait_ge(S["route_t_psum"], b + 1)
                    nc.vector.tensor_copy(route_t[:, :, :].rearrange("p s e -> p (s e)"),
                                          banks[3][:, 0:ST * E]).then_inc(S["route_t_ready"], 1)
                    dve.wait_ge(S["merged_psum"], b + 1)
                    for t in range(KD):
                        nc.vector.tensor_copy(merged[:, t, :, ds(b, 1)].rearrange("p e o -> p (e o)"),
                                              banks[4][:, t * E:(t + 1) * E]).then_inc(S["merged_ready"], 1)
                dve.sem_inc(S["o_copied"], 1)
                dve.sem_inc(S["pre_ready"], EG)
                with dve.Fori(0, NG) as g:
                    group = (NG - 1) - g if second else g
                    for j in range(EG):
                        carried_wait(dve, passed, (weights.w1_used[j], g + 1 + done_before),
                                     (S["gelu_ready"], EG * g + j + 1))
                        nc.vector.tensor_tensor(
                            pre[:, j, :, :], banks[j][:, 0:MH * B].rearrange("p (m b) -> p m b", b=B),
                            free_bcast(b1[:, ds(group * EG + j, 1), :].rearrange("p o m -> p (o m)"), 2, B),
                            ALU.add).then_inc(S["pre_ready"], 1)
                    carried_wait(dve, passed, (weights.w2_used[EG - 1], g + 1 + done_before))
                    for t in range(KD):
                        ins = nc.vector.tensor_copy(
                            o_t[:, t, :, ds(group * EG, EG)],
                            banks[6][:, 0:EG * KD * B].rearrange("p (j t b) -> p t b j", j=EG, t=KD)[:, t, :, :])
                    ins.then_inc(S["o_copied"], 1)
                for q in range(4):
                    dve.wait_ge(S["o_tr_psum"], q + 1)
                    nc.vector.tensor_tensor(o_all[:, 2 * q:2 * q + 2, :],
                                            banks[q][0:E, :].rearrange("e (b d) -> e b d", d=D),
                                            free_bcast(b2[:, :], 1, 2), ALU.add).then_inc(S["o_ready"], 1)
                for b in range(B):
                    dve.wait_ge(S[f"x_again{b % 2}"], 16 * (b // 2 + 1))
                    for i in range(2):
                        dve.wait_ge(S["y_psum"], 2 * b + i + 1)
                        pair = x[b % 2][:, 2 * i:2 * i + 2, :].rearrange("p s d -> p (s d)")
                        nc.vector.tensor_tensor(pair, pair, banks[4 + (2 * b + i) % 4][:, :],
                                                ALU.add).then_inc(S["y_added"], 1)

            @block.tensor
            def _(pe):
                pe.wait_ge(S["params_loaded"], 16 * N_PARAMS)
                with pe.Fori(0, B) as b:
                    pe.wait_ge(ns.xln, ST * b + 2 * ST)
                    transpose_tiles(nc, xln, ident, banks, S["xt_psum"])
                    pe.wait_ge(S["xt_ready"], KD * b + KD)
                    for k in range(KD):
                        ins = nc.tensor.matmul(banks[2][0:E, :], gate[:, k, :], xt[:, k, :],
                                               start=(k == 0), stop=(k == KD - 1))
                    ins.then_inc(S["logit_psum"], 1)
                    carried_wait(pe, passed, (S["route_ready"], b + 1))
                    for st in range(ST):
                        ins = nc.tensor.transpose(banks[3][:, st * E:(st + 1) * E], route[:, st * P:(st + 1) * P],
                                                  ident[0:E, 0:E])
                    ins.then_inc(S["route_t_psum"], 1)
                    pe.wait_ge(S["route_t_ready"], b + 1)
                    pe.wait_ge(S["merged_ready"], KD * b + KD)
                    for t in range(KD):
                        for st in range(ST):
                            ins = nc.tensor.matmul(banks[4][:, t * E:(t + 1) * E],
                                                   xln[:, st, t:D:KD], route_t[:, st, :],
                                                   start=(st == 0), stop=(st == ST - 1))
                    ins.then_inc(S["merged_psum"], 1)
                pe.wait_ge(S["merged_ready"], KD * (B + 1))
                pe.wait_ge(S["route_kept"], B + 1)
                with pe.Fori(0, NG) as g:
                    group = (NG - 1) - g if second else g

                    def hidden(j):
                        carried_wait(pe, passed, (weights.w1_loaded[j], 16 * g + loaded_before),
                                     (S["pre_ready"], EG * g + j + 1))
                        for mt in range(MH):
                            for t in range(KD):
                                ins = nc.tensor.matmul(
                                    banks[j][:, mt * B:(mt + 1) * B],
                                    weights.w1[j][:, t, mt:HID:MH],
                                    merged[:, t, ds(group * EG + j, 1), :].rearrange("p o b -> p (o b)"),
                                    start=(t == 0), stop=(t == KD - 1))
                        ins.then_inc(weights.w1_used[j], 1)

                    def output(j):
                        pe.wait_ge(weights.w2_loaded[j], 16 * g + loaded_before)
                        pe.wait_ge(S["gelu_ready"], EG * g + EG + j + 1)
                        if j == 0:
                            pe.wait_ge(S["o_copied"], g + 1)
                        for t in range(KD):
                            for k in range(MH):
                                ins = nc.tensor.matmul(banks[6][:, (j * KD + t) * B:(j * KD + t + 1) * B],
                                                       weights.w2[j][:, k, t * P:(t + 1) * P], act_h[:, j, k, :],
                                                       start=(k == 0), stop=(k == MH - 1))
                        ins.then_inc(weights.w2_used[j], 1)

                    for j in range(EG):
                        hidden(j)
                        if j:
                            output(j - 1)
                    output(EG - 1)
                pe.wait_ge(S["o_copied"], NG + 1)
                for b in range(B):
                    for t in range(KD):
                        ins = nc.tensor.transpose(banks[b // 2][0:E, (b % 2) * D + t * P:(b % 2) * D + (t + 1) * P],
                                                  o_t[:, t, b, :], ident[:, :])
                    if b % 2:
                        ins.then_inc(S["o_tr_psum"], 1)
                for b in range(B):
                    if b % 2 == 0:
                        pe.wait_ge(S["o_ready"], b // 2 + 1)
                    for i in range(2):
                        if 2 * b + i >= 4:
                            pe.wait_ge(S["y_added"], 2 * b + i - 3)
                        for st in range(2 * i, 2 * i + 2):
                            ins = nc.tensor.matmul(banks[4 + (2 * b + i) % 4][:, (st % 2) * D:(st % 2 + 1) * D],
                                                   route_all[:, b, st * P:(st + 1) * P], o_all[:, b, :],
                                                   start=True, stop=True)
                        ins.then_inc(S["y_psum"], 1)
        m.end_phase()


def delta_phase(nc, banks, consts, x_in, x_out, prm, n_scratch, t_scratch):
    ident, eps = consts["ident"], consts["eps"]
    NT = 3 * KD
    with ExitStack() as ctx:
        m = Mem(nc, ctx)
        w_qkv = m.sb("w_qkv", P, KD, 3 * D)
        w_gates = m.sb("w_gates", P, KD, 2 * H)
        w_o = m.sb("w_o", P, KD, D)
        conv_w = m.sb("conv_w_qkv", P, NT, KC)
        mix_bias = m.sb("mix_bias", P, 2, H)
        o_norm = m.sb("o_norm", P, DK)
        eps_l2 = m.sb("eps_l2", P, 1)
        neg_strict = m.sb("neg_strict", P, C)
        upper = m.sb("upper", P, C)
        head_mask = m.sb("head_mask", P, P)
        x = m.sb("x_delta", P, ST, D)
        xln = m.sb("xln_delta", P, ST, D)
        xt = m.sb("xt_delta", P, KD, L)
        nb = NormBufs(m, "delta")
        xpad = m.sb("xpad_qkv", P, NT, KC - 1 + L)
        conv = m.sb("conv_qkv", P, NT, L)
        feat = m.sb("feat", P, NT, L)
        gates = m.sb("gates", P, ST, 2 * H)
        tok = m.sb("tok", P, ST, NT * P)
        ssq = m.sb("ssq", P, ST * 2 * H)
        rnorm = m.sb("rnorm", P, ST * 2 * H)
        kb = m.sb("beta_k", P, ST, D)
        vb = m.sb("beta_v", P, ST, D)
        n_tok = m.sb("n_tok", P, ST, H, C)
        attn_t = m.sb("attn_t", P, ST, H, C)
        n_lane = m.sb("n_lane", P, C, C)
        t_lane = m.sb("t_lane", P, C, C)
        prod = m.sb("prod", P, C * C)
        t_tok = m.sb("t_tok", P, ST, H, C)
        y = m.sb("y_chunk", P, KD, P)
        u = m.sb("u_chunk", P, KD, P)
        state = [m.sb(f"s_delta{i}", P, P) for i in range(KD)]
        o = m.sb("o_delta", P, ST, D)
        oms = m.sb("o_ms", P, ST * H)
        ostd = m.sb("o_std", P, ST * H)
        orstd = m.sb("o_rstd", P, ST * H)
        squares = conv[:, 0:4, :].rearrange("p t l -> p (t l)")

        ns = NormSems(m, "delta")
        S = {k: m.sem("de_" + k) for k in (
            "params_loaded", "masks", "mix_ready", "lane_init", "x_loaded", "xt_psum", "xt_ready", "qkv_psum",
            "qkv_read", "conv_step", "feat_ready", "gate_psum", "gate_pre", "gate_ready", "tok_psum", "tok_ready",
            "sq_ready", "ssq_ready", "l2_std", "l2_ready", "pool_step", "featn_psum", "featn_ready", "gram_psum",
            "gram_read", "n_stored", "n_loaded", "solve", "t_stored", "t_loaded", "x_chunk", "y_ready", "u_psum",
            "u_ready", "s_psum", "s_ready", "o_psum", "o_read", "o_sq", "o_ms", "o_std", "o_rstd", "ot_psum",
            "ot_ready", "out_psum", "out_added", "x_stored")}
        N_PARAMS = 12
        KPB = (KC - 1) * NT
        SOLVE = 2 * (C - 1)
        CH = KD * (NC - 1)
        POOL = 7

        passed = m.sem(f"sync_passed_{m.nc.next_id()}")
        with nc.Block() as block:
            @block.sync
            def _(sp):
                for dst, src in [(w_qkv[:, :, i * D:(i + 1) * D], prm[f"{n}_w"].rearrange("(k p) n -> p k n", p=P))
                                 for i, n in enumerate("qkv")] + \
                        [(conv_w[:, KD * i:KD * i + KD, :], prm[f"conv_{n}_w"].rearrange("(k p) n -> p k n", p=P))
                         for i, n in enumerate("qkv")] + \
                        [(w_gates[:, :, i * H:(i + 1) * H], prm[n].rearrange("(k p) n -> p k n", p=P))
                         for i, n in enumerate(("b_w", "mix_w"))] + \
                        [(mix_bias[:, i, :], prm[n].partition_broadcast(P)) for i, n in enumerate(("mix_b", "mix_bias"))] + \
                        [(o_norm[:, :], prm["o_norm_w"].partition_broadcast(P)),
                         (w_o[:, :, :], prm["o_w"].rearrange("(k p) n -> p k n", p=P))]:
                    sp.dma_start(dst, src).then_inc(S["params_loaded"], 16)
                sp.sem_inc(S["x_stored"], 16)
                with sp.Fori(0, B) as b:
                    carried_wait(sp, passed, (S["x_stored"], 16 * b + 16))
                    sp.dma_start(x[:, :, :], token_major(x_in, b)).then_inc(S["x_loaded"], 16)
                    carried_wait(sp, passed, (S["gram_read"], ST * 2 * CT * (b + 1)))
                    for st in range(ST):
                        sp.dma_start(n_scratch[ds(b, 1), :, st * P:(st + 1) * P, :].rearrange("o h p j -> p (o h) j"),
                                     n_tok[:, st, :, :]).then_inc(S["n_stored"], 16)
                    carried_wait(sp, passed, (S["n_stored"], 16 * ST * b + 16 * ST))
                    sp.dma_start(n_lane[:, :, :], n_scratch[ds(b, 1), :, :, :].rearrange(
                        "o h (c i) j -> (o h c) i j", i=C)).then_inc(S["n_loaded"], 16)
                    carried_wait(sp, passed, (S["solve"], SOLVE * b + SOLVE))
                    sp.dma_start(t_scratch[ds(b, 1), :, :, :].rearrange("o h (c i) j -> (o h c) i j", i=C),
                                 t_lane[:, :, :]).then_inc(S["t_stored"], 16)
                    carried_wait(sp, passed, (S["t_stored"], 16 * b + 16))
                    for st in range(ST):
                        sp.dma_start(t_tok[:, st, :, :], t_scratch[ds(b, 1), :, st * P:(st + 1) * P, :].rearrange(
                            "o h p j -> p (o h) j")).then_inc(S["t_loaded"], 16)
                    carried_wait(sp, passed, (S["out_added"], 2 * b + 2))
                    sp.dma_start(token_major(x_out, b), x[:, :, :]).then_inc(S["x_stored"], 16)
                sp.wait_ge(S["x_stored"], 16 * (B + 1))

            @block.gpsimd
            def _(pool):
                nc.gpsimd.memset(neg_strict[:, :], -1.0).then_inc(S["masks"], 1)
                nc.gpsimd.memset(upper[:, :], 1.0).then_inc(S["masks"], 1)
                nc.gpsimd.memset(head_mask[:, :], 0.0).then_inc(S["masks"], 1)
                nc.gpsimd.memset(eps_l2[:, :], 1e-12).then_inc(S["masks"], 1)
                nc.gpsimd.memset(t_lane[:, :, :], 0.0).then_inc(S["lane_init"], 1)
                pool.wait_ge(S["masks"], 4)
                pool.wait_ge(S["lane_init"], 1)
                for c in range(CT):
                    rows = slice(c * C, (c + 1) * C)
                    nc.gpsimd.affine_select(out=neg_strict[rows, :], in_=neg_strict[rows, :], compare_op=ALU.is_gt,
                                            fill=0.0, base=0, pattern=[[-1, C]], channel_multiplier=1).then_inc(S["masks"], 1)
                    pool.wait_ge(S["masks"], 4 + 3 * c + 1)
                    nc.gpsimd.affine_select(out=upper[rows, :], in_=upper[rows, :], compare_op=ALU.is_ge,
                                            fill=0.0, base=0, pattern=[[1, C]], channel_multiplier=-1).then_inc(S["masks"], 1)
                    pool.wait_ge(S["masks"], 4 + 3 * c + 2)
                    nc.gpsimd.memset(head_mask[rows, rows], 1.0).then_inc(S["masks"], 1)
                    pool.wait_ge(S["masks"], 4 + 3 * c + 3)
                nc.gpsimd.memset(t_lane[:, :, :].rearrange("p i j -> p (i j)")[:, 0:C * C:C + 1], 1.0).then_inc(S["lane_init"], 1)
                with pool.Fori(0, B) as b:
                    ch = Chain(pool, S["pool_step"], POOL * b)
                    qk = tok[:, :, 0:2 * D].rearrange("p s (h d) -> p s h d", d=DK)
                    v = tok[:, :, 2 * D:3 * D].rearrange("p s (h d) -> p s h d", d=DK)
                    beta = free_bcast(gates[:, :, 0:H], 3, DK)
                    g = free_bcast(gates[:, :, H:2 * H], 3, DK)
                    heads = lambda t: t[:, :, :].rearrange("p s (h d) -> p s h d", d=DK)
                    pool.wait_ge(S["gate_ready"], b + 1)
                    pool.wait_ge(S["tok_ready"], NT * (b + 1))
                    ch.step(nc.gpsimd.tensor_tensor(heads(vb), v, beta, ALU.mult))
                    pool.wait_ge(S["l2_ready"], b + 1)
                    pool.wait_ge(S["sq_ready"], b + 1)
                    ch.step(nc.gpsimd.tensor_tensor(qk, qk, free_bcast(rnorm[:, :], 2, DK).rearrange(
                        "p (s h) d -> p s h d", s=ST), ALU.mult))
                    ch.wait()
                    ch.step(nc.gpsimd.tensor_tensor(heads(kb), qk[:, :, H:2 * H, :], beta, ALU.mult))
                    pool.wait_ge(S["o_read"], ST * KD * (b + 2))
                    ch.step(nc.gpsimd.tensor_tensor(heads(o), heads(o), g, ALU.mult))
                    ch.wait()
                    ch.step(nc.gpsimd.tensor_tensor(heads(o), heads(o), v, ALU.add))
                    pool.wait_ge(S["o_rstd"], b + 1)
                    ch.step(nc.gpsimd.tensor_tensor(heads(o), heads(o), free_bcast(orstd[:, :], 2, DK).rearrange(
                        "p (s h) d -> p s h d", s=ST), ALU.mult))
                    ch.wait()
                    flat = o[:, :, :].rearrange("p s (h d) -> p (s h) d", d=DK)
                    ch.step(nc.gpsimd.tensor_tensor(flat, flat, free_bcast(o_norm[:, :], 1, ST * H), ALU.mult))
                    assert ch.n == POOL

            @block.scalar
            def _(act):
                act.wait_ge(S["params_loaded"], 16 * N_PARAMS)
                act.wait_ge(S["masks"], 4 + 3 * CT)
                act.wait_ge(S["conv_step"], 1)
                with act.Fori(0, B) as b:
                    norm_scalar(nc, act, b, nb, ns, eps)
                    for kt in range(KD):
                        act.wait_ge(S["xt_psum"], KD * b + kt + 1)
                        nc.scalar.copy(xt[:, kt, :], banks[kt][:, :]).then_inc(S["xt_ready"], 1)
                    for t in range(NT):
                        act.wait_ge(S["qkv_psum"], NT * b + t + 1)
                        nc.scalar.activation(conv[:, t, :], banks[2 + t][:, :], ACT.Copy, scale=conv_w[:, t, KC - 1:KC])
                        nc.scalar.copy(xpad[:, t, KC - 1:], banks[2 + t][:, :]).then_inc(S["qkv_read"], 1)
                    act.wait_ge(S["gate_pre"], b + 1)
                    nc.scalar.activation(gates[:, :, :], gates[:, :, :], ACT.Sigmoid).then_inc(S["gate_ready"], 1)
                    for t in range(NT):
                        act.wait_ge(S["conv_step"], 1 + KPB * b + NT * (KC - 2) + t + 1)
                        nc.scalar.activation(feat[:, t, :], conv[:, t, :], ACT.Silu).then_inc(S["feat_ready"], 1)
                    for t in range(NT):
                        act.wait_ge(S["tok_psum"], NT * b + t + 1)
                        nc.scalar.copy(tok[:, :, t * P:(t + 1) * P],
                                       banks[2 + t][:, :].rearrange("p (s c) -> p s c", c=P)).then_inc(S["tok_ready"], 1)
                    act.wait_ge(S["tok_ready"], NT * (b + 1))
                    nc.scalar.activation(squares.rearrange("p (s c) -> p s c", s=ST), tok[:, :, 0:2 * D],
                                         ACT.Square).then_inc(S["sq_ready"], 1)
                    act.wait_ge(S["ssq_ready"], b + 1)
                    nc.scalar.activation(ssq[:, :], ssq[:, :], ACT.Sqrt, bias=eps_l2[:, :]).then_inc(S["l2_std"], 1)
                    for t in range(NT):
                        act.wait_ge(S["featn_psum"], NT * b + t + 1)
                        nc.scalar.copy(feat[:, t, :], banks[2 + t][:, :]).then_inc(S["featn_ready"], 1)
                    for n in range(NC):
                        for hh in range(KD):
                            rows = slice((n % CT) * C, (n % CT + 1) * C)
                            act.wait_ge(S["u_psum"], KD * NC * b + KD * n + hh + 1)
                            nc.scalar.copy(u[rows, hh, :], banks[hh][rows, 0:P]).then_inc(S["u_ready"], 1)
                    act.wait_ge(S["pool_step"], POOL * b + 5)
                    nc.scalar.activation(squares[:, 0:ST * D].rearrange("p (s c) -> p s c", s=ST), o[:, :, :],
                                         ACT.Square).then_inc(S["o_sq"], 1)
                    act.wait_ge(S["o_ms"], b + 1)
                    nc.scalar.activation(ostd[:, :], oms[:, :], ACT.Sqrt, bias=eps[:, :], scale=1.0 / DK).then_inc(S["o_std"], 1)
                    for kt in range(KD):
                        act.wait_ge(S["ot_psum"], KD * b + kt + 1)
                        nc.scalar.copy(xt[:, kt, :], banks[kt][:, :]).then_inc(S["ot_ready"], 1)

            @block.vector
            def _(dve):
                nc.vector.memset(xpad[:, :, 0:KC - 1], 0.0).then_inc(S["conv_step"], 1)
                dve.wait_ge(S["params_loaded"], 16 * N_PARAMS)
                nc.vector.tensor_tensor(mix_bias[:, 0, :], mix_bias[:, 0, :], mix_bias[:, 1, :], ALU.add).then_inc(S["mix_ready"], 1)
                dve.wait_ge(S["mix_ready"], 1)
                dve.wait_ge(S["conv_step"], 1)
                dve.wait_ge(S["masks"], 4 + 3 * CT)
                dve.wait_ge(S["lane_init"], 2)
                dve.sem_inc(S["o_read"], ST * KD)
                with dve.Fori(0, B) as b:
                    dve.wait_ge(S["x_loaded"], 16 * b + 16)
                    norm_vector(nc, dve, b, x, xln, nb, ns)
                    for k in range(KC - 1):
                        for t in range(NT):
                            if k == 0:
                                dve.wait_ge(S["qkv_read"], NT * b + t + 1)
                            else:
                                dve.wait_ge(S["conv_step"], 1 + KPB * b + NT * (k - 1) + t + 1)
                            nc.vector.scalar_tensor_tensor(conv[:, t, :], xpad[:, t, k:k + L], conv_w[:, t, k:k + 1],
                                                           conv[:, t, :], ALU.mult, ALU.add).then_inc(S["conv_step"], 1)
                        if k == 0:
                            dve.wait_ge(S["gate_psum"], b + 1)
                            gp = banks[0][:, 0:ST * 2 * H].rearrange("p (s h) -> p s h", s=ST)
                            nc.vector.tensor_copy(gates[:, :, 0:H], gp[:, :, 0:H])
                            nc.vector.tensor_tensor(gates[:, :, H:2 * H], gp[:, :, H:2 * H],
                                                    free_bcast(mix_bias[:, 0, :], 1, ST), ALU.add).then_inc(S["gate_pre"], 1)
                    dve.wait_ge(S["sq_ready"], b + 1)
                    nc.vector.tensor_reduce(ssq[:, :], squares.rearrange("p (a d) -> p a d", d=DK),
                                            AX_X, ALU.add).then_inc(S["ssq_ready"], 1)
                    dve.wait_ge(S["l2_std"], b + 1)
                    nc.vector.reciprocal(rnorm[:, :], ssq[:, :]).then_inc(S["l2_ready"], 1)
                    for st in range(ST):
                        for i, (dst, mask) in enumerate(((n_tok, neg_strict), (attn_t, upper))):
                            dve.wait_ge(S["gram_psum"], 2 * ST * b + 2 * st + i + 1)
                            for c in range(CT):
                                rows = slice(c * C, (c + 1) * C)
                                blocks = banks.whole[rows, HS * i:HS * i + HS, :].rearrange("p g (q k) -> p q g k", k=P)[
                                    :, 0:KD, :, c * C:(c + 1) * C]
                                out = dst[rows, st, :, :].rearrange("p (q g) j -> p q g j", g=HS)
                                m4 = free_bcast(free_bcast(mask[rows, :], 1, HS), 1, KD)
                                nc.vector.tensor_tensor(out, blocks, m4, ALU.mult).then_inc(S["gram_read"], 1)
                    ch = Chain(dve, S["solve"], SOLVE * b)
                    dve.wait_ge(S["n_loaded"], 16 * b + 16)
                    for i in range(1, C):
                        pr = prod[:, 0:i * i].rearrange("p (k j) -> p k j", j=i)
                        if i > 1:
                            ch.wait()
                        ch.step(nc.vector.tensor_tensor(pr, t_lane[:, 0:i, 0:i], free_bcast(n_lane[:, i, 0:i], 1, i), ALU.mult))
                        ch.wait()
                        ch.step(nc.vector.tensor_reduce(t_lane[:, 0:i, i], pr, AX_X, ALU.add))
                    assert ch.n == SOLVE
                    for n in range(NC):
                        st, rows = n // CT, slice((n % CT) * C, (n % CT + 1) * C)
                        if n:
                            for hh in range(KD):
                                dve.wait_ge(S["x_chunk"], CH * b + KD * (n - 1) + hh + 1)
                                nc.vector.tensor_tensor(y[rows, hh, :], vb[rows, st, hh * P:(hh + 1) * P],
                                                        banks[hh][rows, 0:P], ALU.subtract).then_inc(S["y_ready"], 1)
                        if n < NC - 1:
                            for hh in range(KD):
                                dve.wait_ge(S["s_psum"], CH * b + KD * n + hh + 1)
                                nc.vector.tensor_tensor(state[hh][:, :], banks[2 + hh][:, 0:P], head_mask[:, :],
                                                        ALU.mult).then_inc(S["s_ready"], 1)
                        if n % CT == CT - 1:
                            for hh in range(KD):
                                dve.wait_ge(S["o_psum"], ST * KD * b + KD * st + hh + 1)
                                nc.vector.tensor_tensor(o[:, st, hh * P:(hh + 1) * P], banks[4 + 2 * (st % 2) + hh][:, 0:P],
                                                        tok[:, st, 2 * D + hh * P:2 * D + (hh + 1) * P],
                                                        ALU.subtract).then_inc(S["o_read"], 1)
                    dve.wait_ge(S["o_sq"], b + 1)
                    nc.vector.tensor_reduce(oms[:, :], squares[:, 0:ST * D].rearrange("p (a d) -> p a d", d=DK),
                                            AX_X, ALU.add).then_inc(S["o_ms"], 1)
                    dve.wait_ge(S["o_std"], b + 1)
                    nc.vector.reciprocal(orstd[:, :], ostd[:, :]).then_inc(S["o_rstd"], 1)
                    for i in range(2):
                        dve.wait_ge(S["out_psum"], 2 * b + i + 1)
                        pair = x[:, 2 * i:2 * i + 2, :].rearrange("p s d -> p (s d)")
                        nc.vector.tensor_tensor(pair, pair, banks[2 + i][:, :], ALU.add).then_inc(S["out_added"], 1)

            @block.tensor
            def _(pe):
                pe.wait_ge(S["params_loaded"], 16 * N_PARAMS)
                with pe.Fori(0, B) as b:
                    pe.wait_ge(ns.xln, ST * b + ST)
                    transpose_tiles(nc, xln, ident, banks, S["xt_psum"])
                    pe.wait_ge(S["xt_ready"], KD * b + KD)
                    for t in range(NT):
                        for k in range(KD):
                            ins = nc.tensor.matmul(banks[2 + t][:, :], w_qkv[:, k, t * P:(t + 1) * P], xt[:, k, :],
                                                   start=(k == 0), stop=(k == KD - 1))
                        ins.then_inc(S["qkv_psum"], 1)
                    for st in range(ST):
                        for k in range(KD):
                            ins = nc.tensor.matmul(banks[0][:, st * 2 * H:(st + 1) * 2 * H], xt[:, k, st * P:(st + 1) * P],
                                                   w_gates[:, k, :], start=(k == 0), stop=(k == KD - 1))
                    ins.then_inc(S["gate_psum"], 1)
                    for t in range(NT):
                        pe.wait_ge(S["feat_ready"], NT * b + t + 1)
                        for st in range(ST):
                            ins = nc.tensor.transpose(banks[2 + t][:, st * P:(st + 1) * P], feat[:, t, st * P:(st + 1) * P], ident[:, :])
                        ins.then_inc(S["tok_psum"], 1)
                    for t in range(NT):
                        if t == 0:
                            pe.wait_ge(S["pool_step"], POOL * b + 2)
                            pe.wait_ge(S["tok_ready"], NT * (b + 1))
                        if t == 2 * KD:
                            pe.wait_ge(S["pool_step"], POOL * b + 3)
                        for st in range(ST):
                            src = tok[:, st, t * P:(t + 1) * P] if t < 2 * KD else kb[:, st, (t - 2 * KD) * P:(t - 2 * KD + 1) * P]
                            ins = nc.tensor.transpose(banks[2 + t][:, st * P:(st + 1) * P], src, ident[:, :])
                        ins.then_inc(S["featn_psum"], 1)
                    pe.wait_ge(S["featn_ready"], NT * (b + 1))
                    q_f, k_f, kb_f = feat[:, 0:KD, :], feat[:, KD:2 * KD, :], feat[:, 2 * KD:3 * KD, :]
                    for st in range(ST):
                        cols = slice(st * P, (st + 1) * P)
                        for i, (left, right) in enumerate(((kb_f, k_f), (k_f, q_f))):
                            if st:
                                pe.wait_ge(S["gram_read"], ST * 2 * CT * b + 2 * CT * (st - 1) + CT * (i + 1))
                            for hh in range(KD):
                                for g in range(HS):
                                    rows = slice(g * DK, (g + 1) * DK)
                                    ins = nc.tensor.matmul(banks[HS * i + g][:, hh * P:(hh + 1) * P], left[rows, hh, cols],
                                                           right[rows, hh, cols], start=True, stop=True)
                            ins.then_inc(S["gram_psum"], 1)
                    pe.wait_ge(S["gram_read"], ST * 2 * CT * (b + 1))
                    carried_wait(pe, passed, (S["t_loaded"], 16 * ST * b + 16 * ST))
                    for n in range(NC):
                        st, c = n // CT, n % CT
                        rows, cols = slice(c * C, (c + 1) * C), slice(n * C, (n + 1) * C)
                        obank = [banks[4 + 2 * (st % 2) + hh] for hh in range(KD)]
                        if n:
                            for hh in range(KD):
                                pe.wait_ge(S["s_ready"], CH * b + KD * (n - 1) + hh + 1)
                                nc.tensor.matmul(banks[hh][rows, 0:P], kb_f[:, hh, cols], state[hh][:, :],
                                                 start=True, stop=True).then_inc(S["x_chunk"], 1)
                        if c == 0 and st >= 2:
                            pe.wait_ge(S["o_read"], ST * KD * (b + 1) + KD * (st - 1))
                        if n:
                            for hh in range(KD):
                                nc.tensor.matmul(obank[hh][rows, 0:P], q_f[:, hh, cols], state[hh][:, :],
                                                 start=True, stop=True, skip_group_check=True)
                        for hh in range(KD):
                            if n:
                                carried_wait(pe, passed, (S["y_ready"], CH * b + KD * (n - 1) + hh + 1))
                            for g in range(HS):
                                h, hc = hh * HS + g, slice(g * DK, (g + 1) * DK)
                                rhs = y[rows, hh, hc] if n else vb[rows, st, h * DK:(h + 1) * DK]
                                ins = nc.tensor.matmul(banks[hh][rows, hc], t_tok[rows, st, h, :], rhs,
                                                       start=True, stop=True)
                            ins.then_inc(S["u_psum"], 1)
                        for hh in range(KD):
                            carried_wait(pe, passed, (S["u_ready"], KD * NC * b + KD * n + hh + 1))
                            if n < NC - 1:
                                nc.tensor.matmul(banks[2 + hh][:, 0:P], tok[rows, st, D + hh * P:D + (hh + 1) * P], u[rows, hh, :],
                                                 start=(n == 0), stop=True, skip_group_check=True).then_inc(S["s_psum"], 1)
                        for hh in range(KD):
                            for g in range(HS):
                                h, hc = hh * HS + g, slice(g * DK, (g + 1) * DK)
                                ins = nc.tensor.matmul(obank[hh][rows, hc], attn_t[rows, st, h, :], u[rows, hh, hc],
                                                       start=(n == 0), stop=True, skip_group_check=True)
                            if c == CT - 1:
                                ins.then_inc(S["o_psum"], 1)
                    pe.wait_ge(S["pool_step"], POOL * b + POOL)
                    for kt in range(KD):
                        for st in range(ST):
                            ins = nc.tensor.transpose(banks[kt][:, st * P:(st + 1) * P], o[:, st, kt * P:(kt + 1) * P], ident[:, :])
                        ins.then_inc(S["ot_psum"], 1)
                    pe.wait_ge(S["ot_ready"], KD * b + KD)
                    for i in range(2):
                        for st in range(2 * i, 2 * i + 2):
                            for k in range(KD):
                                ins = nc.tensor.matmul(banks[2 + i][:, (st % 2) * D:(st % 2 + 1) * D], xt[:, k, st * P:(st + 1) * P],
                                                       w_o[:, k, :], start=(k == 0), stop=(k == KD - 1))
                        ins.then_inc(S["out_psum"], 1)
                    pe.wait_ge(S["out_added"], 2 * b + 2)
        m.end_phase()


class Banks:

    def __init__(self, whole):
        self.whole = whole

    def __getitem__(self, i):
        if isinstance(i, slice):
            return [self[j] for j in range(i.start, i.stop)]
        return self.whole[:, i, :]


def build(nc, a, out):
    ctx = ExitStack()
    with ctx:
        m = Mem(nc, ctx)
        banks = Banks(ctx.enter_context(nc.psum_tensor("psum", [P, 8, BANK], F32)))
        consts = {"ident": m.sb("ident", P, P), "eps": m.sb("eps", P, 1)}
        weights = Weights(m, a["w1"], a["w2"])
        x1, x2, x3 = (nc.dram_tensor(f"x_after_{i}", [B, L, D], F32, kind="Internal").ap() for i in (1, 2, 3))
        bc_scratch = nc.dram_tensor("bc_scratch", [B, 2 * NS, L], F32, kind="Internal").ap()
        n_scratch = nc.dram_tensor("n_scratch", [B, H, L, C], F32, kind="Internal").ap()
        t_scratch = nc.dram_tensor("t_scratch", [B, H, L, C], F32, kind="Internal").ap()
        const_ready = m.sem("const_ready")
        with nc.Block() as block:
            @block.gpsimd
            def _(pool):
                nc.gpsimd.memset(consts["ident"][:, :], 0.0).then_inc(const_ready, 1)
                nc.gpsimd.memset(consts["eps"][:, :], EPS).then_inc(const_ready, 1)
                pool.wait_ge(const_ready, 2)
                nc.gpsimd.affine_select(out=consts["ident"][:, :], in_=consts["ident"][:, :], compare_op=ALU.not_equal,
                                        fill=1.0, base=0, pattern=[[-1, P]], channel_multiplier=1).then_inc(const_ready, 1)
                pool.wait_ge(const_ready, 3)
        steps = [lambda i, o: mamba_phase(nc, banks, consts, weights, i, o, a, bc_scratch),
                 lambda i, o: moe_phase(nc, banks, consts, weights, i, o, a, False),
                 lambda i, o: delta_phase(nc, banks, consts, i, o, a, n_scratch, t_scratch),
                 lambda i, o: moe_phase(nc, banks, consts, weights, i, o, a, True)][:PHASES]
        flow = [a["x"], x1, x2, x3][:PHASES] + [out]
        for i, step in enumerate(steps):
            step(flow[i], flow[i + 1])


PHASES = 4
_A, _B, _F = "L0_attn_a_", "L0_attn_b_", "L0_ffn_"
_PLAIN = {_A + "x": "x", _A + "conv_w": "conv_w", _A + "A_log": "A_log",
          **{_B + n: n for n in ("q_w", "k_w", "v_w", "conv_q_w", "conv_k_w", "conv_v_w", "b_w", "mix_w", "mix_b",
                                 "mix_bias", "o_norm_w", "o_w")},
          _F + "gate_b": "gate_b", _F + "w1": "w1", _F + "w2": "w2"}
_TRANSPOSED = {_A + "W_in": "W_inT", _A + "W_x": "W_xT", _A + "W_dt": "W_dtT", _A + "W_out": "W_outT",
               _F + "gate_w": "gate_wT"}
_COLUMNS = {_A + "conv_b": "conv_bT", _A + "b_dt": "b_dtT", _A + "Dp": "DpT"}


def kernel(**inputs):
    import numpy as _np
    import concourse.bacc as _bacc
    from concourse import mybir as _mybir
    from concourse.bass_utils import run_bass_kernel_spmd as _run

    nc = _bacc.Bacc("TRN2", target_bir_lowering=False, num_devices=1)
    arrays, args = {}, {}
    for names, lay in ((_PLAIN, lambda v: v), (_TRANSPOSED, lambda v: v.T), (_COLUMNS, lambda v: v.reshape(-1, P).T)):
        for name, short in names.items():
            v = _np.ascontiguousarray(lay(_np.asarray(inputs[name])))
            arrays[f"in_{short}"] = v
            args[short] = nc.dram_tensor(f"in_{short}", v.shape, _mybir.dt.from_np(v.dtype), kind="ExternalInput").ap()
    out = nc.dram_tensor("out_0", (B, L, D), F32, kind="ExternalOutput").ap()
    build(nc, args, out)
    r = _run(nc, [arrays], core_ids=[0])
    return r.results[0]["out_0"]
```

```python
from contextlib import ExitStack

import concourse.bass as bass
from concourse import mybir

ALU = mybir.AluOpType
ACT = mybir.ActivationFunctionType
F32 = mybir.dt.float32
AX_X = mybir.AxisListType.X
ds = bass.ds

P = 128
B, L, D = 8, 512, 256
ST = L // P
KD = D // P
BANK = 512
EPS = 1e-5

DI, NS, RK, KC = 512, 16, 64, 4
DT = DI // P
H, DK, C = 8, 32, 32
HS = P // DK
NC = L // C
CT = P // C
E, HID, TOP = 32, 1024, 8
EG, EQ = 4, 32
NG = E // EG
GP = NG // 2
QB = 4
HALVES = B // QB
MH = HID // P


class Mem:

    def __init__(self, nc, ctx):
        self.nc, self.ctx, self.sems = nc, ctx, []

    def sb(self, name, *shape):
        return self.ctx.enter_context(self.nc.sbuf_tensor(name, list(shape), F32))

    def sem(self, name):
        self.sems.append(self.nc.alloc_semaphore(name))
        return self.sems[-1]

    def end_phase(self):
        self.nc.clear_and_free_semaphores(self.sems)
        self.nc.all_engine_barrier()


class Chain:

    def __init__(self, eng, sem, base):
        self.eng, self.sem, self.base, self.n = eng, sem, base, 0

    def step(self, ins):
        self.n += 1
        ins.then_inc(self.sem, 1)

    def wait(self, passed=None):
        self.eng.wait_ge(self.sem, self.base + self.n)
        if passed:
            self.eng.sem_inc(passed, 1)


def free_bcast(ap, axis, n):
    shape = list(ap.shape)
    shape.insert(axis, n)
    return ap.unsqueeze(axis).to_broadcast(shape)


class NormSems:
    def __init__(self, m, tag):
        self.stats, self.turn, self.mv, self.std, self.rstd, self.xln = (
            m.sem(f"{tag}_{s}") for s in ("ln_stats", "ln_turn", "ln_mean_var", "ln_std", "ln_rstd", "ln_done"))


class NormBufs:
    def __init__(self, m, tag):
        self.stats = m.sb(f"{tag}_bn_stats", P, ST, 6)
        self.mv = m.sb(f"{tag}_mean_var", P, ST, 2)
        self.std = m.sb(f"{tag}_std", P, ST)
        self.rstd = m.sb(f"{tag}_rstd", P, ST)


def norm_vector(nc, dve, b, x, out, nb, ns):
    for st in range(ST):
        nc.vector.bn_stats(nb.stats[:, st, :], x[:, st, :]).then_inc(ns.stats, 1)
    carried_wait(dve, ns.turn, (ns.stats, ST * (b + 1)))
    for st in range(ST):
        nc.vector.bn_aggr(nb.mv[:, st, :], nb.stats[:, st, :]).then_inc(ns.mv, 1)
    dve.wait_ge(ns.std, b + 1)
    nc.vector.reciprocal(nb.rstd[:, :], nb.std[:, :]).then_inc(ns.rstd, 1)
    dve.wait_ge(ns.rstd, b + 1)
    for st in range(ST):
        nc.vector.tensor_scalar(out[:, st, :], x[:, st, :], nb.mv[:, st, 0:1], nb.rstd[:, st:st + 1],
                                ALU.subtract, ALU.mult).then_inc(ns.xln, 1)


def norm_scalar(nc, act, b, nb, ns, eps):
    act.wait_ge(ns.mv, ST * (b + 1))
    nc.scalar.activation(nb.std[:, :], nb.mv[:, :, 1], ACT.Sqrt, bias=eps[:, :]).then_inc(ns.std, 1)


def transpose_tiles(nc, xln, ident, banks, done):
    for kt in range(KD):
        for st in range(ST):
            ins = nc.tensor.transpose(banks[kt][:, st * P:(st + 1) * P], xln[:, st, kt * P:(kt + 1) * P], ident[:, :])
        ins.then_inc(done, 1)


def carried_wait(eng, passed, *waits):
    for sem, value in waits:
        eng.wait_ge(sem, value)
    eng.sem_inc(passed, 1)


def token_major(x_dram, b):
    if isinstance(b, int):
        return x_dram[b].rearrange("(s p) d -> p s d", p=P)
    return x_dram[ds(b, 1), :, :].rearrange("o (s p) d -> p (o s) d", p=P)


class Weights:

    def __init__(self, m, w1, w2):
        self.w1_dram, self.w2_dram = w1, w2
        self.w1, self.w2, self.loaded = [], [], []
        self.add_set(m, "first")
        self.loaded = [[m.sem(f"w{which}_set{s}_loaded") for which in (1, 2)] for s in range(2)]

    def add_set(self, m, tag):
        self.w1.append(m.sb(f"w1_{tag}", P, EG, KD, HID))
        self.w2.append(m.sb(f"w2_{tag}", P, EG, MH, D))

    def second_set(self, m, tag):
        del self.w1[1:], self.w2[1:]
        self.add_set(m, tag)

    def load(self, nc, s, which, group):
        slots, dram, rows, per = ((self.w1, self.w1_dram, D, KD), (self.w2, self.w2_dram, HID, MH))[which - 1]
        nc.sync.dma_start(slots[s][:, :, :, :], dram[ds(group * EG, EG), 0:rows, :].rearrange(
            "e (p t) n -> p e t n", t=per)).then_inc(self.loaded[s][which - 1], 16)


def mamba_phase(nc, banks, consts, weights, x_in, x_out, prm, scratch):
    ident, eps = consts["ident"], consts["eps"]
    ybank, fbank = banks[0:4], banks[4:8]
    with ExitStack() as ctx:
        m = Mem(nc, ctx)
        w_in = m.sb("w_in", P, KD, 2 * DI)
        w_x = m.sb("w_x", P, DT, RK + 2 * NS)
        w_dt = m.sb("w_dt", RK, DI)
        w_out = m.sb("w_out", P, DT, D)
        conv_w = m.sb("conv_w", P, DT, KC)
        conv_b = m.sb("conv_b", P, DT)
        b_dt = m.sb("b_dt", P, DT)
        dp = m.sb("dp", P, DT)
        a_neg = m.sb("a_neg", P, DT, NS)
        a_exp = m.sb("a_exp", P, DT, NS)
        dp_diag = m.sb("dp_diag", P, DT, P)
        x = m.sb("x_mamba", P, ST, D)
        dx = m.sb("delta_x", P, DT, L)
        xln = dx[:, 0:2, :].rearrange("p t l -> p (t l)").rearrange("p (s d) -> p s d", d=D)
        xt = dx[:, 2:4, :]
        nb = NormBufs(m, "mamba")
        xpad = m.sb("xpad", P, DT, KC - 1 + L)
        conv = m.sb("conv", P, DT, L)
        zs = m.sb("z_silu", P, DT, L)
        xc = m.sb("x_conv", P, DT, L)
        dbc = m.sb("dbc", RK + 2 * NS, L)
        delta = m.sb("delta", P, DT, L)
        bc = [m.sb(f"b_and_c{i}", P, 2, L) for i in range(2)]
        decay = [m.sb(f"decay{i}", P, DT, L) for i in range(2)]
        bx = [m.sb(f"bx{i}", P, DT, L) for i in range(2)]
        hs = m.sb("state", P, DT, L)
        hc = [m.sb(f"state_c{i}", P, DT, L) for i in range(2)]

        ns = NormSems(m, "mamba")
        S = {k: m.sem("ma_" + k) for k in (
            "params_loaded", "a_exp", "a_ready", "dp_diag", "pads_zero", "x_loaded", "xt_psum", "xt_ready",
            "xz_psum", "xz_read", "conv_step", "xc_ready", "dbc_psum", "dbc_ready", "bc_stored",
            "bc_loaded0", "bc_loaded1", "delta_psum", "soft", "soft_done", "delta_ready", "dx_ready", "decay_ready", "bx_ready",
            "scan_done", "hc_ready", "sum_done", "y_psum", "yz_done", "out_psum", "out_added", "x_stored")}
        N_PARAMS = 9

        passed = m.sem(f"sync_passed_{m.nc.next_id()}")
        with nc.Block() as block:
            @block.sync
            def _(sp):
                for dst, src in (
                        (w_in[:, :, :], prm["W_inT"].rearrange("(k p) n -> p k n", p=P)),
                        (w_x[:, :, :], prm["W_xT"].rearrange("(k p) n -> p k n", p=P)),
                        (w_dt[:, :], prm["W_dtT"]),
                        (w_out[:, :, :], prm["W_outT"].rearrange("(k p) n -> p k n", p=P)),
                        (conv_w[:, :, :], prm["conv_w"].rearrange("(t p) k -> p t k", p=P)),
                        (conv_b[:, :], prm["conv_bT"]),
                        (b_dt[:, :], prm["b_dtT"]),
                        (dp[:, :], prm["DpT"]),
                        (a_exp[:, :, :], prm["A_log"].rearrange("(t p) n -> p t n", p=P))):
                    sp.dma_start(dst, src).then_inc(S["params_loaded"], 16)
                weights.load(nc, 0, 1, 0)
                weights.load(nc, 0, 2, 0)
                sp.sem_inc(S["x_stored"], 16)
                with sp.Fori(0, B) as b:
                    carried_wait(sp, passed, (S["x_stored"], 16 * b + 16))
                    sp.dma_start(x[:, :, :], token_major(x_in, b)).then_inc(S["x_loaded"], 16)
                    carried_wait(sp, passed, (S["dbc_ready"], b + 1))
                    sp.dma_start(scratch[ds(b, 1), :, :].rearrange("o r l -> (o r) l"),
                                 dbc[RK:RK + 2 * NS, :]).then_inc(S["bc_stored"], 16)
                    carried_wait(sp, passed, (S["bc_stored"], 16 * b + 16))
                    for n in range(NS):
                        carried_wait(sp, passed, (S["hc_ready"], NS * b + n + 1), (S["bx_ready"], NS * b + n + 1))
                        src = scratch[ds(b, 1), n:n + NS + 1:NS, :].rearrange("o r l -> (o r) l")
                        sp.dma_start(bc[n % 2][:, :, :], src.partition_broadcast(P)).then_inc(
                            S[f"bc_loaded{n % 2}"], 16)
                    carried_wait(sp, passed, (S["out_added"], 2 * b + 4))
                    sp.dma_start(token_major(x_out, b), x[:, :, :]).then_inc(S["x_stored"], 16)
                sp.wait_ge(S["x_stored"], 16 * (B + 1))

            @block.gpsimd
            def _(pool):
                for i in range(2):
                    nc.gpsimd.memset(decay[i][:, :, 0], 0.0).then_inc(S["pads_zero"], 1)
                nc.gpsimd.memset(xpad[:, :, 0:KC - 1], 0.0).then_inc(S["pads_zero"], 1)
                pool.sem_inc(S["bx_ready"], 2)
                with pool.Fori(0, B) as b:
                    pool.wait_ge(S["soft"], 2 * b + 2)
                    nc.gpsimd.tensor_tensor(delta[:, :, :], delta[:, :, :], conv[:, :, :], ALU.add).then_inc(S["delta_ready"], 1)
                    pool.wait_ge(S["delta_ready"], b + 1)
                    pool.wait_ge(S["xc_ready"], b + 1)
                    nc.gpsimd.tensor_tensor(dx[:, :, :], delta[:, :, :], xc[:, :, :], ALU.mult).then_inc(S["dx_ready"], 1)
                    pool.wait_ge(S["dx_ready"], b + 1)
                    for n in range(NS):
                        pool.wait_ge(S[f"bc_loaded{n % 2}"], 16 * (NS // 2) * b + 16 * (n // 2 + 1))
                        pool.wait_ge(S["scan_done"], NS * b + n + 1)
                        nc.gpsimd.tensor_tensor(bx[n % 2][:, :, :], dx[:, :, :],
                                                free_bcast(bc[n % 2][:, 0, :], 1, DT), ALU.mult).then_inc(S["bx_ready"], 1)

            @block.scalar
            def _(act):
                act.wait_ge(S["params_loaded"], 16 * N_PARAMS)
                nc.scalar.activation(a_neg[:, :, :], a_exp[:, :, :], ACT.Exp).then_inc(S["a_exp"], 1)
                act.wait_ge(S["pads_zero"], 3)
                act.wait_ge(S["a_ready"], 1)
                act.sem_inc(S["soft_done"], DT)
                with act.Fori(0, B) as b:
                    norm_scalar(nc, act, b, nb, ns, eps)
                    for kt in range(KD):
                        act.wait_ge(S["xt_psum"], KD * b + kt + 1)
                        nc.scalar.copy(xt[:, kt, :], fbank[kt][:, :]).then_inc(S["xt_ready"], 1)
                    for t in range(DT):
                        act.wait_ge(S["xz_psum"], 2 * DT * b + t + 1)
                        nc.scalar.activation(conv[:, t, :], fbank[t][:, :], ACT.Identity, bias=conv_b[:, t:t + 1],
                                             scale=conv_w[:, t, KC - 1:KC])
                        nc.scalar.copy(xpad[:, t, KC - 1:], fbank[t][:, :]).then_inc(S["xz_read"], 1)
                    act.wait_ge(S["yz_done"], DT * b + DT)
                    for t in range(DT):
                        act.wait_ge(S["xz_psum"], 2 * DT * b + DT + t + 1)
                        nc.scalar.activation(zs[:, t, :], fbank[t][:, :], ACT.Silu).then_inc(S["xz_read"], 1)
                    act.wait_ge(S["conv_step"], DT * (KC - 1) * b + DT * (KC - 1))
                    nc.scalar.activation(xc[:, :, :], conv[:, :, :], ACT.Silu).then_inc(S["xc_ready"], 1)
                    act.wait_ge(S["dbc_psum"], b + 1)
                    nc.scalar.copy(dbc[:, :], fbank[0][0:RK + 2 * NS, :]).then_inc(S["dbc_ready"], 1)
                    for t in range(DT):
                        act.wait_ge(S["delta_psum"], DT * b + t + 1)
                        nc.scalar.activation(conv[:, t, :], fbank[t][:, :], ACT.Abs, bias=b_dt[:, t:t + 1])
                        nc.scalar.activation(delta[:, t, :], fbank[t][:, :], ACT.Relu,
                                             bias=b_dt[:, t:t + 1]).then_inc(S["soft_done"], 1)
                    act.wait_ge(S["soft_done"], DT * b + 2 * DT)
                    nc.scalar.activation(conv[:, :, :], conv[:, :, :], ACT.Exp, scale=-1.0).then_inc(S["soft"], 1)
                    act.wait_ge(S["soft"], 2 * b + 1)
                    nc.scalar.activation(conv[:, :, :], conv[:, :, :], ACT.Ln, bias=1.0).then_inc(S["soft"], 1)
                    act.wait_ge(S["delta_ready"], b + 1)
                    for n in range(NS):
                        act.wait_ge(S["scan_done"], NS * b + n + 1)
                        for t in range(DT):
                            ins = nc.scalar.activation(decay[n % 2][:, t, 1:], delta[:, t, 1:], ACT.Exp,
                                                       scale=a_neg[:, t, n:n + 1])
                        ins.then_inc(S["decay_ready"], 1)

            @block.vector
            def _(dve):
                dve.wait_ge(S["a_exp"], 1)
                nc.vector.tensor_scalar(a_neg[:, :, :], a_neg[:, :, :], -1.0, None, ALU.mult).then_inc(S["a_ready"], 1)
                for t in range(DT):
                    nc.vector.tensor_scalar(dp_diag[:, t, :], ident[:, :], dp[:, t:t + 1], None,
                                            ALU.mult).then_inc(S["dp_diag"], 1)
                dve.wait_ge(S["pads_zero"], 3)
                dve.sem_inc(S["scan_done"], 2)
                dve.sem_inc(S["hc_ready"], 2)
                dve.sem_inc(S["yz_done"], DT)
                dve.sem_inc(S["out_added"], 2)
                with dve.Fori(0, B) as b:
                    dve.wait_ge(S["x_loaded"], 16 * b + 16)
                    norm_vector(nc, dve, b, x, xln, nb, ns)
                    for k in range(KC - 1):
                        for t in range(DT):
                            if k == 0:
                                dve.wait_ge(S["xz_read"], 2 * DT * b + t + 1)
                            else:
                                dve.wait_ge(S["conv_step"], DT * (KC - 1) * b + DT * (k - 1) + t + 1)
                            nc.vector.scalar_tensor_tensor(conv[:, t, :], xpad[:, t, k:k + L], conv_w[:, t, k:k + 1],
                                                           conv[:, t, :], ALU.mult, ALU.add).then_inc(S["conv_step"], 1)
                    for n in range(NS):
                        dve.wait_ge(S["decay_ready"], NS * b + n + 1)
                        dve.wait_ge(S["bx_ready"], NS * b + n + 3)
                        dve.wait_ge(S["hc_ready"], NS * b + n + 2)
                        nc.vector.tensor_tensor_scan(hs[:, :, :].rearrange("p t l -> p (t l)"),
                                                     decay[n % 2][:, :, :].rearrange("p t l -> p (t l)"),
                                                     bx[n % 2][:, :, :].rearrange("p t l -> p (t l)"), 0.0,
                                                     ALU.mult, ALU.add).then_inc(S["scan_done"], 1)
                        dve.wait_ge(S["scan_done"], NS * b + n + 3)
                        dve.wait_ge(S["sum_done"], NS * b + n + 1)
                        dve.wait_ge(S[f"bc_loaded{n % 2}"], 16 * (NS // 2) * b + 16 * (n // 2 + 1))
                        nc.vector.tensor_tensor(hc[n % 2][:, :, :], hs[:, :, :],
                                                free_bcast(bc[n % 2][:, 1, :], 1, DT), ALU.mult).then_inc(S["hc_ready"], 1)
                    for t in range(DT):
                        dve.wait_ge(S["y_psum"], b + 1)
                        nc.vector.tensor_tensor(conv[:, t, :], ybank[t][:, :], zs[:, t, :], ALU.mult).then_inc(S["yz_done"], 1)
                    for i in range(2):
                        dve.wait_ge(S["out_psum"], 2 * b + i + 1)
                        pair = x[:, 2 * i:2 * i + 2, :].rearrange("p s d -> p (s d)")
                        nc.vector.tensor_tensor(pair, pair, fbank[i][:, :], ALU.add).then_inc(S["out_added"], 1)

            @block.tensor
            def _(pe):
                pe.wait_ge(S["params_loaded"], 16 * N_PARAMS)
                pe.wait_ge(S["dp_diag"], DT)
                pe.sem_inc(S["sum_done"], 2)
                with pe.Fori(0, B) as b:
                    pe.wait_ge(ns.xln, ST * b + ST)
                    pe.wait_ge(S["out_added"], 2 * b + 2)
                    transpose_tiles(nc, xln, ident, fbank, S["xt_psum"])
                    pe.wait_ge(S["xt_ready"], KD * b + KD)
                    pe.wait_ge(S["soft_done"], DT * b + DT)
                    for t in range(2 * DT):
                        if t >= DT:
                            pe.wait_ge(S["xz_read"], 2 * DT * b + t - DT + 1)
                        for k in range(KD):
                            ins = nc.tensor.matmul(fbank[t % DT][:, :], w_in[:, k, t * P:(t + 1) * P], xt[:, k, :],
                                                   start=(k == 0), stop=(k == KD - 1))
                        ins.then_inc(S["xz_psum"], 1)
                    pe.wait_ge(S["xc_ready"], b + 1)
                    pe.wait_ge(S["xz_read"], 2 * DT * b + 2 * DT)
                    for k in range(DT):
                        ins = nc.tensor.matmul(fbank[0][0:RK + 2 * NS, :], w_x[:, k, :], xc[:, k, :],
                                               start=(k == 0), stop=(k == DT - 1))
                    ins.then_inc(S["dbc_psum"], 1)
                    pe.wait_ge(S["dbc_ready"], b + 1)
                    for t in range(DT):
                        nc.tensor.matmul(fbank[t][:, :], w_dt[:, t * P:(t + 1) * P], dbc[0:RK, :],
                                         start=True, stop=True).then_inc(S["delta_psum"], 1)
                    pe.wait_ge(S["yz_done"], DT * b + DT)
                    for n in range(NS):
                        pe.wait_ge(S["hc_ready"], NS * b + n + 3)
                        for t in range(DT):
                            ins = nc.tensor.matmul(ybank[t][:, :], ident[:, :], hc[n % 2][:, t, :],
                                                   start=(n == 0), stop=False)
                        ins.then_inc(S["sum_done"], 1)
                    for t in range(DT):
                        ins = nc.tensor.matmul(ybank[t][:, :], dp_diag[:, t, :], xc[:, t, :], start=False, stop=True)
                    ins.then_inc(S["y_psum"], 1)
                    pe.wait_ge(S["yz_done"], DT * b + 2 * DT)
                    pe.wait_ge(S["soft_done"], DT * b + 2 * DT)
                    for i in range(2):
                        for st in range(2 * i, 2 * i + 2):
                            for k in range(DT):
                                ins = nc.tensor.matmul(fbank[i][:, (st % 2) * D:(st % 2 + 1) * D],
                                                       conv[:, k, st * P:(st + 1) * P], w_out[:, k, :],
                                                       start=(k == 0), stop=(k == DT - 1))
                        ins.then_inc(S["out_psum"], 1)
        m.end_phase()


def moe_phase(nc, banks, consts, weights, x_in, x_out, prm, o_scratch, second):
    tag = "moe2" if second else "moe1"
    ident, eps = consts["ident"], consts["eps"]
    with ExitStack() as ctx:
        m = Mem(nc, ctx)
        weights.second_set(m, tag)
        gate = m.sb(f"{tag}_gate", P, KD, E)
        gate_b = m.sb(f"{tag}_gate_b", P, 1)
        b2 = m.sb(f"{tag}_b2", P, D)
        x = m.sb(f"{tag}_x", P, B, ST, D)
        xt = [m.sb(f"{tag}_xt{i}", P, KD, L) for i in range(2)]
        stats = m.sb(f"{tag}_bn_stats", P, QB * ST, 6)
        mv = m.sb(f"{tag}_mean_var", P, QB * ST, 2)
        std = m.sb(f"{tag}_std", P, QB * ST)
        rstd = m.sb(f"{tag}_rstd", P, QB * ST)
        probs = m.sb(f"{tag}_probs", P, L)
        nmax = m.sb(f"{tag}_nmax", P, 1)
        total = m.sb(f"{tag}_total", P, 1)
        inv = m.sb(f"{tag}_inv", P, 1)
        top = m.sb(f"{tag}_top", P, TOP)
        rest = m.sb(f"{tag}_rest", P, L)
        route = m.sb(f"{tag}_route", P, HALVES, L)
        route_t = m.sb(f"{tag}_route_t", P, ST, P)
        mrg = m.sb(f"{tag}_merged_e", P, D)
        merged = m.sb(f"{tag}_merged", P, KD, E, B)
        mg = [m.sb(f"{tag}_merged_g{s}", P, KD, EG, EQ) for s in range(2)]
        b1 = [m.sb(f"{tag}_b1_{s}", P, HID) for s in range(2)]
        hid = xt[0][:, :, :].rearrange("p k l -> p (k l)")
        hid_t = xt[1][:, :, :].rearrange("p k l -> p (k l)").rearrange("p (k c) -> p k c", c=P)
        o_sb = [m.sb(f"{tag}_o{s}", P, D) for s in range(2)]
        o_all = m.sb(f"{tag}_o_all", P, HALVES, D)

        S = {k: m.sem(f"{tag}_{k}") for k in (
            "params_loaded", "zeroed", "x_loaded0", "x_loaded1", "stats", "mv", "std", "rstd", "xln", "xt_psum",
            "xt_ready", "logit_psum", "soft", "exp_done", "route_ready", "route_t_psum", "route_t_ready",
            "mrg_psum", "mrg_ready", "merged_psum", "merged_ready", "mg_ready", "b1_loaded0", "b1_loaded1", "h_psum", "pre_ready",
            "gelu_ready", "ht_psum", "ht_ready", "o_psum", "o_ready", "o_stored0", "o_stored1", "o_loaded", "o_all_ready",
            "x_again0", "x_again1", "y_psum", "y_added", "x_stored")}
        N_PARAMS = 1 + 2 * QB
        SOFT = 6
        loaded = [16 * (GP if second else 1), 16 * (GP + 1 if second else 1)]
        passed = m.sem(f"{tag}_passed")
        group_of = lambda i, s: 2 * ((GP - 1) - i) + s if second else 2 * i + s

        with nc.Block() as block:
            @block.sync
            def _(sp):
                for half in range(HALVES):
                    for q in range(QB):
                        sp.dma_start(x[:, half * QB + q, :, :], token_major(x_in, half * QB + q)).then_inc(
                            S[f"x_loaded{half}"], 16)
                    if half == 0:
                        sp.dma_start(gate[:, :, :], prm["gate_wT"].rearrange("(k p) e -> p k e", p=P)).then_inc(
                            S["params_loaded"], 16)
                        for q in range(QB):
                            rows = slice(q * E, (q + 1) * E)
                            sp.dma_start(gate_b[rows, :], prm["gate_b"].unsqueeze(1)).then_inc(S["params_loaded"], 16)
                            sp.dma_start(b2[rows, :], weights.w2_dram[:, HID, :]).then_inc(S["params_loaded"], 16)
                weights.load(nc, 1, 1, group_of(0, 1))
                weights.load(nc, 1, 2, group_of(0, 1))
                with sp.Fori(1, GP) as i:
                    for s in range(2):
                        for which, used in ((1, "pre_ready"), (2, "o_ready")):
                            carried_wait(sp, passed, (S[used], 2 * i + s - 1))
                            weights.load(nc, s, which, group_of(i, s))
                sp.wait_ge(S["mrg_psum"], HALVES)
                for b in range(B):
                    sp.dma_start(x[:, b, :, :], token_major(x_in, b)).then_inc(S[f"x_again{b // QB}"], 16)
                for b in range(B):
                    sp.wait_ge(S["y_added"], 2 * (b + 1))
                    sp.dma_start(token_major(x_out, b), x[:, b, :, :]).then_inc(S["x_stored"], 16)
                sp.wait_ge(S["x_stored"], 16 * B)

            @block.gpsimd
            def _(pool):
                for s in range(2):
                    nc.gpsimd.memset(mg[s][:, :, :, :], 0.0).then_inc(S["zeroed"], 1)
                    nc.gpsimd.memset(b1[s][:, :], 0.0).then_inc(S["zeroed"], 1)
                pool.wait_ge(S["zeroed"], 4)

                def load_b1(i, s):
                    for j in range(EG):
                        row = weights.w1_dram[ds(group_of(i, s) * EG + j, 1), D, :]
                        pool.dma_start(b1[s][j * EQ:j * EQ + B, :], row.partition_broadcast(B)).then_inc(S[f"b1_loaded{s}"], 16)

                for s in range(2):
                    load_b1(0, s)
                with pool.Fori(1, GP) as i:
                    for s in range(2):
                        carried_wait(pool, passed, (S["pre_ready"], 2 * i + s - 1))
                        load_b1(i, s)
                for s in range(2):
                    pool.wait_ge(S[f"o_stored{s}"], 16 * EG * (GP + 1))
                for q in range(QB):
                    for half in range(HALVES):
                        pool.dma_start(o_all[q * E:(q + 1) * E, half, :],
                                       o_scratch[:, half * QB + q, :]).then_inc(S["o_loaded"], 16)

            @block.scalar
            def _(act):
                act.wait_ge(S["params_loaded"], 16 * N_PARAMS)
                for half in range(HALVES):
                    act.wait_ge(S["mv"], QB * ST * (half + 1))
                    nc.scalar.activation(std[:, :], mv[:, :, 1], ACT.Sqrt, bias=eps[:, :]).then_inc(S["std"], 1)
                    for q in range(QB):
                        for kt in range(KD):
                            n = (half * QB + q) * KD + kt
                            act.wait_ge(S["xt_psum"], n + 1)
                            if q >= 2 or half:
                                act.wait_ge(S["logit_psum"], half * QB + q - 1)
                            nc.scalar.copy(xt[q % 2][:, kt, :], banks[2 * (q % 2) + kt][:, :]).then_inc(S["xt_ready"], 1)
                    act.wait_ge(S["soft"], SOFT * half + 2)
                    nc.scalar.activation(probs[:, :], probs[:, :], ACT.Exp, bias=nmax[:, :],
                                         accum_out=total[:, :]).then_inc(S["exp_done"], 1)
                act.wait_ge(S["logit_psum"], B)
                act.sem_inc(S["gelu_ready"], 1)
                for s in range(2):
                    act.sem_inc(S[f"o_stored{s}"], 16 * EG)
                with act.Fori(0, GP) as i:
                    for s in range(2):
                        n = 2 * i + s
                        act.wait_ge(S["pre_ready"], n + 1)
                        nc.scalar.activation(hid, hid, ACT.Gelu).then_inc(S["gelu_ready"], 1)
                        act.wait_ge(S["ht_psum"], 2 * n + 4)
                        act.wait_ge(S["o_psum"], n + 1)
                        nc.scalar.copy(hid_t[:, MH // 2:, :].rearrange("p k c -> p (k c)"), banks[5][:, :]).then_inc(
                            S["ht_ready"], 1)
                        carried_wait(act, passed, (S["o_ready"], n + 1))
                        for j in range(EG):
                            row = o_scratch[ds(group_of(i, s) * EG + j, 1), :, :].rearrange("o b d -> (o b) d")
                            act.dma_start(row, o_sb[s][j * EQ:j * EQ + B, :]).then_inc(S[f"o_stored{s}"], 16)

            @block.vector
            def _(dve):
                dve.wait_ge(S["params_loaded"], 16 * N_PARAMS)
                for half in range(HALVES):
                    dve.wait_ge(S["x_loaded%d" % half], 16 * QB)
                    for t in range(QB * ST):
                        nc.vector.bn_stats(stats[:, t, :], x[:, half * QB + t // ST, t % ST, :]).then_inc(S["stats"], 1)
                    dve.wait_ge(S["stats"], QB * ST * (half + 1))
                    for t in range(QB * ST):
                        nc.vector.bn_aggr(mv[:, t, :], stats[:, t, :]).then_inc(S["mv"], 1)
                    dve.wait_ge(S["std"], half + 1)
                    nc.vector.reciprocal(rstd[:, :], std[:, :]).then_inc(S["rstd"], 1)
                    dve.wait_ge(S["rstd"], half + 1)
                    for t in range(QB * ST):
                        tile = x[:, half * QB + t // ST, t % ST, :]
                        nc.vector.tensor_scalar(tile, tile, mv[:, t, 0:1], rstd[:, t:t + 1],
                                                ALU.subtract, ALU.mult).then_inc(S["xln"], 1)
                    ch = Chain(dve, S["soft"], SOFT * half)
                    dve.wait_ge(S["logit_psum"], QB * (half + 1))
                    ch.step(nc.vector.tensor_scalar(probs[:, :], banks[4][:, :], gate_b[:, :], None, ALU.add))
                    ch.wait()
                    ch.step(nc.vector.tensor_reduce(nmax[:, :], probs[:, :], AX_X, ALU.max, negate=True))
                    dve.wait_ge(S["exp_done"], half + 1)
                    ch.step(nc.vector.reciprocal(inv[:, :], total[:, :]))
                    ch.wait()
                    ch.step(nc.vector.tensor_scalar(probs[:, :], probs[:, :], inv[:, :], None, ALU.mult))
                    ch.wait()
                    ch.step(nc.vector.max(top[:, :], probs[:, :]))
                    ch.wait()
                    ch.step(nc.vector.match_replace(rest[:, :], top[:, :], probs[:, :], 0.0))
                    ch.wait()
                    nc.vector.tensor_tensor(route[:, half, :], probs[:, :], rest[:, :], ALU.subtract).then_inc(
                        S["route_ready"], 1)
                    dve.wait_ge(S["route_t_psum"], half + 1)
                    nc.vector.tensor_copy(route_t[:, :, :].rearrange("p s c -> p (s c)"), banks[5][:, :]).then_inc(
                        S["route_t_ready"], 1)
                    dve.wait_ge(S["mrg_psum"], half + 1)
                    nc.vector.tensor_copy(mrg[:, :], banks[6][:, 0:D]).then_inc(S["mrg_ready"], 1)
                    dve.wait_ge(S["merged_psum"], half + 1)
                    for t in range(KD):
                        nc.vector.tensor_copy(
                            merged[:, t, :, half * QB:(half + 1) * QB],
                            banks[7][:, t * P:(t + 1) * P].rearrange("p (q e) -> p e q", q=QB)).then_inc(S["merged_ready"], 1)
                dve.wait_ge(S["merged_ready"], KD * HALVES)
                dve.wait_ge(S["logit_psum"], B)
                dve.wait_ge(S["zeroed"], 4)
                dve.sem_inc(S["h_psum"], 1)
                with dve.Fori(0, GP) as i:
                    for s in range(2):
                        n = 2 * i + s
                        carried_wait(dve, passed, (S["h_psum"], n + 1))
                        for t in range(KD):
                            ins = nc.vector.tensor_copy(mg[s][:, t, :, 0:B], merged[:, t, ds(group_of(i, s) * EG, EG), :])
                        ins.then_inc(S["mg_ready"], 1)
                        dve.wait_ge(S["h_psum"], n + 2)
                        dve.wait_ge(S[f"b1_loaded{s}"], 16 * EG * i + 16 * EG)
                        dve.wait_ge(S["gelu_ready"], n + 1)
                        dve.wait_ge(S["ht_psum"], 2 * n + 2)
                        for c in range(2):
                            ins = nc.vector.tensor_tensor(hid[:, c * BANK:(c + 1) * BANK], banks[2 * s + c][:, :],
                                                          b1[s][:, c * BANK:(c + 1) * BANK], ALU.add)
                        ins.then_inc(S["pre_ready"], 1)
                        dve.wait_ge(S["ht_psum"], 2 * n + 3)
                        dve.wait_ge(S["o_psum"], n + 1)
                        nc.vector.tensor_copy(hid_t[:, 0:MH // 2, :].rearrange("p k c -> p (k c)"), banks[4][:, :]).then_inc(
                            S["ht_ready"], 1)
                        dve.wait_ge(S["o_psum"], n + 2)
                        dve.wait_ge(S[f"o_stored{s}"], 16 * EG * i + 16 * EG)
                        nc.vector.tensor_copy(o_sb[s][:, :], banks[6 + s][:, 0:D]).then_inc(S["o_ready"], 1)
                dve.wait_ge(S["o_loaded"], 16 * HALVES * QB)
                nc.vector.tensor_tensor(o_all[:, :, :], o_all[:, :, :], free_bcast(b2[:, :], 1, HALVES), ALU.add).then_inc(
                    S["o_all_ready"], 1)
                for b in range(B):
                    dve.wait_ge(S[f"x_again{b // QB}"], 16 * QB)
                    for c in range(2):
                        dve.wait_ge(S["y_psum"], b // QB * 2 + c + 1)
                        pair = x[:, b, 2 * c:2 * c + 2, :].rearrange("p s d -> p (s d)")
                        nc.vector.tensor_tensor(pair, pair, banks[2 * (b % QB) + c][:, :], ALU.add).then_inc(S["y_added"], 1)

            @block.tensor
            def _(pe):
                pe.wait_ge(S["params_loaded"], 16 * N_PARAMS)
                for half in range(HALVES):
                    for q in range(QB):
                        n = half * QB + q
                        pe.wait_ge(S["xln"], ST * (n + 1))
                        pair = banks[2 * (q % 2):2 * (q % 2) + 2]
                        if n >= 2:
                            pe.wait_ge(S["xt_ready"], KD * (n - 1))
                        transpose_tiles(nc, x[:, n, :, :], ident, pair, S["xt_psum"])
                        pe.wait_ge(S["xt_ready"], KD * (n + 1))
                        if half and q == 0:
                            pe.wait_ge(S["soft"], 1)
                        for k in range(KD):
                            ins = nc.tensor.matmul(banks[4][q * E:(q + 1) * E, :], gate[:, k, :], xt[q % 2][:, k, :],
                                                   start=(k == 0), stop=(k == KD - 1))
                        ins.then_inc(S["logit_psum"], 1)
                    pe.wait_ge(S["route_ready"], half + 1)
                    for st in range(ST):
                        ins = nc.tensor.transpose(banks[5][:, st * P:(st + 1) * P], route[:, half, st * P:(st + 1) * P], ident[:, :])
                    ins.then_inc(S["route_t_psum"], 1)
                    pe.wait_ge(S["route_t_ready"], half + 1)
                    for st in range(ST):
                        for q in range(QB):
                            ins = nc.tensor.matmul(banks[6][q * E:(q + 1) * E, 0:D], route_t[:, st, q * E:(q + 1) * E],
                                                   x[:, half * QB + q, st, :], start=(st == 0), stop=(st == ST - 1))
                    ins.then_inc(S["mrg_psum"], 1)
                    pe.wait_ge(S["mrg_ready"], half + 1)
                    for t in range(KD):
                        ins = nc.tensor.transpose(banks[7][:, t * P:(t + 1) * P], mrg[:, t:D:KD], ident[:, :])
                    ins.then_inc(S["merged_psum"], 1)
                pe.wait_ge(S["merged_ready"], KD * HALVES)
                pe.sem_inc(S["ht_psum"], 2)
                pe.sem_inc(S["o_psum"], 1)
                with pe.Fori(0, GP) as i:
                    for s in range(2):
                        n = 2 * i + s
                        pe.wait_ge(S["mg_ready"], n + 1)
                        pe.wait_ge(weights.loaded[s][0], 16 * i + loaded[s])
                        for c in range(2):
                            for t in range(KD):
                                for j in range(EG):
                                    ins = nc.tensor.matmul(banks[2 * s + c][j * EQ:(j + 1) * EQ, :], mg[s][:, t, j, :],
                                                           weights.w1[s][:, j, t, c * BANK:(c + 1) * BANK],
                                                           start=(t == 0), stop=(t == KD - 1))
                        ins.then_inc(S["h_psum"], 1)
                        pe.wait_ge(S["gelu_ready"], n + 2)
                        for k in range(MH):
                            ins = nc.tensor.transpose(banks[4 + k // (MH // 2)][:, k % (MH // 2) * P:(k % (MH // 2) + 1) * P],
                                                      hid[:, k:HID:MH], ident[:, :])
                            if k % (MH // 2) == MH // 2 - 1:
                                ins.then_inc(S["ht_psum"], 1)
                        carried_wait(pe, passed, (weights.loaded[s][1], 16 * i + loaded[s]),
                                     (S["ht_ready"], 2 * n + 2))
                        for k in range(MH):
                            for j in range(EG):
                                ins = nc.tensor.matmul(banks[6 + s][j * EQ:(j + 1) * EQ, 0:D],
                                                       hid_t[:, k, j * EQ:(j + 1) * EQ], weights.w2[s][:, j, k, :],
                                                       start=(k == 0), stop=(k == MH - 1))
                        ins.then_inc(S["o_psum"], 1)
                pe.wait_ge(S["o_all_ready"], 1)
                for half in range(HALVES):
                    for c in range(2):
                        if half:
                            pe.wait_ge(S["y_added"], 2 * QB)
                        for st in range(2 * c, 2 * c + 2):
                            for q in range(QB):
                                rows = slice(q * E, (q + 1) * E)
                                ins = nc.tensor.matmul(banks[2 * q + c][:, (st % 2) * D:(st % 2 + 1) * D],
                                                       route[rows, half, st * P:(st + 1) * P], o_all[rows, half, :],
                                                       start=True, stop=True)
                        ins.then_inc(S["y_psum"], 1)
        m.end_phase()


def delta_phase(nc, banks, consts, x_in, x_out, prm, n_scratch, t_scratch):
    ident, eps = consts["ident"], consts["eps"]
    NT = 3 * KD
    with ExitStack() as ctx:
        m = Mem(nc, ctx)
        w_qkv = m.sb("w_qkv", P, KD, 3 * D)
        w_gates = m.sb("w_gates", P, KD, 2 * H)
        w_o = m.sb("w_o", P, KD, D)
        conv_w = m.sb("conv_w_qkv", P, NT, KC)
        mix_bias = m.sb("mix_bias", P, 2, H)
        o_norm = m.sb("o_norm", P, DK)
        eps_l2 = m.sb("eps_l2", P, 1)
        neg_strict = m.sb("neg_strict", P, C)
        upper = m.sb("upper", P, C)
        head_mask = m.sb("head_mask", P, P)
        x = m.sb("x_delta", P, ST, D)
        xln = m.sb("xln_delta", P, ST, D)
        xt = m.sb("xt_delta", P, KD, L)
        nb = NormBufs(m, "delta")
        xpad = m.sb("xpad_qkv", P, NT, KC - 1 + L)
        conv = m.sb("conv_qkv", P, NT, L)
        feat = m.sb("feat", P, NT, L)
        gates = m.sb("gates", P, ST, 2 * H)
        tok = m.sb("tok", P, ST, NT * P)
        ssq = m.sb("ssq", P, ST * 2 * H)
        rnorm = m.sb("rnorm", P, ST * 2 * H)
        kb = m.sb("beta_k", P, ST, D)
        vb = m.sb("beta_v", P, ST, D)
        n_tok = m.sb("n_tok", P, ST, H, C)
        attn_t = m.sb("attn_t", P, ST, H, C)
        n_lane = m.sb("n_lane", P, C, C)
        t_lane = m.sb("t_lane", P, C, C)
        prod = m.sb("prod", P, C * C)
        t_tok = m.sb("t_tok", P, ST, H, C)
        y = m.sb("y_chunk", P, KD, P)
        u = m.sb("u_chunk", P, KD, P)
        state = [m.sb(f"s_delta{i}", P, P) for i in range(KD)]
        o = m.sb("o_delta", P, ST, D)
        oms = m.sb("o_ms", P, ST * H)
        ostd = m.sb("o_std", P, ST * H)
        orstd = m.sb("o_rstd", P, ST * H)
        squares = conv[:, 0:4, :].rearrange("p t l -> p (t l)")

        ns = NormSems(m, "delta")
        S = {k: m.sem("de_" + k) for k in (
            "params_loaded", "masks", "mix_ready", "lane_init", "x_loaded", "xt_psum", "xt_ready", "qkv_psum",
            "qkv_read", "conv_step", "feat_ready", "gate_psum", "gate_pre", "gate_ready", "tok_psum", "tok_ready",
            "sq_ready", "ssq_ready", "l2_std", "l2_ready", "pool_step", "featn_psum", "featn_ready", "gram_psum",
            "gram_read", "n_stored", "n_loaded", "solve", "t_stored", "t_loaded", "x_chunk", "y_ready", "u_psum",
            "u_ready", "s_psum", "s_ready", "o_psum", "o_read", "o_sq", "o_ms", "o_std", "o_rstd", "ot_psum",
            "ot_ready", "out_psum", "out_added", "x_stored")}
        N_PARAMS = 12
        KPB = (KC - 1) * NT
        SOLVE = 2 * (C - 1)
        CH = KD * (NC - 1)
        POOL = 7

        passed = m.sem(f"sync_passed_{m.nc.next_id()}")
        with nc.Block() as block:
            @block.sync
            def _(sp):
                for dst, src in [(w_qkv[:, :, i * D:(i + 1) * D], prm[f"{n}_w"].rearrange("(k p) n -> p k n", p=P))
                                 for i, n in enumerate("qkv")] + \
                        [(conv_w[:, KD * i:KD * i + KD, :], prm[f"conv_{n}_w"].rearrange("(k p) n -> p k n", p=P))
                         for i, n in enumerate("qkv")] + \
                        [(w_gates[:, :, i * H:(i + 1) * H], prm[n].rearrange("(k p) n -> p k n", p=P))
                         for i, n in enumerate(("b_w", "mix_w"))] + \
                        [(mix_bias[:, i, :], prm[n].partition_broadcast(P)) for i, n in enumerate(("mix_b", "mix_bias"))] + \
                        [(o_norm[:, :], prm["o_norm_w"].partition_broadcast(P)),
                         (w_o[:, :, :], prm["o_w"].rearrange("(k p) n -> p k n", p=P))]:
                    sp.dma_start(dst, src).then_inc(S["params_loaded"], 16)
                sp.sem_inc(S["x_stored"], 16)
                with sp.Fori(0, B) as b:
                    carried_wait(sp, passed, (S["x_stored"], 16 * b + 16))
                    sp.dma_start(x[:, :, :], token_major(x_in, b)).then_inc(S["x_loaded"], 16)
                    carried_wait(sp, passed, (S["gram_read"], ST * 2 * CT * (b + 1)))
                    for st in range(ST):
                        sp.dma_start(n_scratch[ds(b, 1), :, st * P:(st + 1) * P, :].rearrange("o h p j -> p (o h) j"),
                                     n_tok[:, st, :, :]).then_inc(S["n_stored"], 16)
                    carried_wait(sp, passed, (S["n_stored"], 16 * ST * b + 16 * ST))
                    sp.dma_start(n_lane[:, :, :], n_scratch[ds(b, 1), :, :, :].rearrange(
                        "o h (c i) j -> (o h c) i j", i=C)).then_inc(S["n_loaded"], 16)
                    carried_wait(sp, passed, (S["solve"], SOLVE * b + SOLVE))
                    sp.dma_start(t_scratch[ds(b, 1), :, :, :].rearrange("o h (c i) j -> (o h c) i j", i=C),
                                 t_lane[:, :, :]).then_inc(S["t_stored"], 16)
                    carried_wait(sp, passed, (S["t_stored"], 16 * b + 16))
                    for st in range(ST):
                        sp.dma_start(t_tok[:, st, :, :], t_scratch[ds(b, 1), :, st * P:(st + 1) * P, :].rearrange(
                            "o h p j -> p (o h) j")).then_inc(S["t_loaded"], 16)
                    carried_wait(sp, passed, (S["out_added"], 2 * b + 2))
                    sp.dma_start(token_major(x_out, b), x[:, :, :]).then_inc(S["x_stored"], 16)
                sp.wait_ge(S["x_stored"], 16 * (B + 1))

            @block.gpsimd
            def _(pool):
                nc.gpsimd.memset(neg_strict[:, :], -1.0).then_inc(S["masks"], 1)
                nc.gpsimd.memset(upper[:, :], 1.0).then_inc(S["masks"], 1)
                nc.gpsimd.memset(head_mask[:, :], 0.0).then_inc(S["masks"], 1)
                nc.gpsimd.memset(eps_l2[:, :], 1e-12).then_inc(S["masks"], 1)
                nc.gpsimd.memset(t_lane[:, :, :], 0.0).then_inc(S["lane_init"], 1)
                pool.wait_ge(S["masks"], 4)
                pool.wait_ge(S["lane_init"], 1)
                for c in range(CT):
                    rows = slice(c * C, (c + 1) * C)
                    nc.gpsimd.affine_select(out=neg_strict[rows, :], in_=neg_strict[rows, :], compare_op=ALU.is_gt,
                                            fill=0.0, base=0, pattern=[[-1, C]], channel_multiplier=1).then_inc(S["masks"], 1)
                    pool.wait_ge(S["masks"], 4 + 3 * c + 1)
                    nc.gpsimd.affine_select(out=upper[rows, :], in_=upper[rows, :], compare_op=ALU.is_ge,
                                            fill=0.0, base=0, pattern=[[1, C]], channel_multiplier=-1).then_inc(S["masks"], 1)
                    pool.wait_ge(S["masks"], 4 + 3 * c + 2)
                    nc.gpsimd.memset(head_mask[rows, rows], 1.0).then_inc(S["masks"], 1)
                    pool.wait_ge(S["masks"], 4 + 3 * c + 3)
                nc.gpsimd.memset(t_lane[:, :, :].rearrange("p i j -> p (i j)")[:, 0:C * C:C + 1], 1.0).then_inc(S["lane_init"], 1)
                with pool.Fori(0, B) as b:
                    ch = Chain(pool, S["pool_step"], POOL * b)
                    qk = tok[:, :, 0:2 * D].rearrange("p s (h d) -> p s h d", d=DK)
                    v = tok[:, :, 2 * D:3 * D].rearrange("p s (h d) -> p s h d", d=DK)
                    beta = free_bcast(gates[:, :, 0:H], 3, DK)
                    g = free_bcast(gates[:, :, H:2 * H], 3, DK)
                    heads = lambda t: t[:, :, :].rearrange("p s (h d) -> p s h d", d=DK)
                    pool.wait_ge(S["gate_ready"], b + 1)
                    pool.wait_ge(S["tok_ready"], NT * (b + 1))
                    ch.step(nc.gpsimd.tensor_tensor(heads(vb), v, beta, ALU.mult))
                    pool.wait_ge(S["l2_ready"], b + 1)
                    pool.wait_ge(S["sq_ready"], b + 1)
                    ch.step(nc.gpsimd.tensor_tensor(qk, qk, free_bcast(rnorm[:, :], 2, DK).rearrange(
                        "p (s h) d -> p s h d", s=ST), ALU.mult))
                    ch.wait()
                    ch.step(nc.gpsimd.tensor_tensor(heads(kb), qk[:, :, H:2 * H, :], beta, ALU.mult))
                    pool.wait_ge(S["o_read"], ST * KD * (b + 2))
                    ch.step(nc.gpsimd.tensor_tensor(heads(o), heads(o), g, ALU.mult))
                    ch.wait()
                    ch.step(nc.gpsimd.tensor_tensor(heads(o), heads(o), v, ALU.add))
                    pool.wait_ge(S["o_rstd"], b + 1)
                    ch.step(nc.gpsimd.tensor_tensor(heads(o), heads(o), free_bcast(orstd[:, :], 2, DK).rearrange(
                        "p (s h) d -> p s h d", s=ST), ALU.mult))
                    ch.wait()
                    flat = o[:, :, :].rearrange("p s (h d) -> p (s h) d", d=DK)
                    ch.step(nc.gpsimd.tensor_tensor(flat, flat, free_bcast(o_norm[:, :], 1, ST * H), ALU.mult))
                    assert ch.n == POOL

            @block.scalar
            def _(act):
                act.wait_ge(S["params_loaded"], 16 * N_PARAMS)
                act.wait_ge(S["masks"], 4 + 3 * CT)
                act.wait_ge(S["conv_step"], 1)
                with act.Fori(0, B) as b:
                    norm_scalar(nc, act, b, nb, ns, eps)
                    for kt in range(KD):
                        act.wait_ge(S["xt_psum"], KD * b + kt + 1)
                        nc.scalar.copy(xt[:, kt, :], banks[kt][:, :]).then_inc(S["xt_ready"], 1)
                    for t in range(NT):
                        act.wait_ge(S["qkv_psum"], NT * b + t + 1)
                        nc.scalar.activation(conv[:, t, :], banks[2 + t][:, :], ACT.Copy, scale=conv_w[:, t, KC - 1:KC])
                        nc.scalar.copy(xpad[:, t, KC - 1:], banks[2 + t][:, :]).then_inc(S["qkv_read"], 1)
                    act.wait_ge(S["gate_pre"], b + 1)
                    nc.scalar.activation(gates[:, :, :], gates[:, :, :], ACT.Sigmoid).then_inc(S["gate_ready"], 1)
                    for t in range(NT):
                        act.wait_ge(S["conv_step"], 1 + KPB * b + NT * (KC - 2) + t + 1)
                        nc.scalar.activation(feat[:, t, :], conv[:, t, :], ACT.Silu).then_inc(S["feat_ready"], 1)
                    for t in range(NT):
                        act.wait_ge(S["tok_psum"], NT * b + t + 1)
                        nc.scalar.copy(tok[:, :, t * P:(t + 1) * P],
                                       banks[2 + t][:, :].rearrange("p (s c) -> p s c", c=P)).then_inc(S["tok_ready"], 1)
                    act.wait_ge(S["tok_ready"], NT * (b + 1))
                    nc.scalar.activation(squares.rearrange("p (s c) -> p s c", s=ST), tok[:, :, 0:2 * D],
                                         ACT.Square).then_inc(S["sq_ready"], 1)
                    act.wait_ge(S["ssq_ready"], b + 1)
                    nc.scalar.activation(ssq[:, :], ssq[:, :], ACT.Sqrt, bias=eps_l2[:, :]).then_inc(S["l2_std"], 1)
                    for t in range(NT):
                        act.wait_ge(S["featn_psum"], NT * b + t + 1)
                        nc.scalar.copy(feat[:, t, :], banks[2 + t][:, :]).then_inc(S["featn_ready"], 1)
                    for n in range(NC):
                        for hh in range(KD):
                            rows = slice((n % CT) * C, (n % CT + 1) * C)
                            act.wait_ge(S["u_psum"], KD * NC * b + KD * n + hh + 1)
                            nc.scalar.copy(u[rows, hh, :], banks[hh][rows, 0:P]).then_inc(S["u_ready"], 1)
                    act.wait_ge(S["pool_step"], POOL * b + 5)
                    nc.scalar.activation(squares[:, 0:ST * D].rearrange("p (s c) -> p s c", s=ST), o[:, :, :],
                                         ACT.Square).then_inc(S["o_sq"], 1)
                    act.wait_ge(S["o_ms"], b + 1)
                    nc.scalar.activation(ostd[:, :], oms[:, :], ACT.Sqrt, bias=eps[:, :], scale=1.0 / DK).then_inc(S["o_std"], 1)
                    for kt in range(KD):
                        act.wait_ge(S["ot_psum"], KD * b + kt + 1)
                        nc.scalar.copy(xt[:, kt, :], banks[kt][:, :]).then_inc(S["ot_ready"], 1)

            @block.vector
            def _(dve):
                nc.vector.memset(xpad[:, :, 0:KC - 1], 0.0).then_inc(S["conv_step"], 1)
                dve.wait_ge(S["params_loaded"], 16 * N_PARAMS)
                nc.vector.tensor_tensor(mix_bias[:, 0, :], mix_bias[:, 0, :], mix_bias[:, 1, :], ALU.add).then_inc(S["mix_ready"], 1)
                dve.wait_ge(S["mix_ready"], 1)
                dve.wait_ge(S["conv_step"], 1)
                dve.wait_ge(S["masks"], 4 + 3 * CT)
                dve.wait_ge(S["lane_init"], 2)
                dve.sem_inc(S["o_read"], ST * KD)
                with dve.Fori(0, B) as b:
                    dve.wait_ge(S["x_loaded"], 16 * b + 16)
                    norm_vector(nc, dve, b, x, xln, nb, ns)
                    for k in range(KC - 1):
                        for t in range(NT):
                            if k == 0:
                                dve.wait_ge(S["qkv_read"], NT * b + t + 1)
                            else:
                                dve.wait_ge(S["conv_step"], 1 + KPB * b + NT * (k - 1) + t + 1)
                            nc.vector.scalar_tensor_tensor(conv[:, t, :], xpad[:, t, k:k + L], conv_w[:, t, k:k + 1],
                                                           conv[:, t, :], ALU.mult, ALU.add).then_inc(S["conv_step"], 1)
                        if k == 0:
                            dve.wait_ge(S["gate_psum"], b + 1)
                            gp = banks[0][:, 0:ST * 2 * H].rearrange("p (s h) -> p s h", s=ST)
                            nc.vector.tensor_copy(gates[:, :, 0:H], gp[:, :, 0:H])
                            nc.vector.tensor_tensor(gates[:, :, H:2 * H], gp[:, :, H:2 * H],
                                                    free_bcast(mix_bias[:, 0, :], 1, ST), ALU.add).then_inc(S["gate_pre"], 1)
                    dve.wait_ge(S["sq_ready"], b + 1)
                    nc.vector.tensor_reduce(ssq[:, :], squares.rearrange("p (a d) -> p a d", d=DK),
                                            AX_X, ALU.add).then_inc(S["ssq_ready"], 1)
                    dve.wait_ge(S["l2_std"], b + 1)
                    nc.vector.reciprocal(rnorm[:, :], ssq[:, :]).then_inc(S["l2_ready"], 1)
                    for st in range(ST):
                        for i, (dst, mask) in enumerate(((n_tok, neg_strict), (attn_t, upper))):
                            dve.wait_ge(S["gram_psum"], 2 * ST * b + 2 * st + i + 1)
                            for c in range(CT):
                                rows = slice(c * C, (c + 1) * C)
                                blocks = banks.whole[rows, HS * i:HS * i + HS, :].rearrange("p g (q k) -> p q g k", k=P)[
                                    :, 0:KD, :, c * C:(c + 1) * C]
                                out = dst[rows, st, :, :].rearrange("p (q g) j -> p q g j", g=HS)
                                m4 = free_bcast(free_bcast(mask[rows, :], 1, HS), 1, KD)
                                nc.vector.tensor_tensor(out, blocks, m4, ALU.mult).then_inc(S["gram_read"], 1)
                    ch = Chain(dve, S["solve"], SOLVE * b)
                    dve.wait_ge(S["n_loaded"], 16 * b + 16)
                    for i in range(1, C):
                        pr = prod[:, 0:i * i].rearrange("p (k j) -> p k j", j=i)
                        if i > 1:
                            ch.wait()
                        ch.step(nc.vector.tensor_tensor(pr, t_lane[:, 0:i, 0:i], free_bcast(n_lane[:, i, 0:i], 1, i), ALU.mult))
                        ch.wait()
                        ch.step(nc.vector.tensor_reduce(t_lane[:, 0:i, i], pr, AX_X, ALU.add))
                    assert ch.n == SOLVE
                    for n in range(NC):
                        st, rows = n // CT, slice((n % CT) * C, (n % CT + 1) * C)
                        if n:
                            for hh in range(KD):
                                dve.wait_ge(S["x_chunk"], CH * b + KD * (n - 1) + hh + 1)
                                nc.vector.tensor_tensor(y[rows, hh, :], vb[rows, st, hh * P:(hh + 1) * P],
                                                        banks[hh][rows, 0:P], ALU.subtract).then_inc(S["y_ready"], 1)
                        if n < NC - 1:
                            for hh in range(KD):
                                dve.wait_ge(S["s_psum"], CH * b + KD * n + hh + 1)
                                nc.vector.tensor_tensor(state[hh][:, :], banks[2 + hh][:, 0:P], head_mask[:, :],
                                                        ALU.mult).then_inc(S["s_ready"], 1)
                        if n % CT == CT - 1:
                            for hh in range(KD):
                                dve.wait_ge(S["o_psum"], ST * KD * b + KD * st + hh + 1)
                                nc.vector.tensor_tensor(o[:, st, hh * P:(hh + 1) * P], banks[4 + 2 * (st % 2) + hh][:, 0:P],
                                                        tok[:, st, 2 * D + hh * P:2 * D + (hh + 1) * P],
                                                        ALU.subtract).then_inc(S["o_read"], 1)
                    dve.wait_ge(S["o_sq"], b + 1)
                    nc.vector.tensor_reduce(oms[:, :], squares[:, 0:ST * D].rearrange("p (a d) -> p a d", d=DK),
                                            AX_X, ALU.add).then_inc(S["o_ms"], 1)
                    dve.wait_ge(S["o_std"], b + 1)
                    nc.vector.reciprocal(orstd[:, :], ostd[:, :]).then_inc(S["o_rstd"], 1)
                    for i in range(2):
                        dve.wait_ge(S["out_psum"], 2 * b + i + 1)
                        pair = x[:, 2 * i:2 * i + 2, :].rearrange("p s d -> p (s d)")
                        nc.vector.tensor_tensor(pair, pair, banks[2 + i][:, :], ALU.add).then_inc(S["out_added"], 1)

            @block.tensor
            def _(pe):
                pe.wait_ge(S["params_loaded"], 16 * N_PARAMS)
                with pe.Fori(0, B) as b:
                    pe.wait_ge(ns.xln, ST * b + ST)
                    transpose_tiles(nc, xln, ident, banks, S["xt_psum"])
                    pe.wait_ge(S["xt_ready"], KD * b + KD)
                    for t in range(NT):
                        for k in range(KD):
                            ins = nc.tensor.matmul(banks[2 + t][:, :], w_qkv[:, k, t * P:(t + 1) * P], xt[:, k, :],
                                                   start=(k == 0), stop=(k == KD - 1))
                        ins.then_inc(S["qkv_psum"], 1)
                    for st in range(ST):
                        for k in range(KD):
                            ins = nc.tensor.matmul(banks[0][:, st * 2 * H:(st + 1) * 2 * H], xt[:, k, st * P:(st + 1) * P],
                                                   w_gates[:, k, :], start=(k == 0), stop=(k == KD - 1))
                    ins.then_inc(S["gate_psum"], 1)
                    for t in range(NT):
                        pe.wait_ge(S["feat_ready"], NT * b + t + 1)
                        for st in range(ST):
                            ins = nc.tensor.transpose(banks[2 + t][:, st * P:(st + 1) * P], feat[:, t, st * P:(st + 1) * P], ident[:, :])
                        ins.then_inc(S["tok_psum"], 1)
                    for t in range(NT):
                        if t == 0:
                            pe.wait_ge(S["pool_step"], POOL * b + 2)
                            pe.wait_ge(S["tok_ready"], NT * (b + 1))
                        if t == 2 * KD:
                            pe.wait_ge(S["pool_step"], POOL * b + 3)
                        for st in range(ST):
                            src = tok[:, st, t * P:(t + 1) * P] if t < 2 * KD else kb[:, st, (t - 2 * KD) * P:(t - 2 * KD + 1) * P]
                            ins = nc.tensor.transpose(banks[2 + t][:, st * P:(st + 1) * P], src, ident[:, :])
                        ins.then_inc(S["featn_psum"], 1)
                    pe.wait_ge(S["featn_ready"], NT * (b + 1))
                    q_f, k_f, kb_f = feat[:, 0:KD, :], feat[:, KD:2 * KD, :], feat[:, 2 * KD:3 * KD, :]
                    for st in range(ST):
                        cols = slice(st * P, (st + 1) * P)
                        for i, (left, right) in enumerate(((kb_f, k_f), (k_f, q_f))):
                            if st:
                                pe.wait_ge(S["gram_read"], ST * 2 * CT * b + 2 * CT * (st - 1) + CT * (i + 1))
                            for hh in range(KD):
                                for g in range(HS):
                                    rows = slice(g * DK, (g + 1) * DK)
                                    ins = nc.tensor.matmul(banks[HS * i + g][:, hh * P:(hh + 1) * P], left[rows, hh, cols],
                                                           right[rows, hh, cols], start=True, stop=True)
                            ins.then_inc(S["gram_psum"], 1)
                    pe.wait_ge(S["gram_read"], ST * 2 * CT * (b + 1))
                    carried_wait(pe, passed, (S["t_loaded"], 16 * ST * b + 16 * ST))
                    for n in range(NC):
                        st, c = n // CT, n % CT
                        rows, cols = slice(c * C, (c + 1) * C), slice(n * C, (n + 1) * C)
                        obank = [banks[4 + 2 * (st % 2) + hh] for hh in range(KD)]
                        if n:
                            for hh in range(KD):
                                pe.wait_ge(S["s_ready"], CH * b + KD * (n - 1) + hh + 1)
                                nc.tensor.matmul(banks[hh][rows, 0:P], kb_f[:, hh, cols], state[hh][:, :],
                                                 start=True, stop=True).then_inc(S["x_chunk"], 1)
                        if c == 0 and st >= 2:
                            pe.wait_ge(S["o_read"], ST * KD * (b + 1) + KD * (st - 1))
                        if n:
                            for hh in range(KD):
                                nc.tensor.matmul(obank[hh][rows, 0:P], q_f[:, hh, cols], state[hh][:, :],
                                                 start=True, stop=True, skip_group_check=True)
                        for hh in range(KD):
                            if n:
                                carried_wait(pe, passed, (S["y_ready"], CH * b + KD * (n - 1) + hh + 1))
                            for g in range(HS):
                                h, hc = hh * HS + g, slice(g * DK, (g + 1) * DK)
                                rhs = y[rows, hh, hc] if n else vb[rows, st, h * DK:(h + 1) * DK]
                                ins = nc.tensor.matmul(banks[hh][rows, hc], t_tok[rows, st, h, :], rhs,
                                                       start=True, stop=True)
                            ins.then_inc(S["u_psum"], 1)
                        for hh in range(KD):
                            carried_wait(pe, passed, (S["u_ready"], KD * NC * b + KD * n + hh + 1))
                            if n < NC - 1:
                                nc.tensor.matmul(banks[2 + hh][:, 0:P], tok[rows, st, D + hh * P:D + (hh + 1) * P], u[rows, hh, :],
                                                 start=(n == 0), stop=True, skip_group_check=True).then_inc(S["s_psum"], 1)
                        for hh in range(KD):
                            for g in range(HS):
                                h, hc = hh * HS + g, slice(g * DK, (g + 1) * DK)
                                ins = nc.tensor.matmul(obank[hh][rows, hc], attn_t[rows, st, h, :], u[rows, hh, hc],
                                                       start=(n == 0), stop=True, skip_group_check=True)
                            if c == CT - 1:
                                ins.then_inc(S["o_psum"], 1)
                    pe.wait_ge(S["pool_step"], POOL * b + POOL)
                    for kt in range(KD):
                        for st in range(ST):
                            ins = nc.tensor.transpose(banks[kt][:, st * P:(st + 1) * P], o[:, st, kt * P:(kt + 1) * P], ident[:, :])
                        ins.then_inc(S["ot_psum"], 1)
                    pe.wait_ge(S["ot_ready"], KD * b + KD)
                    for i in range(2):
                        for st in range(2 * i, 2 * i + 2):
                            for k in range(KD):
                                ins = nc.tensor.matmul(banks[2 + i][:, (st % 2) * D:(st % 2 + 1) * D], xt[:, k, st * P:(st + 1) * P],
                                                       w_o[:, k, :], start=(k == 0), stop=(k == KD - 1))
                        ins.then_inc(S["out_psum"], 1)
                    pe.wait_ge(S["out_added"], 2 * b + 2)
        m.end_phase()


class Banks:

    def __init__(self, whole):
        self.whole = whole

    def __getitem__(self, i):
        if isinstance(i, slice):
            return [self[j] for j in range(i.start, i.stop)]
        return self.whole[:, i, :]


def build(nc, a, out):
    ctx = ExitStack()
    with ctx:
        m = Mem(nc, ctx)
        banks = Banks(ctx.enter_context(nc.psum_tensor("psum", [P, 8, BANK], F32)))
        consts = {"ident": m.sb("ident", P, P), "eps": m.sb("eps", P, 1)}
        weights = Weights(m, a["w1"], a["w2"])
        x1, x2, x3 = (nc.dram_tensor(f"x_after_{i}", [B, L, D], F32, kind="Internal").ap() for i in (1, 2, 3))
        bc_scratch = nc.dram_tensor("bc_scratch", [B, 2 * NS, L], F32, kind="Internal").ap()
        o_scratch = nc.dram_tensor("o_scratch", [E, B, D], F32, kind="Internal").ap()
        n_scratch = nc.dram_tensor("n_scratch", [B, H, L, C], F32, kind="Internal").ap()
        t_scratch = nc.dram_tensor("t_scratch", [B, H, L, C], F32, kind="Internal").ap()
        const_ready = m.sem("const_ready")
        with nc.Block() as block:
            @block.gpsimd
            def _(pool):
                nc.gpsimd.memset(consts["ident"][:, :], 0.0).then_inc(const_ready, 1)
                nc.gpsimd.memset(consts["eps"][:, :], EPS).then_inc(const_ready, 1)
                pool.wait_ge(const_ready, 2)
                nc.gpsimd.affine_select(out=consts["ident"][:, :], in_=consts["ident"][:, :], compare_op=ALU.not_equal,
                                        fill=1.0, base=0, pattern=[[-1, P]], channel_multiplier=1).then_inc(const_ready, 1)
                pool.wait_ge(const_ready, 3)
        steps = [lambda i, o: mamba_phase(nc, banks, consts, weights, i, o, a, bc_scratch),
                 lambda i, o: moe_phase(nc, banks, consts, weights, i, o, a, o_scratch, False),
                 lambda i, o: delta_phase(nc, banks, consts, i, o, a, n_scratch, t_scratch),
                 lambda i, o: moe_phase(nc, banks, consts, weights, i, o, a, o_scratch, True)][:PHASES]
        flow = [a["x"], x1, x2, x3][:PHASES] + [out]
        for i, step in enumerate(steps):
            step(flow[i], flow[i + 1])


PHASES = 4
_A, _B, _F = "L0_attn_a_", "L0_attn_b_", "L0_ffn_"
_PLAIN = {_A + "x": "x", _A + "conv_w": "conv_w", _A + "A_log": "A_log",
          **{_B + n: n for n in ("q_w", "k_w", "v_w", "conv_q_w", "conv_k_w", "conv_v_w", "b_w", "mix_w", "mix_b",
                                 "mix_bias", "o_norm_w", "o_w")},
          _F + "gate_b": "gate_b", _F + "w1": "w1", _F + "w2": "w2"}
_TRANSPOSED = {_A + "W_in": "W_inT", _A + "W_x": "W_xT", _A + "W_dt": "W_dtT", _A + "W_out": "W_outT",
               _F + "gate_w": "gate_wT"}
_COLUMNS = {_A + "conv_b": "conv_bT", _A + "b_dt": "b_dtT", _A + "Dp": "DpT"}


def kernel(**inputs):
    import numpy as _np
    import concourse.bacc as _bacc
    from concourse import mybir as _mybir
    from concourse.bass_utils import run_bass_kernel_spmd as _run

    nc = _bacc.Bacc("TRN2", target_bir_lowering=False, num_devices=1)
    arrays, args = {}, {}
    for names, lay in ((_PLAIN, lambda v: v), (_TRANSPOSED, lambda v: v.T), (_COLUMNS, lambda v: v.reshape(-1, P).T)):
        for name, short in names.items():
            v = _np.ascontiguousarray(lay(_np.asarray(inputs[name])))
            arrays[f"in_{short}"] = v
            args[short] = nc.dram_tensor(f"in_{short}", v.shape, _mybir.dt.from_np(v.dtype), kind="ExternalInput").ap()
    out = nc.dram_tensor("out_0", (B, L, D), F32, kind="ExternalOutput").ap()
    build(nc, args, out)
    r = _run(nc, [arrays], core_ids=[0])
    return r.results[0]["out_0"]
```

```python
from contextlib import ExitStack

import concourse.bass as bass
from concourse import mybir

ALU = mybir.AluOpType
ACT = mybir.ActivationFunctionType
F32 = mybir.dt.float32
AX_X = mybir.AxisListType.X
ds = bass.ds

P = 128
B, L, D = 8, 512, 256
ST = L // P
KD = D // P
BANK = 512
EPS = 1e-5

DI, NS, RK, KC = 512, 16, 64, 4
DT = DI // P
H, DK, C = 8, 32, 32
HS = P // DK
NC = L // C
CT = P // C
E, HID, TOP = 32, 1024, 8
EG, EQ = 4, 32
NG = E // EG
GP = NG // 2
QB = 4
HALVES = B // QB
MH = HID // P


class Mem:

    def __init__(self, nc, ctx):
        self.nc, self.ctx, self.sems = nc, ctx, []

    def sb(self, name, *shape):
        return self.ctx.enter_context(self.nc.sbuf_tensor(name, list(shape), F32))

    def sem(self, name):
        self.sems.append(self.nc.alloc_semaphore(name))
        return self.sems[-1]

    def end_phase(self):
        self.nc.clear_and_free_semaphores(self.sems)
        self.nc.all_engine_barrier()


class Chain:

    def __init__(self, eng, sem, base):
        self.eng, self.sem, self.base, self.n = eng, sem, base, 0

    def step(self, ins):
        self.n += 1
        ins.then_inc(self.sem, 1)

    def wait(self, passed=None):
        self.eng.wait_ge(self.sem, self.base + self.n)
        if passed:
            self.eng.sem_inc(passed, 1)


def free_bcast(ap, axis, n):
    shape = list(ap.shape)
    shape.insert(axis, n)
    return ap.unsqueeze(axis).to_broadcast(shape)


class NormSems:
    def __init__(self, m, tag):
        self.stats, self.turn, self.mv, self.std, self.rstd, self.xln = (
            m.sem(f"{tag}_{s}") for s in ("ln_stats", "ln_turn", "ln_mean_var", "ln_std", "ln_rstd", "ln_done"))


class NormBufs:
    def __init__(self, m, tag):
        self.stats = m.sb(f"{tag}_bn_stats", P, ST, 6)
        self.mv = m.sb(f"{tag}_mean_var", P, ST, 2)
        self.std = m.sb(f"{tag}_std", P, ST)
        self.rstd = m.sb(f"{tag}_rstd", P, ST)


def norm_vector(nc, dve, b, x, out, nb, ns):
    for st in range(ST):
        nc.vector.bn_stats(nb.stats[:, st, :], x[:, st, :]).then_inc(ns.stats, 1)
    carried_wait(dve, ns.turn, (ns.stats, ST * (b + 1)))
    for st in range(ST):
        nc.vector.bn_aggr(nb.mv[:, st, :], nb.stats[:, st, :]).then_inc(ns.mv, 1)
    dve.wait_ge(ns.std, b + 1)
    nc.vector.reciprocal(nb.rstd[:, :], nb.std[:, :]).then_inc(ns.rstd, 1)
    dve.wait_ge(ns.rstd, b + 1)
    for st in range(ST):
        nc.vector.tensor_scalar(out[:, st, :], x[:, st, :], nb.mv[:, st, 0:1], nb.rstd[:, st:st + 1],
                                ALU.subtract, ALU.mult).then_inc(ns.xln, 1)


def norm_scalar(nc, act, b, nb, ns, eps):
    act.wait_ge(ns.mv, ST * (b + 1))
    nc.scalar.activation(nb.std[:, :], nb.mv[:, :, 1], ACT.Sqrt, bias=eps[:, :]).then_inc(ns.std, 1)


def transpose_tiles(nc, xln, ident, banks, done):
    for kt in range(KD):
        for st in range(ST):
            ins = nc.tensor.transpose(banks[kt][:, st * P:(st + 1) * P], xln[:, st, kt * P:(kt + 1) * P], ident[:, :])
        ins.then_inc(done, 1)


def carried_wait(eng, passed, *waits):
    for sem, value in waits:
        if not isinstance(value, int) or value > 0:
            eng.wait_ge(sem, value)
    eng.sem_inc(passed, 1)


def token_major(x_dram, b):
    if isinstance(b, int):
        return x_dram[b].rearrange("(s p) d -> p s d", p=P)
    return x_dram[ds(b, 1), :, :].rearrange("o (s p) d -> p (o s) d", p=P)


class Weights:

    def __init__(self, m, tag, w1, w2):
        self.w1_dram, self.w2_dram = w1, w2
        self.w1 = [m.sb(f"{tag}_w1_set{s}", P, EG, KD, HID) for s in range(2)]
        self.w2 = [m.sb(f"{tag}_w2_set{s}", P, EG, MH, D) for s in range(2)]
        self.loaded = [[m.sem(f"{tag}_w{which}_set{s}_loaded") for which in (1, 2)] for s in range(2)]

    def load(self, nc, s, which, group):
        slots, dram, rows, per = ((self.w1, self.w1_dram, D, KD), (self.w2, self.w2_dram, HID, MH))[which - 1]
        nc.sync.dma_start(slots[s][:, :, :, :], dram[ds(group * EG, EG), 0:rows, :].rearrange(
            "e (p t) n -> p e t n", t=per)).then_inc(self.loaded[s][which - 1], 16)


def mamba_phase(nc, banks, consts, x_in, x_out, prm, scratch):
    ident, eps = consts["ident"], consts["eps"]
    ybank, fbank = banks[0:4], banks[4:8]
    RING = 8
    AHEAD = 4
    with ExitStack() as ctx:
        m = Mem(nc, ctx)
        w_in = m.sb("w_in", P, KD, 2 * DI)
        w_x = m.sb("w_x", P, DT, RK + 2 * NS)
        w_dt = m.sb("w_dt", RK, DI)
        w_out = m.sb("w_out", P, DT, D)
        conv_w = m.sb("conv_w", P, DT, KC)
        conv_b = m.sb("conv_b", P, DT)
        b_dt = m.sb("b_dt", P, DT)
        dp = m.sb("dp", P, DT)
        a_neg = m.sb("a_neg", P, DT, NS)
        a_exp = m.sb("a_exp", P, DT, NS)
        dp_diag = m.sb("dp_diag", P, DT, P)
        x = m.sb("x_mamba", P, ST, D)
        nb = NormBufs(m, "mamba")
        xt = m.sb("xt", P, KD, L)
        xpad = m.sb("xpad", P, DT, KC - 1 + L)
        conv = m.sb("conv", P, DT, L)
        xln = conv[:, 0:2, :].rearrange("p t l -> p (t l)").rearrange("p (s d) -> p s d", d=D)
        x_res = conv[:, 2:4, :].rearrange("p t l -> p (t l)").rearrange("p (s d) -> p s d", d=D)
        zs = m.sb("z_silu", P, DT, L)
        xc = m.sb("x_conv", P, DT, L)
        dbc = m.sb("dbc", RK + 2 * NS, L)
        deltas = [m.sb(f"delta{i}", P, DT, L) for i in range(2)]
        dx = m.sb("delta_x", P, DT, L)
        b_row = [m.sb(f"b_row{i}", P, 1, L) for i in range(2)]
        c_row = [m.sb(f"c_row{i}", P, 1, L) for i in range(2)]
        decay = [m.sb(f"decay{i}", P, DT, L) for i in range(AHEAD)]
        ring = [m.sb(f"state{i}", P, DT, L) for i in range(RING)]

        ns = NormSems(m, "mamba")
        S = {k: m.sem("ma_" + k) for k in (
            "params_loaded", "a_exp", "a_ready", "dp_diag", "pads_zero", "x_loaded", "res_loaded", "xt_psum", "xt_ready",
            "xp_psum", "xp_read", "z_psum", "z_read", "conv_step", "xc_ready", "dbc_psum", "dbc_ready", "bc_stored",
            "b_loaded0", "b_loaded1", "c_loaded0", "c_loaded1", "delta_psum", "soft", "soft_done", "delta_ready",
            "dx_ready", "decay_ready", "bx_ready", "scan_done", "hc_ready", "sum_done", "yz_done",
            "out_psum", "out_added", "x_stored")}
        N_PARAMS = 9

        passed = m.sem(f"sync_passed_{m.nc.next_id()}")

        def iterations(eng, iteration):
            iteration(0, 0)
            with eng.Fori(0, (B - 2) // 2) as i:
                iteration(2 * i + 1, 1)
                iteration(2 * i + 2, 0)
            iteration(B - 1, (B - 1) % 2)

        first = lambda b: isinstance(b, int) and b == 0
        last = lambda b: isinstance(b, int) and b == B - 1

        with nc.Block() as block:
            @block.sync
            def _(sp):
                def load_x(b):
                    sp.dma_start(x[:, :, :], token_major(x_in, b)).then_inc(S["x_loaded"], 16)

                def store_bc(b):
                    carried_wait(sp, passed, (S["dbc_ready"], b + 1))
                    sp.dma_start(scratch[ds(b, 1), :, :].rearrange("o r l -> (o r) l"),
                                 dbc[RK:RK + 2 * NS, :]).then_inc(S["bc_stored"], 16)

                def load_row(b, n, which, rows, used):
                    carried_wait(sp, passed, (used, NS * b + n - 1))
                    src = scratch[ds(b, 1), which * NS + n:which * NS + n + 1, :].rearrange("o r l -> (o r) l")
                    sp.dma_start(rows[n % 2][:, :, :], src.partition_broadcast(P)).then_inc(
                        S[f"{'bc'[which]}_loaded{n % 2}"], 16)

                def load_residual(b):
                    carried_wait(sp, passed, (S["x_stored"], 16 * b), (S["delta_ready"], B if last(b) else b + 2))
                    sp.dma_start(x_res, token_major(x_in, b)).then_inc(S["res_loaded"], 16)

                def store_x(b):
                    carried_wait(sp, passed, (S["out_added"], 2 * b + 2))
                    sp.dma_start(token_major(x_out, b), x_res).then_inc(S["x_stored"], 16)

                def iteration(b, parity):
                    if not last(b):
                        carried_wait(sp, passed, (ns.xln, ST * b + ST))
                        load_x(b + 1)
                    carried_wait(sp, passed, (S["bc_stored"], 16 * b + 16))
                    for n in range(NS + 1):
                        if n < NS:
                            load_row(b, n, 0, b_row, S["bx_ready"])
                        if n:
                            load_row(b, n - 1, 1, c_row, S["hc_ready"])
                        if n == 1 and not first(b):
                            load_residual(b - 1)
                        if n == 6 and not first(b):
                            store_x(b - 1)
                    if not last(b):
                        store_bc(b + 1)

                load_x(0)
                for dst, src in (
                        (w_in[:, :, :], prm["W_inT"].rearrange("(k p) n -> p k n", p=P)),
                        (w_x[:, :, :], prm["W_xT"].rearrange("(k p) n -> p k n", p=P)),
                        (w_dt[:, :], prm["W_dtT"]),
                        (w_out[:, :, :], prm["W_outT"].rearrange("(k p) n -> p k n", p=P)),
                        (conv_w[:, :, :], prm["conv_w"].rearrange("(t p) k -> p t k", p=P)),
                        (conv_b[:, :], prm["conv_bT"]),
                        (b_dt[:, :], prm["b_dtT"]),
                        (dp[:, :], prm["DpT"]),
                        (a_exp[:, :, :], prm["A_log"].rearrange("(t p) n -> p t n", p=P))):
                    sp.dma_start(dst, src).then_inc(S["params_loaded"], 16)
                store_bc(0)
                iterations(sp, iteration)
                load_residual(B - 1)
                store_x(B - 1)
                sp.wait_ge(S["x_stored"], 16 * B)

            @block.gpsimd
            def _(pool):
                def iteration(b, parity):
                    pool.wait_ge(S["delta_ready"], b + 1)
                    pool.wait_ge(S["xc_ready"], b + 1)
                    if not first(b):
                        pool.wait_ge(S["bx_ready"], NS * b)
                    nc.gpsimd.tensor_tensor(dx[:, :, :], deltas[parity][:, :, :], xc[:, :, :],
                                            ALU.mult).then_inc(S["dx_ready"], 1)
                    pool.wait_ge(S["dx_ready"], b + 1)
                    for n in range(NS):
                        pool.wait_ge(S[f"b_loaded{n % 2}"], 16 * (NS // 2) * b + 16 * (n // 2 + 1))
                        if not first(b) or n >= RING:
                            pool.wait_ge(S["sum_done"], NS * b + n - RING + 1)
                        nc.gpsimd.tensor_tensor(ring[n % RING][:, :, :], dx[:, :, :],
                                                free_bcast(b_row[n % 2][:, 0, :], 1, DT), ALU.mult).then_inc(S["bx_ready"], 1)

                for i in range(AHEAD):
                    nc.gpsimd.memset(decay[i][:, :, 0], 0.0).then_inc(S["pads_zero"], 1)
                nc.gpsimd.memset(xpad[:, :, 0:KC - 1], 0.0).then_inc(S["pads_zero"], 1)
                iterations(pool, iteration)

            @block.scalar
            def _(act):
                def xt_copies(b):
                    for kt in range(KD):
                        act.wait_ge(S["xt_psum"], KD * b + kt + 1)
                        nc.scalar.copy(xt[:, kt, :], fbank[kt][:, :]).then_inc(S["xt_ready"], 1)

                def last_tap(b):
                    if not first(b):
                        act.wait_ge(S["delta_ready"], b)
                    if not first(b) and not (isinstance(b, int) and b == 1):
                        act.wait_ge(S["x_stored"], 16 * b - 16)
                    for t in range(DT):
                        act.wait_ge(S["xp_psum"], DT * b + t + 1)
                        nc.scalar.activation(conv[:, t, :], fbank[t][:, :], ACT.Identity, bias=conv_b[:, t:t + 1],
                                             scale=conv_w[:, t, KC - 1:KC])
                        nc.scalar.copy(xpad[:, t, KC - 1:], fbank[t][:, :]).then_inc(S["xp_read"], 1)

                def conv_silu(b):
                    act.wait_ge(S["conv_step"], DT * (KC - 1) * b + DT * (KC - 1))
                    if not first(b):
                        act.wait_ge(S["dx_ready"], b)
                    nc.scalar.activation(xc[:, :, :], conv[:, :, :], ACT.Silu).then_inc(S["xc_ready"], 1)

                def copy_dbc(b):
                    act.wait_ge(S["dbc_psum"], b + 1)
                    if not first(b):
                        act.wait_ge(S["bc_stored"], 16 * b)
                    nc.scalar.copy(dbc[:, :], fbank[0][0:RK + 2 * NS, :]).then_inc(S["dbc_ready"], 1)

                def softplus_parts(b, parity):
                    for t in range(DT):
                        act.wait_ge(S["delta_psum"], DT * b + t + 1)
                        nc.scalar.activation(conv[:, t, :], fbank[t][:, :], ACT.Abs, bias=b_dt[:, t:t + 1])
                        nc.scalar.activation(deltas[parity][:, t, :], fbank[t][:, :], ACT.Relu,
                                             bias=b_dt[:, t:t + 1]).then_inc(S["soft_done"], 1)
                    act.wait_ge(S["soft_done"], DT * b + DT)
                    nc.scalar.activation(conv[:, :, :], conv[:, :, :], ACT.Exp, scale=-1.0).then_inc(S["soft"], 1)
                    act.wait_ge(S["soft"], 2 * b + 1)
                    nc.scalar.activation(conv[:, :, :], conv[:, :, :], ACT.Ln, bias=1.0).then_inc(S["soft"], 1)

                def z_silu(b, tiles):
                    if not first(b):
                        act.wait_ge(S["out_psum"], 2 * b)
                    for t in tiles:
                        act.wait_ge(S["z_psum"], DT * b + t + 1)
                        nc.scalar.activation(zs[:, t, :], fbank[2 + t % 2][:, :], ACT.Silu).then_inc(S["z_read"], 1)

                def iteration(b, parity):
                    act.wait_ge(S["delta_ready"], b + 1)
                    for n in range(NS):
                        if not first(b) or n >= AHEAD:
                            act.wait_ge(S["scan_done"], NS * b + n - AHEAD + 1)
                        for t in range(DT):
                            ins = nc.scalar.activation(decay[n % AHEAD][:, t, 1:], deltas[parity][:, t, 1:], ACT.Exp,
                                                       scale=a_neg[:, t, n:n + 1])
                        ins.then_inc(S["decay_ready"], 1)
                        if n == 3:
                            z_silu(b, (0, 1))
                        if n == 4:
                            z_silu(b, (2, 3))
                        if last(b):
                            continue
                        if n == 2:
                            norm_scalar(nc, act, b + 1, nb, ns, eps)
                        if n == 5:
                            xt_copies(b + 1)
                        if n == 6:
                            last_tap(b + 1)
                        if n == 9:
                            conv_silu(b + 1)
                        if n == 11:
                            copy_dbc(b + 1)
                        if n == 13:
                            softplus_parts(b + 1, 1 - parity)

                norm_scalar(nc, act, 0, nb, ns, eps)
                act.wait_ge(S["params_loaded"], 16 * N_PARAMS)
                nc.scalar.activation(a_neg[:, :, :], a_exp[:, :, :], ACT.Exp).then_inc(S["a_exp"], 1)
                act.wait_ge(S["pads_zero"], AHEAD + 1)
                xt_copies(0)
                last_tap(0)
                conv_silu(0)
                copy_dbc(0)
                softplus_parts(0, 0)
                act.wait_ge(S["a_ready"], 1)
                iterations(act, iteration)

            @block.vector
            def _(dve):
                def norm_statistics(b):
                    dve.wait_ge(S["x_loaded"], 16 * b + 16)
                    for st in range(ST):
                        nc.vector.bn_stats(nb.stats[:, st, :], x[:, st, :]).then_inc(ns.stats, 1)
                    carried_wait(dve, ns.turn, (ns.stats, ST * (b + 1)))
                    for st in range(ST):
                        nc.vector.bn_aggr(nb.mv[:, st, :], nb.stats[:, st, :]).then_inc(ns.mv, 1)

                def norm_apply(b):
                    dve.wait_ge(ns.std, b + 1)
                    nc.vector.reciprocal(nb.rstd[:, :], nb.std[:, :]).then_inc(ns.rstd, 1)
                    dve.wait_ge(ns.rstd, b + 1)
                    if not first(b):
                        dve.wait_ge(S["delta_ready"], b)
                    for st in range(ST):
                        nc.vector.tensor_scalar(xln[:, st, :], x[:, st, :], nb.mv[:, st, 0:1], nb.rstd[:, st:st + 1],
                                                ALU.subtract, ALU.mult).then_inc(ns.xln, 1)

                def tap(b, k):
                    for t in range(DT):
                        if k == 0:
                            dve.wait_ge(S["xp_read"], DT * b + t + 1)
                        else:
                            dve.wait_ge(S["conv_step"], DT * (KC - 1) * b + DT * (k - 1) + t + 1)
                        nc.vector.scalar_tensor_tensor(conv[:, t, :], xpad[:, t, k:k + L], conv_w[:, t, k:k + 1],
                                                       conv[:, t, :], ALU.mult, ALU.add).then_inc(S["conv_step"], 1)

                def softplus_sum(b, parity):
                    dve.wait_ge(S["soft"], 2 * b + 2)
                    nc.vector.tensor_tensor(deltas[parity][:, :, :], deltas[parity][:, :, :], conv[:, :, :],
                                            ALU.add).then_inc(S["delta_ready"], 1)

                def gate_y(b):
                    for t in range(DT):
                        dve.wait_ge(S["sum_done"], NS * b + NS)
                        nc.vector.tensor_tensor(zs[:, t, :], ybank[t][:, :], zs[:, t, :], ALU.mult).then_inc(S["yz_done"], 1)

                def add_output(b):
                    dve.wait_ge(S["res_loaded"], 16 * b + 16)
                    for i in range(2):
                        dve.wait_ge(S["out_psum"], 2 * b + i + 1)
                        pair = x_res[:, 2 * i:2 * i + 2, :].rearrange("p s d -> p (s d)")
                        nc.vector.tensor_tensor(pair, pair, fbank[i][:, :], ALU.add).then_inc(S["out_added"], 1)

                def iteration(b, parity):
                    for n in range(NS):
                        dve.wait_ge(S["decay_ready"], NS * b + n + 1)
                        dve.wait_ge(S["bx_ready"], NS * b + n + 1)
                        flat = ring[n % RING][:, :, :].rearrange("p t l -> p (t l)")
                        nc.vector.tensor_tensor_scan(flat, decay[n % AHEAD][:, :, :].rearrange("p t l -> p (t l)"), flat, 0.0,
                                                     ALU.mult, ALU.add).then_inc(S["scan_done"], 1)
                        dve.wait_ge(S["scan_done"], NS * b + n + 1)
                        dve.wait_ge(S[f"c_loaded{n % 2}"], 16 * (NS // 2) * b + 16 * (n // 2 + 1))
                        nc.vector.tensor_tensor(ring[n % RING][:, :, :], ring[n % RING][:, :, :],
                                                free_bcast(c_row[n % 2][:, 0, :], 1, DT), ALU.mult).then_inc(S["hc_ready"], 1)
                        if n == 0 and not last(b):
                            norm_statistics(b + 1)
                        if n == 1 and not first(b):
                            gate_y(b - 1)
                        if n == 2 and not last(b):
                            norm_apply(b + 1)
                        if n == 3 and not first(b):
                            add_output(b - 1)
                        if 5 <= n < 5 + KC - 1 and not last(b):
                            tap(b + 1, n - 5)
                        if n == 13 and not last(b):
                            softplus_sum(b + 1, 1 - parity)

                norm_statistics(0)
                norm_apply(0)
                dve.wait_ge(S["a_exp"], 1)
                nc.vector.tensor_scalar(a_neg[:, :, :], a_neg[:, :, :], -1.0, None, ALU.mult).then_inc(S["a_ready"], 1)
                for t in range(DT):
                    nc.vector.tensor_scalar(dp_diag[:, t, :], ident[:, :], dp[:, t:t + 1], None,
                                            ALU.mult).then_inc(S["dp_diag"], 1)
                dve.wait_ge(S["pads_zero"], AHEAD + 1)
                for k in range(KC - 1):
                    tap(0, k)
                softplus_sum(0, 0)
                iterations(dve, iteration)
                gate_y(B - 1)
                add_output(B - 1)

            @block.tensor
            def _(pe):
                def transposes(b):
                    pe.wait_ge(ns.xln, ST * b + ST)
                    if not first(b) and not (isinstance(b, int) and b == 1):
                        pe.wait_ge(S["out_added"], 2 * b - 2)
                    transpose_tiles(nc, xln, ident, fbank, S["xt_psum"])

                def project(tile, bank, done):
                    for k in range(KD):
                        ins = nc.tensor.matmul(fbank[bank][:, :], w_in[:, k, tile * P:(tile + 1) * P], xt[:, k, :],
                                               start=(k == 0), stop=(k == KD - 1))
                    ins.then_inc(done, 1)

                def project_x(b):
                    pe.wait_ge(S["xt_ready"], KD * b + KD)
                    for t in range(DT):
                        if t == 2 and not first(b):
                            pe.wait_ge(S["z_read"], DT * b)
                        project(t, t, S["xp_psum"])

                def project_z(b, tiles):
                    for t in tiles:
                        if t < 2:
                            pe.wait_ge(S["soft_done"], DT * b + DT)
                        else:
                            pe.wait_ge(S["z_read"], DT * b + t - 1)
                        project(DT + t, 2 + t % 2, S["z_psum"])

                def project_dbc(b):
                    pe.wait_ge(S["xc_ready"], b + 1)
                    pe.wait_ge(S["xp_read"], DT * b + DT)
                    for k in range(DT):
                        ins = nc.tensor.matmul(fbank[0][0:RK + 2 * NS, :], w_x[:, k, :], xc[:, k, :],
                                               start=(k == 0), stop=(k == DT - 1))
                    ins.then_inc(S["dbc_psum"], 1)

                def project_delta(b):
                    pe.wait_ge(S["dbc_ready"], b + 1)
                    for t in range(DT):
                        nc.tensor.matmul(fbank[t][:, :], w_dt[:, t * P:(t + 1) * P], dbc[0:RK, :],
                                         start=True, stop=True).then_inc(S["delta_psum"], 1)

                def project_out(b):
                    pe.wait_ge(S["yz_done"], DT * b + DT)
                    for i in range(2):
                        for st in range(2 * i, 2 * i + 2):
                            for k in range(DT):
                                ins = nc.tensor.matmul(fbank[i][:, (st % 2) * D:(st % 2 + 1) * D],
                                                       zs[:, k, st * P:(st + 1) * P], w_out[:, k, :],
                                                       start=(k == 0), stop=(k == DT - 1))
                        ins.then_inc(S["out_psum"], 1)

                def iteration(b, parity):
                    for t in range(DT):
                        if not first(b):
                            pe.wait_ge(S["yz_done"], DT * b - DT + t + 1)
                        nc.tensor.matmul(ybank[t][:, :], dp_diag[:, t, :], xc[:, t, :], start=True, stop=False)
                    project_z(b, (0, 1))
                    if not first(b):
                        project_out(b - 1)
                    for n in range(NS):
                        pe.wait_ge(S["hc_ready"], NS * b + n + 1)
                        for t in range(DT):
                            ins = nc.tensor.matmul(ybank[t][:, :], ident[:, :], ring[n % RING][:, t, :],
                                                   start=False, stop=(n == NS - 1))
                        ins.then_inc(S["sum_done"], 1)
                        if n == 0:
                            project_z(b, (2, 3))
                        if last(b):
                            continue
                        if n == 1:
                            transposes(b + 1)
                        if n == 2:
                            project_x(b + 1)
                        if n == 7:
                            project_dbc(b + 1)
                        if n == 8:
                            project_delta(b + 1)

                pe.wait_ge(S["params_loaded"], 16 * N_PARAMS)
                pe.wait_ge(S["dp_diag"], DT)
                transposes(0)
                project_x(0)
                project_dbc(0)
                project_delta(0)
                iterations(pe, iteration)
                project_out(B - 1)
        m.end_phase()


def moe_phase(nc, banks, consts, x_in, x_out, prm, o_scratch, tag):
    ident, eps = consts["ident"], consts["eps"]
    with ExitStack() as ctx:
        m = Mem(nc, ctx)
        weights = Weights(m, tag, prm["w1"], prm["w2"])
        gate = m.sb(f"{tag}_gate", P, KD, E)
        gate_b = m.sb(f"{tag}_gate_b", P, 1)
        b2 = m.sb(f"{tag}_b2", P, D)
        x = m.sb(f"{tag}_x", P, B, ST, D)
        xt = [m.sb(f"{tag}_xt{i}", P, KD, L) for i in range(2)]
        stats = [m.sb(f"{tag}_bn_stats{i}", P, QB * ST, 6) for i in range(HALVES)]
        mv = [m.sb(f"{tag}_mean_var{i}", P, QB * ST, 2) for i in range(HALVES)]
        std = [m.sb(f"{tag}_std{i}", P, QB * ST) for i in range(HALVES)]
        rstd = [m.sb(f"{tag}_rstd{i}", P, QB * ST) for i in range(HALVES)]
        probs = [m.sb(f"{tag}_probs{i}", P, L) for i in range(HALVES)]
        nmax = [m.sb(f"{tag}_nmax{i}", P, 1) for i in range(HALVES)]
        total = [m.sb(f"{tag}_total{i}", P, 1) for i in range(HALVES)]
        inv = [m.sb(f"{tag}_inv{i}", P, 1) for i in range(HALVES)]
        top = [m.sb(f"{tag}_top{i}", P, TOP) for i in range(HALVES)]
        rest = [m.sb(f"{tag}_rest{i}", P, L) for i in range(HALVES)]
        route = m.sb(f"{tag}_route", P, HALVES, L)
        route_t = m.sb(f"{tag}_route_t", P, ST, P)
        mrg = m.sb(f"{tag}_merged_e", P, D)
        merged = m.sb(f"{tag}_merged", P, KD, E, B)
        mg = [m.sb(f"{tag}_merged_g{s}", P, KD, EG, EQ) for s in range(2)]
        b1 = [m.sb(f"{tag}_b1_{s}", P, HID) for s in range(2)]
        hid = xt[0][:, :, :].rearrange("p k l -> p (k l)")
        hid_t = xt[1][:, :, :].rearrange("p k l -> p (k l)").rearrange("p (k c) -> p k c", c=P)
        o_sb = [m.sb(f"{tag}_o{s}", P, D) for s in range(2)]
        o_all = m.sb(f"{tag}_o_all", P, HALVES, D)

        S = {k: m.sem(f"{tag}_{k}") for k in (
            "params_loaded", "zeroed", "x_loaded0", "x_loaded1", "stats", "mv", "std", "rstd", "xln", "xt_psum",
            "xt_ready", "logit_psum", "soft0", "soft1", "exp_done", "route_ready", "route_t_psum", "route_t_ready",
            "mrg_psum", "mrg_ready", "merged_psum", "merged_ready", "mg_ready", "b1_loaded0", "b1_loaded1", "h_psum", "pre_ready",
            "gelu_ready", "ht_psum", "ht_ready", "o_psum", "o_ready", "o_stored0", "o_stored1", "o_loaded", "o_all_ready",
            "x_again0", "x_again1", "y_psum", "y_added", "x_stored")}
        N_PARAMS = 1 + 2 * QB
        logit_bank = (banks[4], banks[7])
        passed = m.sem(f"{tag}_passed")
        group_of = lambda i, s: 2 * i + s

        with nc.Block() as block:
            @block.sync
            def _(sp):
                for half in range(HALVES):
                    for q in range(QB):
                        sp.dma_start(x[:, half * QB + q, :, :], token_major(x_in, half * QB + q)).then_inc(
                            S[f"x_loaded{half}"], 16)
                    if half == 0:
                        sp.dma_start(gate[:, :, :], prm["gate_wT"].rearrange("(k p) e -> p k e", p=P)).then_inc(
                            S["params_loaded"], 16)
                        for q in range(QB):
                            rows = slice(q * E, (q + 1) * E)
                            sp.dma_start(gate_b[rows, :], prm["gate_b"].unsqueeze(1)).then_inc(S["params_loaded"], 16)
                            sp.dma_start(b2[rows, :], weights.w2_dram[:, HID, :]).then_inc(S["params_loaded"], 16)
                for s in range(2):
                    for which in (1, 2):
                        weights.load(nc, s, which, group_of(0, s))
                sp.wait_ge(S["mrg_psum"], HALVES)
                for b in range(B):
                    sp.dma_start(x[:, b, :, :], token_major(x_in, b)).then_inc(S[f"x_again{b // QB}"], 16)
                with sp.Fori(1, GP) as i:
                    for s in range(2):
                        for which, used in ((1, "pre_ready"), (2, "o_ready")):
                            carried_wait(sp, passed, (S[used], 2 * i + s - 1))
                            weights.load(nc, s, which, group_of(i, s))
                for s in range(2):
                    sp.wait_ge(S[f"o_stored{s}"], 16 * EG * (GP + 1))
                for half in range(HALVES):
                    for q in range(QB):
                        sp.dma_start(o_all[q * E:(q + 1) * E, half, :],
                                     o_scratch[:, half * QB + q, :]).then_inc(S["o_loaded"], 16)
                for b in range(B):
                    sp.wait_ge(S["y_added"], 2 * (b + 1))
                    sp.dma_start(token_major(x_out, b), x[:, b, :, :]).then_inc(S["x_stored"], 16)
                sp.wait_ge(S["x_stored"], 16 * B)

            @block.gpsimd
            def _(pool):
                for s in range(2):
                    nc.gpsimd.memset(mg[s][:, :, :, :], 0.0).then_inc(S["zeroed"], 1)
                    nc.gpsimd.memset(b1[s][:, :], 0.0).then_inc(S["zeroed"], 1)
                pool.wait_ge(S["zeroed"], 4)

                def load_b1(i, s):
                    for j in range(EG):
                        row = weights.w1_dram[ds(group_of(i, s) * EG + j, 1), D, :]
                        pool.dma_start(b1[s][j * EQ:j * EQ + B, :], row.partition_broadcast(B)).then_inc(S[f"b1_loaded{s}"], 16)

                for s in range(2):
                    load_b1(0, s)
                with pool.Fori(1, GP) as i:
                    for s in range(2):
                        carried_wait(pool, passed, (S["pre_ready"], 2 * i + s - 1))
                        load_b1(i, s)

            @block.scalar
            def _(act):
                act.wait_ge(S["params_loaded"], 16 * N_PARAMS)
                def root(half):
                    act.wait_ge(S["mv"], QB * ST * (half + 1))
                    nc.scalar.activation(std[half][:, :], mv[half][:, :, 1], ACT.Sqrt, bias=eps[:, :]).then_inc(S["std"], 1)

                def exponential(half):
                    act.wait_ge(S[f"soft{half}"], 2)
                    nc.scalar.activation(probs[half][:, :], probs[half][:, :], ACT.Exp, bias=nmax[half][:, :],
                                         accum_out=total[half][:, :]).then_inc(S["exp_done"], 1)

                root(0)
                for n in range(B):
                    for kt in range(KD):
                        act.wait_ge(S["xt_psum"], n * KD + kt + 1)
                        if n >= 2:
                            act.wait_ge(S["logit_psum"], n - 1)
                        nc.scalar.copy(xt[n % 2][:, kt, :], banks[2 * (n % 2) + kt][:, :]).then_inc(S["xt_ready"], 1)
                    if n == 1:
                        root(1)
                    if n == QB + 1:
                        exponential(0)
                exponential(1)
                act.wait_ge(S["logit_psum"], B)
                act.sem_inc(S["gelu_ready"], 1)
                for s in range(2):
                    act.sem_inc(S[f"o_stored{s}"], 16 * EG)
                with act.Fori(0, GP) as i:
                    for s in range(2):
                        n = 2 * i + s
                        act.wait_ge(S["pre_ready"], n + 1)
                        nc.scalar.activation(hid, hid, ACT.Gelu).then_inc(S["gelu_ready"], 1)
                        act.wait_ge(S["ht_psum"], 2 * n + 4)
                        act.wait_ge(S["o_psum"], n + 1)
                        nc.scalar.copy(hid_t[:, MH // 2:, :].rearrange("p k c -> p (k c)"), banks[5][:, :]).then_inc(
                            S["ht_ready"], 1)
                        carried_wait(act, passed, (S["o_ready"], n + 1))
                        for j in range(EG):
                            row = o_scratch[ds(group_of(i, s) * EG + j, 1), :, :].rearrange("o b d -> (o b) d")
                            act.dma_start(row, o_sb[s][j * EQ:j * EQ + B, :]).then_inc(S[f"o_stored{s}"], 16)

            @block.vector
            def _(dve):
                dve.wait_ge(S["params_loaded"], 16 * N_PARAMS)
                def layer_norm(half):
                    dve.wait_ge(S[f"x_loaded{half}"], 16 * QB)
                    for t in range(QB * ST):
                        nc.vector.bn_stats(stats[half][:, t, :], x[:, half * QB + t // ST, t % ST, :]).then_inc(S["stats"], 1)
                    dve.wait_ge(S["stats"], QB * ST * (half + 1))
                    for t in range(QB * ST):
                        nc.vector.bn_aggr(mv[half][:, t, :], stats[half][:, t, :]).then_inc(S["mv"], 1)
                    dve.wait_ge(S["std"], half + 1)
                    nc.vector.reciprocal(rstd[half][:, :], std[half][:, :]).then_inc(S["rstd"], 1)
                    dve.wait_ge(S["rstd"], half + 1)
                    for t in range(QB * ST):
                        tile = x[:, half * QB + t // ST, t % ST, :]
                        nc.vector.tensor_scalar(tile, tile, mv[half][:, t, 0:1], rstd[half][:, t:t + 1],
                                                ALU.subtract, ALU.mult).then_inc(S["xln"], 1)

                def logits_and_maximum(half):
                    ch = Chain(dve, S[f"soft{half}"], 0)
                    dve.wait_ge(S["logit_psum"], QB * (half + 1))
                    ch.step(nc.vector.tensor_scalar(probs[half][:, :], logit_bank[half][:, :], gate_b[:, :], None, ALU.add))
                    ch.wait()
                    ch.step(nc.vector.tensor_reduce(nmax[half][:, :], probs[half][:, :], AX_X, ALU.max, negate=True))

                def choose(half):
                    ch = Chain(dve, S[f"soft{half}"], 2)
                    dve.wait_ge(S["exp_done"], half + 1)
                    ch.step(nc.vector.reciprocal(inv[half][:, :], total[half][:, :]))
                    ch.wait()
                    ch.step(nc.vector.tensor_scalar(probs[half][:, :], probs[half][:, :], inv[half][:, :], None, ALU.mult))
                    ch.wait()
                    ch.step(nc.vector.max(top[half][:, :], probs[half][:, :]))
                    ch.wait()
                    ch.step(nc.vector.match_replace(rest[half][:, :], top[half][:, :], probs[half][:, :], 0.0))
                    ch.wait()
                    nc.vector.tensor_tensor(route[:, half, :], probs[half][:, :], rest[half][:, :], ALU.subtract).then_inc(
                        S["route_ready"], 1)

                def gathered(half):
                    dve.wait_ge(S["route_t_psum"], half + 1)
                    nc.vector.tensor_copy(route_t[:, :, :].rearrange("p s c -> p (s c)"), banks[5][:, :]).then_inc(
                        S["route_t_ready"], 1)
                    dve.wait_ge(S["mrg_psum"], half + 1)
                    nc.vector.tensor_copy(mrg[:, :], banks[6][:, 0:D]).then_inc(S["mrg_ready"], 1)
                    dve.wait_ge(S["merged_psum"], half + 1)
                    for t in range(KD):
                        nc.vector.tensor_copy(
                            merged[:, t, :, half * QB:(half + 1) * QB],
                            banks[7][:, t * P:(t + 1) * P].rearrange("p (q e) -> p e q", q=QB)).then_inc(S["merged_ready"], 1)

                layer_norm(0)
                layer_norm(1)
                logits_and_maximum(0)
                choose(0)
                logits_and_maximum(1)
                gathered(0)
                choose(1)
                gathered(1)
                dve.wait_ge(S["merged_ready"], KD * HALVES)
                dve.wait_ge(S["logit_psum"], B)
                dve.wait_ge(S["zeroed"], 4)
                dve.sem_inc(S["h_psum"], 1)
                with dve.Fori(0, GP) as i:
                    for s in range(2):
                        n = 2 * i + s
                        carried_wait(dve, passed, (S["h_psum"], n + 1))
                        for t in range(KD):
                            ins = nc.vector.tensor_copy(mg[s][:, t, :, 0:B], merged[:, t, ds(group_of(i, s) * EG, EG), :])
                        ins.then_inc(S["mg_ready"], 1)
                        dve.wait_ge(S["h_psum"], n + 2)
                        dve.wait_ge(S[f"b1_loaded{s}"], 16 * EG * i + 16 * EG)
                        dve.wait_ge(S["gelu_ready"], n + 1)
                        dve.wait_ge(S["ht_psum"], 2 * n + 2)
                        for c in range(2):
                            ins = nc.vector.tensor_tensor(hid[:, c * BANK:(c + 1) * BANK], banks[2 * s + c][:, :],
                                                          b1[s][:, c * BANK:(c + 1) * BANK], ALU.add)
                        ins.then_inc(S["pre_ready"], 1)
                        dve.wait_ge(S["ht_psum"], 2 * n + 3)
                        dve.wait_ge(S["o_psum"], n + 1)
                        nc.vector.tensor_copy(hid_t[:, 0:MH // 2, :].rearrange("p k c -> p (k c)"), banks[4][:, :]).then_inc(
                            S["ht_ready"], 1)
                        dve.wait_ge(S["o_psum"], n + 2)
                        dve.wait_ge(S[f"o_stored{s}"], 16 * EG * i + 16 * EG)
                        nc.vector.tensor_copy(o_sb[s][:, :], banks[6 + s][:, 0:D]).then_inc(S["o_ready"], 1)
                dve.wait_ge(S["o_loaded"], 16 * HALVES * QB)
                nc.vector.tensor_tensor(o_all[:, :, :], o_all[:, :, :], free_bcast(b2[:, :], 1, HALVES), ALU.add).then_inc(
                    S["o_all_ready"], 1)
                for b in range(B):
                    dve.wait_ge(S[f"x_again{b // QB}"], 16 * QB)
                    for c in range(2):
                        dve.wait_ge(S["y_psum"], b // QB * 2 + c + 1)
                        pair = x[:, b, 2 * c:2 * c + 2, :].rearrange("p s d -> p (s d)")
                        nc.vector.tensor_tensor(pair, pair, banks[2 * (b % QB) + c][:, :], ALU.add).then_inc(S["y_added"], 1)

            @block.tensor
            def _(pe):
                pe.wait_ge(S["params_loaded"], 16 * N_PARAMS)
                for n in range(B):
                    half, q = n // QB, n % QB
                    pe.wait_ge(S["xln"], ST * (n + 1))
                    pair = banks[2 * (n % 2):2 * (n % 2) + 2]
                    if n >= 2:
                        pe.wait_ge(S["xt_ready"], KD * (n - 1))
                    transpose_tiles(nc, x[:, n, :, :], ident, pair, S["xt_psum"])
                    pe.wait_ge(S["xt_ready"], KD * (n + 1))
                    for k in range(KD):
                        ins = nc.tensor.matmul(logit_bank[half][q * E:(q + 1) * E, :], gate[:, k, :], xt[n % 2][:, k, :],
                                               start=(k == 0), stop=(k == KD - 1))
                    ins.then_inc(S["logit_psum"], 1)
                for half in range(HALVES):
                    pe.wait_ge(S["route_ready"], half + 1)
                    for st in range(ST):
                        ins = nc.tensor.transpose(banks[5][:, st * P:(st + 1) * P], route[:, half, st * P:(st + 1) * P], ident[:, :])
                    ins.then_inc(S["route_t_psum"], 1)
                    pe.wait_ge(S["route_t_ready"], half + 1)
                    for st in range(ST):
                        for q in range(QB):
                            ins = nc.tensor.matmul(banks[6][q * E:(q + 1) * E, 0:D], route_t[:, st, q * E:(q + 1) * E],
                                                   x[:, half * QB + q, st, :], start=(st == 0), stop=(st == ST - 1))
                    ins.then_inc(S["mrg_psum"], 1)
                    pe.wait_ge(S["mrg_ready"], half + 1)
                    pe.wait_ge(S["soft1"], 1)
                    for t in range(KD):
                        ins = nc.tensor.transpose(banks[7][:, t * P:(t + 1) * P], mrg[:, t:D:KD], ident[:, :])
                    ins.then_inc(S["merged_psum"], 1)
                pe.wait_ge(S["merged_ready"], KD * HALVES)
                pe.sem_inc(S["ht_psum"], 2)
                pe.sem_inc(S["o_psum"], 1)
                with pe.Fori(0, GP) as i:
                    for s in range(2):
                        n = 2 * i + s
                        pe.wait_ge(S["mg_ready"], n + 1)
                        pe.wait_ge(weights.loaded[s][0], 16 * i + 16)
                        for c in range(2):
                            for t in range(KD):
                                for j in range(EG):
                                    ins = nc.tensor.matmul(banks[2 * s + c][j * EQ:(j + 1) * EQ, :], mg[s][:, t, j, :],
                                                           weights.w1[s][:, j, t, c * BANK:(c + 1) * BANK],
                                                           start=(t == 0), stop=(t == KD - 1))
                        ins.then_inc(S["h_psum"], 1)
                        pe.wait_ge(S["gelu_ready"], n + 2)
                        for k in range(MH):
                            ins = nc.tensor.transpose(banks[4 + k // (MH // 2)][:, k % (MH // 2) * P:(k % (MH // 2) + 1) * P],
                                                      hid[:, k:HID:MH], ident[:, :])
                            if k % (MH // 2) == MH // 2 - 1:
                                ins.then_inc(S["ht_psum"], 1)
                        carried_wait(pe, passed, (weights.loaded[s][1], 16 * i + 16),
                                     (S["ht_ready"], 2 * n + 2))
                        for k in range(MH):
                            for j in range(EG):
                                ins = nc.tensor.matmul(banks[6 + s][j * EQ:(j + 1) * EQ, 0:D],
                                                       hid_t[:, k, j * EQ:(j + 1) * EQ], weights.w2[s][:, j, k, :],
                                                       start=(k == 0), stop=(k == MH - 1))
                        ins.then_inc(S["o_psum"], 1)
                pe.wait_ge(S["o_all_ready"], 1)
                for half in range(HALVES):
                    for c in range(2):
                        if half:
                            pe.wait_ge(S["y_added"], 2 * QB)
                        for st in range(2 * c, 2 * c + 2):
                            for q in range(QB):
                                rows = slice(q * E, (q + 1) * E)
                                ins = nc.tensor.matmul(banks[2 * q + c][:, (st % 2) * D:(st % 2 + 1) * D],
                                                       route[rows, half, st * P:(st + 1) * P], o_all[rows, half, :],
                                                       start=True, stop=True)
                        ins.then_inc(S["y_psum"], 1)
        m.end_phase()


def delta_phase(nc, banks, consts, x_in, x_out, prm, n_scratch, t_scratch):
    ident, eps = consts["ident"], consts["eps"]
    NT = 3 * KD
    COPIES = 3
    SLOTS = NC + ST
    FEATN = (2, 3, 4, 5, 0, 1)
    u_bank, s_bank, o_bank, fbank = banks[0], banks[1], banks[2:4], banks[4:8]
    fb = lambda t: fbank[t % 4]
    with ExitStack() as ctx:
        m = Mem(nc, ctx)
        w_qkv = m.sb("w_qkv", P, KD, 3 * D)
        w_gates = m.sb("w_gates", P, KD, 2 * H)
        w_o = m.sb("w_o", P, KD, D)
        conv_w = m.sb("conv_w_qkv", P, NT, KC)
        mix_bias = m.sb("mix_bias", P, 2, H)
        o_norm = m.sb("o_norm", P, 1)
        eps_l2 = m.sb("eps_l2", P, 1)
        neg_strict = m.sb("neg_strict", P, C)
        upper = m.sb("upper", P, C)
        head_mask = m.sb("head_mask", P, P)
        x = m.sb("x_delta", P, ST, D)
        x_res = m.sb("x_res_delta", P, ST, D)
        xln = m.sb("xln_delta", P, ST, D)
        xt = m.sb("xt_delta", P, KD, L)
        nb = NormBufs(m, "delta")
        xpad = m.sb("xpad_qkv", P, NT, KC - 1 + L)
        conv = m.sb("conv_qkv", P, NT, L)
        squares = conv[:, 0:4, :].rearrange("p t l -> p (t l)")
        feats = [m.sb(f"feat{i}", P, NT, L) for i in range(COPIES)]
        all_gates = [m.sb(f"gates{i}", P, ST, 2 * H) for i in range(COPIES)]
        toks = [m.sb(f"tok{i}", P, ST, NT * P) for i in range(COPIES)]
        vbs = [m.sb(f"beta_v{i}", P, ST, D) for i in range(COPIES)]
        attn_ts = [m.sb(f"attn_t{i}", P, ST, H, C) for i in range(COPIES)]
        t_toks = [m.sb(f"t_tok{i}", P, ST, H, C) for i in range(COPIES)]
        ssq = m.sb("ssq", P, ST * 2 * H)
        rnorm = m.sb("rnorm", P, ST * 2 * H)
        kb = m.sb("beta_k", P, ST, D)
        n_tok = m.sb("n_tok", P, ST, H, C)
        n_lane = m.sb("n_lane", P, C, C)
        t_lane = m.sb("t_lane", P, C, C)
        prod = m.sb("prod", P, C * C)
        y = m.sb("y_chunk", P, KD, P)
        u = m.sb("u_chunk", P, KD, P)
        state = m.sb("s_delta", P, KD, P)
        o = m.sb("o_delta", P, ST, D)
        o_sq = m.sb("o_squares", P, ST, D)
        ot = m.sb("ot_delta", P, KD, L)
        oms = m.sb("o_ms", P, ST * H)
        ostd = m.sb("o_std", P, ST * H)
        orstd = m.sb("o_rstd", P, ST * H)

        ns = NormSems(m, "delta")
        S = {k: m.sem("de_" + k) for k in (
            "params_loaded", "masks", "mix_ready", "w_o_ready", "lane_init", "x_loaded", "res_loaded", "xt_psum", "xt_ready",
            "qkv_psum", "qkv_read", "conv_step", "feat_ready", "gate_psum", "gate_pre", "gate_ready", "tok_psum",
            "tok_ready", "sq_ready", "ssq_ready", "l2_std", "l2_ready", "vb_ready", "qk_ready", "kb_ready",
            "featn_psum", "featn_ready", "gram_psum", "gram_read", "n_stored", "n_loaded", "solve", "t_stored",
            "t_loaded", "x_chunk", "y_ready", "u_psum", "u_ready", "s_psum", "s_ready", "o_psum", "o_read", "gated",
            "o_sq", "o_ms", "o_std", "o_rstd", "o_scaled", "ot_psum", "ot_ready", "out_psum", "out_added", "x_stored")}
        N_PARAMS = 11 + HS
        KPB = (KC - 1) * NT
        SOLVE = 2 * (C - 1)
        CH = NC - 1
        GATED = 2 * ST

        passed = m.sem(f"sync_passed_{m.nc.next_id()}")

        def both(bank):
            return bank[:, 0:D].rearrange("p (t c) -> p t c", c=P)

        def iterations(eng, iteration):
            iteration(-2, chain=False, solve=False)
            iteration(-1, chain=False)
            with eng.Fori(0, (B - 2) // COPIES) as j:
                for k in range(COPIES):
                    iteration(COPIES * j + k, k)
            iteration(B - 2, front=False)
            iteration(B - 1, front=False, solve=False)

        def copies(i, k):
            k = i if k is None else k
            return [(k + d) % COPIES for d in range(3)]

        def solve_steps(n):
            lo, hi = (((C - 1) * s) // (NC - 2) + 1 for s in (n - 2, n - 1))
            return range(lo, hi) if 2 <= n < NC else ()

        with nc.Block() as block:
            @block.sync
            def _(sp):
                for dst, src in [(w_qkv[:, :, i * D:(i + 1) * D], prm[f"{n}_w"].rearrange("(k p) n -> p k n", p=P))
                                 for i, n in enumerate("qkv")] + \
                        [(conv_w[:, KD * i:KD * i + KD, :], prm[f"conv_{n}_w"].rearrange("(k p) n -> p k n", p=P))
                         for i, n in enumerate("qkv")] + \
                        [(w_gates[:, :, i * H:(i + 1) * H], prm[n].rearrange("(k p) n -> p k n", p=P))
                         for i, n in enumerate(("b_w", "mix_w"))] + \
                        [(mix_bias[:, i, :], prm[n].partition_broadcast(P)) for i, n in enumerate(("mix_b", "mix_bias"))] + \
                        [(o_norm[g * DK:(g + 1) * DK, :], prm["o_norm_w"].rearrange("(d o) -> d o", o=1)) for g in range(HS)] + \
                        [(w_o[:, :, :], prm["o_w"].rearrange("(k p) n -> p k n", p=P))]:
                    sp.dma_start(dst, src).then_inc(S["params_loaded"], 16)
                sp.sem_inc(S["x_stored"], 16)

                def iteration(i, k=None, chain=True, solve=True, front=True):
                    c, s, f = i, i + 1, i + 2
                    _, s_copy, _ = copies(i, k)
                    if front:
                        carried_wait(sp, passed, (ns.xln, ST * f))
                        sp.dma_start(x[:, :, :], token_major(x_in, f)).then_inc(S["x_loaded"], 16)
                    if chain:
                        carried_wait(sp, passed, (S["x_stored"], 16 * c + 16))
                        sp.dma_start(x_res[:, :, :], token_major(x_in, c)).then_inc(S["res_loaded"], 16)
                    if solve:
                        carried_wait(sp, passed, (S["solve"], SOLVE * s + SOLVE))
                        sp.dma_start(t_scratch[ds(s, 1), :, :, :].rearrange("o h (c i) j -> (o h c) i j", i=C),
                                     t_lane[:, :, :]).then_inc(S["t_stored"], 16)
                        carried_wait(sp, passed, (S["t_stored"], 16 * s + 16))
                        for st in range(ST):
                            sp.dma_start(t_toks[s_copy][:, st, :, :], t_scratch[ds(s, 1), :, st * P:(st + 1) * P, :].rearrange(
                                "o h p j -> p (o h) j")).then_inc(S["t_loaded"], 16)
                    if front:
                        carried_wait(sp, passed, (S["gram_read"], 2 * KD * f + KD))
                        for st in range(ST):
                            sp.dma_start(n_scratch[ds(f, 1), :, st * P:(st + 1) * P, :].rearrange("o h p j -> p (o h) j"),
                                         n_tok[:, st, :, :]).then_inc(S["n_stored"], 16)
                        carried_wait(sp, passed, (S["n_stored"], 16 * ST * (f + 1)))
                        sp.dma_start(n_lane[:, :, :], n_scratch[ds(f, 1), :, :, :].rearrange(
                            "o h (c i) j -> (o h c) i j", i=C)).then_inc(S["n_loaded"], 16)
                    if chain:
                        carried_wait(sp, passed, (S["out_added"], 2 * c + 4))
                        sp.dma_start(token_major(x_out, c), x_res[:, :, :]).then_inc(S["x_stored"], 16)

                iterations(sp, iteration)
                sp.wait_ge(S["x_stored"], 16 * (B + 1))

            @block.gpsimd
            def _(pool):
                nc.gpsimd.memset(neg_strict[:, :], -1.0).then_inc(S["masks"], 1)
                nc.gpsimd.memset(upper[:, :], 1.0).then_inc(S["masks"], 1)
                nc.gpsimd.memset(head_mask[:, :], 0.0).then_inc(S["masks"], 1)
                nc.gpsimd.memset(eps_l2[:, :], 1e-12).then_inc(S["masks"], 1)
                nc.gpsimd.memset(t_lane[:, :, :], 0.0).then_inc(S["lane_init"], 1)
                pool.wait_ge(S["masks"], 4)
                pool.wait_ge(S["lane_init"], 1)
                for c in range(CT):
                    rows = slice(c * C, (c + 1) * C)
                    nc.gpsimd.affine_select(out=neg_strict[rows, :], in_=neg_strict[rows, :], compare_op=ALU.is_gt,
                                            fill=0.0, base=0, pattern=[[1, C]], channel_multiplier=-1).then_inc(S["masks"], 1)
                    pool.wait_ge(S["masks"], 4 + 3 * c + 1)
                    nc.gpsimd.affine_select(out=upper[rows, :], in_=upper[rows, :], compare_op=ALU.is_ge,
                                            fill=0.0, base=0, pattern=[[1, C]], channel_multiplier=-1).then_inc(S["masks"], 1)
                    pool.wait_ge(S["masks"], 4 + 3 * c + 2)
                    nc.gpsimd.memset(head_mask[rows, rows], 1.0).then_inc(S["masks"], 1)
                    pool.wait_ge(S["masks"], 4 + 3 * c + 3)
                nc.gpsimd.memset(t_lane[:, :, :].rearrange("p i j -> p (i j)")[:, 0:C * C:C + 1], 1.0).then_inc(S["lane_init"], 1)

                def normalise(f, tok, gates, vb):
                    heads = lambda t: t.rearrange("p s (h d) -> p s h d", d=DK)
                    beta = free_bcast(gates[:, :, 0:H], 3, DK)
                    pool.wait_ge(S["gate_ready"], f + 1)
                    pool.wait_ge(S["tok_ready"], NT * (f + 1))
                    nc.gpsimd.tensor_tensor(heads(vb[:, :, :]), heads(tok[:, :, 2 * D:3 * D]), beta, ALU.mult).then_inc(S["vb_ready"], 1)
                    pool.wait_ge(S["l2_ready"], f + 1)
                    for i, part in enumerate((tok[:, :, D:2 * D], tok[:, :, 0:D])):
                        scale = free_bcast(rnorm[:, :], 2, DK).rearrange("p (s h) d -> p s h d", s=ST)
                        nc.gpsimd.tensor_tensor(heads(part), heads(part), scale[:, :, (1 - i) * H:(2 - i) * H, :],
                                                ALU.mult).then_inc(S["qk_ready"], 1)
                        if i == 0:
                            pool.wait_ge(S["qk_ready"], 2 * f + 1)
                            nc.gpsimd.tensor_tensor(heads(kb[:, :, :]), heads(part), beta, ALU.mult).then_inc(S["kb_ready"], 1)

                def gate(c, st, tok, gates):
                    heads = lambda t: t.rearrange("p (h d) -> p h d", d=DK)
                    pool.wait_ge(S["o_read"], ST * c + st + 1)
                    nc.gpsimd.tensor_tensor(heads(o[:, st, :]), heads(o[:, st, :]), free_bcast(gates[:, st, H:2 * H], 2, DK),
                                            ALU.mult).then_inc(S["gated"], 1)
                    pool.wait_ge(S["gated"], GATED * c + 2 * st + 1)
                    nc.gpsimd.tensor_tensor(o[:, st, :], o[:, st, :], tok[:, st, 2 * D:3 * D], ALU.add).then_inc(S["gated"], 1)

                def iteration(i, k=None, chain=True, solve=True, front=True):
                    c, s, f = i, i + 1, i + 2
                    c_copy, _, f_copy = copies(i, k)
                    for n in range(SLOTS):
                        if chain and n < NC and n % CT == CT - 1:
                            gate(c, n // CT, toks[c_copy], all_gates[c_copy])
                        if front and n == 9:
                            normalise(f, toks[f_copy], all_gates[f_copy], vbs[f_copy])

                iterations(pool, iteration)

            @block.scalar
            def _(act):
                def xt_copies(f):
                    for kt in range(KD):
                        act.wait_ge(S["xt_psum"], KD * f + kt + 1)
                        nc.scalar.copy(xt[:, kt, :], fbank[kt][:, :]).then_inc(S["xt_ready"], 1)

                def last_tap(f, tiles):
                    for t in tiles:
                        act.wait_ge(S["qkv_psum"], NT * f + t + 1)
                        nc.scalar.activation(conv[:, t, :], fb(t)[:, :], ACT.Copy, scale=conv_w[:, t, KC - 1:KC])
                        nc.scalar.copy(xpad[:, t, KC - 1:], fb(t)[:, :]).then_inc(S["qkv_read"], 1)

                def silu(f, tiles, feat):
                    for t in tiles:
                        act.wait_ge(S["conv_step"], 1 + KPB * f + (KC - 1) * (t + 1))
                        nc.scalar.activation(feat[:, t, :], conv[:, t, :], ACT.Silu).then_inc(S["feat_ready"], 1)

                def gate_sigmoid(f, gates):
                    act.wait_ge(S["gate_pre"], f + 1)
                    nc.scalar.activation(gates[:, :, :], gates[:, :, :], ACT.Sigmoid).then_inc(S["gate_ready"], 1)

                def tok_copies(f, tiles, tok):
                    for t in tiles:
                        act.wait_ge(S["tok_psum"], NT * f + t + 1)
                        nc.scalar.copy(tok[:, :, t * P:(t + 1) * P],
                                       fb(t)[:, :].rearrange("p (s c) -> p s c", c=P)).then_inc(S["tok_ready"], 1)

                def qk_squares(f, tok):
                    act.wait_ge(S["tok_ready"], NT * f + 2 * KD)
                    nc.scalar.activation(squares.rearrange("p (s c) -> p s c", s=ST), tok[:, :, 0:2 * D],
                                         ACT.Square).then_inc(S["sq_ready"], 1)

                def l2_root(f):
                    act.wait_ge(S["ssq_ready"], f + 1)
                    nc.scalar.activation(ssq[:, :], ssq[:, :], ACT.Sqrt, bias=eps_l2[:, :]).then_inc(S["l2_std"], 1)

                def featn_copies(f, places, feat):
                    for j in places:
                        act.wait_ge(S["featn_psum"], NT * f + j + 1)
                        nc.scalar.copy(feat[:, FEATN[j], :], fb(j)[:, :]).then_inc(S["featn_ready"], 1)

                def o_squares(c, st):
                    act.wait_ge(S["gated"], GATED * c + 2 * st + 2)
                    nc.scalar.activation(o_sq[:, st, :], o[:, st, :], ACT.Square).then_inc(S["o_sq"], 1)

                def iteration(i, k=None, chain=True, solve=True, front=True):
                    c, s, f = i, i + 1, i + 2
                    c_copy, _, f_copy = copies(i, k)
                    for n in range(SLOTS):
                        if chain and n < NC:
                            rows = slice((n % CT) * C, (n % CT + 1) * C)
                            act.wait_ge(S["u_psum"], NC * c + n + 1)
                            nc.scalar.copy(u[rows, :, :], both(u_bank)[rows, :, :]).then_inc(S["u_ready"], 1)
                        if chain and 4 <= n <= NC and n % CT == 0:
                            o_squares(c, n // CT - 1)
                        if front:
                            if n == 1:
                                norm_scalar(nc, act, f, nb, ns, eps)
                            if n == 2:
                                xt_copies(f)
                            if 3 <= n < 6:
                                last_tap(f, (2 * n - 6, 2 * n - 5))
                            if 6 <= n < 9:
                                silu(f, (2 * n - 12, 2 * n - 11), feats[f_copy])
                            if n == 7:
                                gate_sigmoid(f, all_gates[f_copy])
                            if 7 <= n < 10:
                                tok_copies(f, (2 * n - 14, 2 * n - 13), toks[f_copy])
                            if n == 8:
                                qk_squares(f, toks[f_copy])
                            if n == 9:
                                l2_root(f)
                            if 11 <= n < 14:
                                featn_copies(f, (2 * n - 22, 2 * n - 21), feats[f_copy])
                        if chain and n == 17:
                            act.wait_ge(S["o_ms"], ST * (c + 1))
                            nc.scalar.activation(ostd[:, :], oms[:, :], ACT.Sqrt, bias=eps[:, :], scale=1.0 / DK).then_inc(S["o_std"], 1)
                        if chain and n == 19:
                            for kt in range(KD):
                                act.wait_ge(S["ot_psum"], KD * c + kt + 1)
                                nc.scalar.copy(ot[:, kt, :], o_bank[kt][:, :]).then_inc(S["ot_ready"], 1)

                act.wait_ge(S["params_loaded"], 16 * N_PARAMS)
                act.wait_ge(S["masks"], 4 + 3 * CT)
                act.wait_ge(S["conv_step"], 1)
                iterations(act, iteration)

            @block.vector
            def _(dve):
                def norm_statistics(f):
                    dve.wait_ge(S["x_loaded"], 16 * f + 16)
                    for st in range(ST):
                        nc.vector.bn_stats(nb.stats[:, st, :], x[:, st, :]).then_inc(ns.stats, 1)
                    carried_wait(dve, ns.turn, (ns.stats, ST * (f + 1)))
                    for st in range(ST):
                        nc.vector.bn_aggr(nb.mv[:, st, :], nb.stats[:, st, :]).then_inc(ns.mv, 1)

                def norm_apply(f):
                    dve.wait_ge(ns.std, f + 1)
                    nc.vector.reciprocal(nb.rstd[:, :], nb.std[:, :]).then_inc(ns.rstd, 1)
                    dve.wait_ge(ns.rstd, f + 1)
                    for st in range(ST):
                        nc.vector.tensor_scalar(xln[:, st, :], x[:, st, :], nb.mv[:, st, 0:1], nb.rstd[:, st:st + 1],
                                                ALU.subtract, ALU.mult).then_inc(ns.xln, 1)

                def taps(f, t):
                    for k in range(KC - 1):
                        if k == 0:
                            dve.wait_ge(S["qkv_read"], NT * f + t + 1)
                        else:
                            dve.wait_ge(S["conv_step"], 1 + KPB * f + (KC - 1) * t + k)
                        nc.vector.scalar_tensor_tensor(conv[:, t, :], xpad[:, t, k:k + L], conv_w[:, t, k:k + 1],
                                                       conv[:, t, :], ALU.mult, ALU.add).then_inc(S["conv_step"], 1)

                def gate_inputs(f, gates):
                    dve.wait_ge(S["gate_psum"], f + 1)
                    gp = fbank[2][:, 0:ST * 2 * H].rearrange("p (s h) -> p s h", s=ST)
                    nc.vector.tensor_copy(gates[:, :, 0:H], gp[:, :, 0:H])
                    nc.vector.tensor_tensor(gates[:, :, H:2 * H], gp[:, :, H:2 * H],
                                            free_bcast(mix_bias[:, 0, :], 1, ST), ALU.add).then_inc(S["gate_pre"], 1)

                def l2_sums(f):
                    dve.wait_ge(S["sq_ready"], f + 1)
                    nc.vector.tensor_reduce(ssq[:, :], squares.rearrange("p (a d) -> p a d", d=DK),
                                            AX_X, ALU.add).then_inc(S["ssq_ready"], 1)

                def l2_reciprocal(f):
                    dve.wait_ge(S["l2_std"], f + 1)
                    nc.vector.reciprocal(rnorm[:, :], ssq[:, :]).then_inc(S["l2_ready"], 1)

                def mask_gram(f, attn_t):
                    dve.wait_ge(S["gram_psum"], f + 1)
                    for i, (dst, mask) in ((1, (n_tok, neg_strict)), (0, (attn_t, upper))):
                        for hh in range(KD):
                            blocks = banks.whole[:, 4:4 + HS, hh * ST * 2 * C:(hh + 1) * ST * 2 * C].rearrange(
                                "p g (s i j) -> p s g i j", i=2, j=C)[:, :, :, i, :]
                            nc.vector.tensor_tensor(dst[:, :, hh * HS:(hh + 1) * HS, :], blocks,
                                                    free_bcast(free_bcast(mask[:, :], 1, HS), 1, ST),
                                                    ALU.mult).then_inc(S["gram_read"], 1)

                def solve_row(s, i):
                    ch = Chain(dve, S["solve"], SOLVE * s + 2 * (i - 1))
                    pr = prod[:, 0:i * i].rearrange("p (k j) -> p k j", j=i)
                    if i == 1:
                        dve.wait_ge(S["n_loaded"], 16 * s + 16)
                    else:
                        ch.wait()
                    ch.step(nc.vector.tensor_tensor(pr, t_lane[:, 0:i, 0:i], free_bcast(n_lane[:, 0:i, i], 1, i), ALU.mult))
                    ch.wait()
                    ch.step(nc.vector.tensor_reduce(t_lane[:, 0:i, i], pr, AX_X, ALU.add))

                def o_mean_squares(c, st):
                    dve.wait_ge(S["o_sq"], ST * c + st + 1)
                    nc.vector.tensor_reduce(oms[:, st * H:(st + 1) * H], o_sq[:, st, :].rearrange("p (a d) -> p a d", d=DK),
                                            AX_X, ALU.add).then_inc(S["o_ms"], 1)

                def iteration(i, k=None, chain=True, solve=True, front=True):
                    c, s, f = i, i + 1, i + 2
                    c_copy, _, f_copy = copies(i, k)
                    vb, tok = vbs[c_copy], toks[c_copy]
                    for n in range(SLOTS):
                        st, rows = n // CT, slice((n % CT) * C, (n % CT + 1) * C)
                        if chain and 0 < n < NC:
                            dve.wait_ge(S["x_chunk"], CH * c + n)
                            nc.vector.tensor_tensor(y[rows, :, :], vb[rows, st, :].rearrange("p (t c) -> p t c", c=P),
                                                    both(u_bank)[rows, :, :], ALU.subtract).then_inc(S["y_ready"], 1)
                        if solve:
                            for row in solve_steps(n):
                                solve_row(s, row)
                        if chain and n < NC - 1:
                            dve.wait_ge(S["s_psum"], CH * c + n + 1)
                            blocks = free_bcast(s_bank[:, 0:KD * DK].rearrange("p (t e) -> p t e", t=KD), 2, HS)
                            nc.vector.tensor_tensor(state[:, :, :].rearrange("p t (g e) -> p t g e", g=HS), blocks,
                                                    free_bcast(head_mask[:, :].rearrange("p (g e) -> p g e", g=HS), 1, KD),
                                                    ALU.mult).then_inc(S["s_ready"], 1)
                        if chain and n < NC and n % CT == CT - 1:
                            dve.wait_ge(S["o_psum"], ST * c + st + 1)
                            nc.vector.tensor_tensor(o[:, st, :], o_bank[st % 2][:, 0:D], tok[:, st, 2 * D:3 * D],
                                                    ALU.subtract).then_inc(S["o_read"], 1)
                        if chain and 5 <= n < NC and n % CT == 1:
                            o_mean_squares(c, st - 1)
                        if front:
                            if n == 1:
                                norm_statistics(f)
                            if n == 2:
                                norm_apply(f)
                            if 4 <= n < 7:
                                taps(f, 2 * n - 8)
                                taps(f, 2 * n - 7)
                            if n == 6:
                                gate_inputs(f, all_gates[f_copy])
                            if n == 9:
                                l2_sums(f)
                            if n == 10:
                                l2_reciprocal(f)
                            if n == 18:
                                mask_gram(f, attn_ts[f_copy])
                        if chain and n == 16:
                            o_mean_squares(c, ST - 1)
                        if chain and n == 17:
                            dve.wait_ge(S["o_std"], c + 1)
                            nc.vector.reciprocal(orstd[:, :], ostd[:, :]).then_inc(S["o_rstd"], 1)
                            dve.wait_ge(S["o_rstd"], c + 1)
                            heads = o[:, :, :].rearrange("p s (h d) -> p (s h) d", d=DK)
                            nc.vector.tensor_tensor(heads, heads, free_bcast(orstd[:, :], 2, DK), ALU.mult).then_inc(S["o_scaled"], 1)
                        if chain and n == 19:
                            dve.wait_ge(S["res_loaded"], 16 * c + 16)
                            for half in range(2):
                                dve.wait_ge(S["out_psum"], 2 * c + half + 1)
                                pair = x_res[:, 2 * half:2 * half + 2, :].rearrange("p s d -> p (s d)")
                                nc.vector.tensor_tensor(pair, pair, o_bank[half][:, :], ALU.add).then_inc(S["out_added"], 1)

                nc.vector.memset(xpad[:, :, 0:KC - 1], 0.0).then_inc(S["conv_step"], 1)
                dve.wait_ge(S["params_loaded"], 16 * N_PARAMS)
                nc.vector.tensor_tensor(mix_bias[:, 0, :], mix_bias[:, 0, :], mix_bias[:, 1, :], ALU.add).then_inc(S["mix_ready"], 1)
                nc.vector.tensor_scalar(w_o[:, :, :], w_o[:, :, :], o_norm[:, 0:1], None, ALU.mult).then_inc(S["w_o_ready"], 1)
                dve.wait_ge(S["mix_ready"], 1)
                dve.wait_ge(S["conv_step"], 1)
                dve.wait_ge(S["masks"], 4 + 3 * CT)
                dve.wait_ge(S["lane_init"], 2)
                dve.sem_inc(S["out_added"], 2)
                iterations(dve, iteration)

            @block.tensor
            def _(pe):
                def project(f, tiles):
                    pe.wait_ge(S["xt_ready"], KD * f + KD)
                    for t in tiles:
                        if t >= 4:
                            pe.wait_ge(S["qkv_read"], NT * f + t - 3)
                        for k in range(KD):
                            ins = nc.tensor.matmul(fb(t)[:, :], w_qkv[:, k, t * P:(t + 1) * P], xt[:, k, :],
                                                   start=(k == 0), stop=(k == KD - 1))
                        ins.then_inc(S["qkv_psum"], 1)

                def project_gates(f):
                    pe.wait_ge(S["qkv_read"], NT * f + 3)
                    for st in range(ST):
                        for k in range(KD):
                            ins = nc.tensor.matmul(fbank[2][:, st * 2 * H:(st + 1) * 2 * H], xt[:, k, st * P:(st + 1) * P],
                                                   w_gates[:, k, :], start=(k == 0), stop=(k == KD - 1))
                    ins.then_inc(S["gate_psum"], 1)

                def to_tokens(f, tiles, feat):
                    for t in tiles:
                        pe.wait_ge(S["feat_ready"], NT * f + t + 1)
                        pe.wait_ge(S["qkv_read"], NT * f + NT)
                        if t == 2:
                            pe.wait_ge(S["gate_pre"], f + 1)
                        if t >= 4:
                            pe.wait_ge(S["tok_ready"], NT * f + t - 3)
                        for st in range(ST):
                            ins = nc.tensor.transpose(fb(t)[:, st * P:(st + 1) * P], feat[:, t, st * P:(st + 1) * P], ident[:, :])
                        ins.then_inc(S["tok_psum"], 1)

                def to_features(f, places, tok):
                    for j in places:
                        t = FEATN[j]
                        if j < KD:
                            pe.wait_ge(S["qk_ready"], 2 * f + 1)
                            pe.wait_ge(S["tok_ready"], NT * (f + 1))
                        elif j < 2 * KD:
                            pe.wait_ge(S["kb_ready"], f + 1)
                        else:
                            pe.wait_ge(S["qk_ready"], 2 * f + 2)
                            pe.wait_ge(S["featn_ready"], NT * f + j - 3)
                        for st in range(ST):
                            src = tok[:, st, t * P:(t + 1) * P] if t < 2 * KD else kb[:, st, (t - 2 * KD) * P:(t - 2 * KD + 1) * P]
                            ins = nc.tensor.transpose(fb(j)[:, st * P:(st + 1) * P], src, ident[:, :])
                        ins.then_inc(S["featn_psum"], 1)

                def gram(f, st, feat):
                    if st == 0:
                        carried_wait(pe, passed, (S["featn_ready"], NT * (f + 1)))
                    for hh in range(KD):
                        place = (hh * ST + st) * 2 * C
                        for d in range(CT):
                            for g in range(HS):
                                c = (g + d) % CT
                                rows, cols = slice(g * DK, (g + 1) * DK), slice(st * P + c * C, st * P + (c + 1) * C)
                                ins = nc.tensor.matmul(fbank[g][c * C:(c + 1) * C, place:place + 2 * C], feat[rows, KD + hh, cols],
                                                       feat[rows, hh:NT:2 * KD, cols], start=True, stop=True)
                    if st == ST - 1:
                        ins.then_inc(S["gram_psum"], 1)

                def chunk(c, n, feat, tok, vb, t_tok, attn_t):
                    q_f, kb_f = feat[:, 0:KD, :], feat[:, 2 * KD:3 * KD, :]
                    st, ct = n // CT, n % CT
                    rows, cols = slice(ct * C, (ct + 1) * C), slice(n * C, (n + 1) * C)
                    obank = o_bank[st % 2]
                    if n:
                        pe.wait_ge(S["s_ready"], CH * c + n)
                        for hh in range(KD):
                            ins = nc.tensor.matmul(u_bank[rows, hh * P:(hh + 1) * P], kb_f[:, hh, cols], state[:, hh, :],
                                                   start=True, stop=True, skip_group_check=True)
                        ins.then_inc(S["x_chunk"], 1)
                    if ct == 0 and st >= 2:
                        pe.wait_ge(S["o_read"], ST * c + st - 1)
                    if n:
                        for hh in range(KD):
                            nc.tensor.matmul(obank[rows, hh * P:(hh + 1) * P], q_f[:, hh, cols], state[:, hh, :],
                                             start=(hh == 0), stop=True, skip_group_check=True)
                    if n:
                        carried_wait(pe, passed, (S["y_ready"], CH * c + n))
                    for hh in range(KD):
                        for g in range(HS):
                            h, hc = hh * HS + g, slice(g * DK, (g + 1) * DK)
                            rhs = y[rows, hh, hc] if n else vb[rows, st, h * DK:(h + 1) * DK]
                            ins = nc.tensor.matmul(u_bank[rows, h * DK:(h + 1) * DK], t_tok[rows, st, h, :], rhs,
                                                   start=True, stop=True, skip_group_check=True)
                    ins.then_inc(S["u_psum"], 1)
                    carried_wait(pe, passed, (S["u_ready"], NC * c + n + 1))
                    if n < NC - 1:
                        for hh in range(KD):
                            for g in range(HS):
                                h = hh * HS + g
                                ins = nc.tensor.matmul(s_bank[g * DK:(g + 1) * DK, hh * DK:(hh + 1) * DK],
                                                       tok[rows, st, D + h * DK:D + (h + 1) * DK], u[rows, hh, g * DK:(g + 1) * DK],
                                                       start=(n == 0 and hh == 0), stop=True, skip_group_check=True)
                        ins.then_inc(S["s_psum"], 1)
                    for hh in range(KD):
                        for g in range(HS):
                            h, hc = hh * HS + g, slice(hh * P + g * DK, hh * P + (g + 1) * DK)
                            ins = nc.tensor.matmul(obank[rows, hc], attn_t[rows, st, h, :], u[rows, hh, g * DK:(g + 1) * DK],
                                                   start=(n == 0 and h == 0), stop=True, skip_group_check=True)
                    if ct == CT - 1:
                        ins.then_inc(S["o_psum"], 1)

                def output(c):
                    pe.wait_ge(S["o_scaled"], c + 1)
                    for kt in range(KD):
                        for st in range(ST):
                            ins = nc.tensor.transpose(o_bank[kt][:, st * P:(st + 1) * P], o[:, st, kt * P:(kt + 1) * P], ident[:, :])
                        ins.then_inc(S["ot_psum"], 1)
                    pe.wait_ge(S["ot_ready"], KD * c + KD)
                    for half in range(2):
                        for st in range(2 * half, 2 * half + 2):
                            for k in range(KD):
                                ins = nc.tensor.matmul(o_bank[half][:, (st % 2) * D:(st % 2 + 1) * D], ot[:, k, st * P:(st + 1) * P],
                                                       w_o[:, k, :], start=(k == 0), stop=(k == KD - 1))
                        ins.then_inc(S["out_psum"], 1)

                def iteration(i, k=None, chain=True, solve=True, front=True):
                    c, s, f = i, i + 1, i + 2
                    c_copy, _, f_copy = copies(i, k)
                    if chain:
                        carried_wait(pe, passed, (S["t_loaded"], 16 * ST * (c + 1)), (S["out_added"], 2 * c + 2))
                    for n in range(SLOTS):
                        if chain and n < NC:
                            chunk(c, n, feats[c_copy], toks[c_copy], vbs[c_copy], t_toks[c_copy], attn_ts[c_copy])
                        if front:
                            if n == 2:
                                pe.wait_ge(ns.xln, ST * f + ST)
                                if not (isinstance(f, int) and f == 0):
                                    pe.wait_ge(S["gram_read"], 2 * KD * f)
                                transpose_tiles(nc, xln, ident, fbank, S["xt_psum"])
                            if 3 <= n < 6:
                                project(f, (2 * n - 6, 2 * n - 5))
                            if n == 5:
                                project_gates(f)
                            if 7 <= n < 10:
                                to_tokens(f, (2 * n - 14, 2 * n - 13), feats[f_copy])
                            if 11 <= n < 14:
                                to_features(f, (2 * n - 22, 2 * n - 21), toks[f_copy])
                            if 14 <= n < 14 + ST:
                                gram(f, n - 14, feats[f_copy])
                        if chain and n == 19:
                            output(c)

                pe.wait_ge(S["params_loaded"], 16 * N_PARAMS)
                pe.wait_ge(S["w_o_ready"], 1)
                iterations(pe, iteration)
        m.end_phase()


class Banks:

    def __init__(self, whole):
        self.whole = whole

    def __getitem__(self, i):
        if isinstance(i, slice):
            return [self[j] for j in range(i.start, i.stop)]
        return self.whole[:, i, :]


def build(nc, a, out):
    ctx = ExitStack()
    with ctx:
        m = Mem(nc, ctx)
        banks = Banks(ctx.enter_context(nc.psum_tensor("psum", [P, 8, BANK], F32)))
        consts = {"ident": m.sb("ident", P, P), "eps": m.sb("eps", P, 1)}
        x1, x2, x3 = (nc.dram_tensor(f"x_after_{i}", [B, L, D], F32, kind="Internal").ap() for i in (1, 2, 3))
        bc_scratch = nc.dram_tensor("bc_scratch", [B, 2 * NS, L], F32, kind="Internal").ap()
        o_scratch = nc.dram_tensor("o_scratch", [E, B, D], F32, kind="Internal").ap()
        n_scratch = nc.dram_tensor("n_scratch", [B, H, L, C], F32, kind="Internal").ap()
        t_scratch = nc.dram_tensor("t_scratch", [B, H, L, C], F32, kind="Internal").ap()
        const_ready = m.sem("const_ready")
        with nc.Block() as block:
            @block.gpsimd
            def _(pool):
                nc.gpsimd.memset(consts["ident"][:, :], 0.0).then_inc(const_ready, 1)
                nc.gpsimd.memset(consts["eps"][:, :], EPS).then_inc(const_ready, 1)
                pool.wait_ge(const_ready, 2)
                nc.gpsimd.affine_select(out=consts["ident"][:, :], in_=consts["ident"][:, :], compare_op=ALU.not_equal,
                                        fill=1.0, base=0, pattern=[[-1, P]], channel_multiplier=1).then_inc(const_ready, 1)
                pool.wait_ge(const_ready, 3)
        steps = [lambda i, o: mamba_phase(nc, banks, consts, i, o, a, bc_scratch),
                 lambda i, o: moe_phase(nc, banks, consts, i, o, a, o_scratch, "moe1"),
                 lambda i, o: delta_phase(nc, banks, consts, i, o, a, n_scratch, t_scratch),
                 lambda i, o: moe_phase(nc, banks, consts, i, o, a, o_scratch, "moe2")]
        flow = [a["x"], x1, x2, x3, out]
        for i, step in enumerate(steps):
            step(flow[i], flow[i + 1])


_A, _B, _F = "L0_attn_a_", "L0_attn_b_", "L0_ffn_"
_PLAIN = {_A + "x": "x", _A + "conv_w": "conv_w", _A + "A_log": "A_log",
          **{_B + n: n for n in ("q_w", "k_w", "v_w", "conv_q_w", "conv_k_w", "conv_v_w", "b_w", "mix_w", "mix_b",
                                 "mix_bias", "o_norm_w", "o_w")},
          _F + "gate_b": "gate_b", _F + "w1": "w1", _F + "w2": "w2"}
_TRANSPOSED = {_A + "W_in": "W_inT", _A + "W_x": "W_xT", _A + "W_dt": "W_dtT", _A + "W_out": "W_outT",
               _F + "gate_w": "gate_wT"}
_COLUMNS = {_A + "conv_b": "conv_bT", _A + "b_dt": "b_dtT", _A + "Dp": "DpT"}


def kernel(**inputs):
    import numpy as _np
    import concourse.bacc as _bacc
    from concourse import mybir as _mybir
    from concourse.bass_utils import run_bass_kernel_spmd as _run

    nc = _bacc.Bacc("TRN2", target_bir_lowering=False, num_devices=1)
    arrays, args = {}, {}
    for names, lay in ((_PLAIN, lambda v: v), (_TRANSPOSED, lambda v: v.T), (_COLUMNS, lambda v: v.reshape(-1, P).T)):
        for name, short in names.items():
            v = _np.ascontiguousarray(lay(_np.asarray(inputs[name])))
            arrays[f"in_{short}"] = v
            args[short] = nc.dram_tensor(f"in_{short}", v.shape, _mybir.dt.from_np(v.dtype), kind="ExternalInput").ap()
    out = nc.dram_tensor("out_0", (B, L, D), F32, kind="ExternalOutput").ap()
    build(nc, args, out)
    r = _run(nc, [arrays], core_ids=[0])
    return r.results[0]["out_0"]
```
